# Optimizing a Trainium2 kernel written in Bass

```python
import numpy as np
import jax
import jax.numpy as jnp

def _softmax(x, axis=-1):
    return jax.nn.softmax(x, axis=axis)

def _gelu(x):
    return jax.nn.gelu(x, approximate=True)

def _silu(x):
    return jax.nn.silu(x)

def _sigmoid(x):
    return jax.nn.sigmoid(x)

def _layernorm(x, axis=-1, eps=1e-05):
    m = jnp.mean(x, axis=axis, keepdims=True)
    v = jnp.var(x, axis=axis, keepdims=True)
    return (x - m) / jnp.sqrt(v + eps)

def _scatter_add(tgt, idx, src, axis=0):
    return tgt.at[idx].add(src)

def _segment_sum(src, seg, n):
    return jax.ops.segment_sum(src, seg, n)
kernel_name = 'mk_recurrent_d1_jaxref_r4_894da2'

def setup_inputs(seed: int=0):
    np.random.seed(seed)
    _w = jnp.asarray

    def _L0_attn_setup():
        import jax, jax.numpy as jnp
        import numpy as np
        HIDDEN = 512
        KEY = 512
        EPS = 1e-05
        key = jax.random.key(seed)
        k1, k2, k3 = jax.random.split(key, 3)
        B, S = (4, 512)
        x = jax.random.normal(k1, (B, S, HIDDEN), dtype=jnp.float32)
        bq = 1.0 / np.sqrt(HIDDEN)
        qkv = jax.random.uniform(k2, (HIDDEN, KEY * 3), minval=-bq, maxval=bq, dtype=jnp.float32)
        bo = 1.0 / np.sqrt(KEY)
        o_proj = jax.random.uniform(k3, (KEY, HIDDEN), minval=-bo, maxval=bo, dtype=jnp.float32)
        gamma = jnp.ones((HIDDEN,), dtype=jnp.float32)
        beta = jnp.zeros((HIDDEN,), dtype=jnp.float32)
        return {'x': x, 'qkv': qkv, 'o_proj': o_proj, 'gamma': gamma, 'beta': beta}
    _L0_attn_in = _L0_attn_setup()

    def _L0_ffn_setup():
        import jax, jax.numpy as jnp
        import numpy as np
        from jax import lax
        E = 8
        K = 2
        D = 512
        H = 352
        NS = 2
        B, T = (2, 512)
        EPS = 1e-20
        HS = H * NS

        def _silu(v):
            return v * jax.nn.sigmoid(v)
        key = jax.random.key(seed)
        ks = jax.random.split(key, 8)
        s = 0.02
        return {'x': jax.random.normal(ks[0], (B, T, D), jnp.float32), 'router_w': jax.random.normal(ks[1], (E, D), jnp.float32) * 0.006, 'wg': jax.random.normal(ks[2], (E, D, H), jnp.float32) * s, 'wu': jax.random.normal(ks[3], (E, D, H), jnp.float32) * s, 'wd': jax.random.normal(ks[4], (E, H, D), jnp.float32) * s, 'sg': jax.random.normal(ks[5], (D, HS), jnp.float32) * s, 'su': jax.random.normal(ks[6], (D, HS), jnp.float32) * s, 'sd': jax.random.normal(ks[7], (HS, D), jnp.float32) * s}
    _L0_ffn_in = _L0_ffn_setup()
    _d = {'L0_attn_x': _L0_attn_in['x'], 'L0_attn_qkv': _L0_attn_in['qkv'], 'L0_attn_o_proj': _L0_attn_in['o_proj'], 'L0_attn_gamma': _L0_attn_in['gamma'], 'L0_attn_beta': _L0_attn_in['beta'], 'L0_ffn_router_w': _L0_ffn_in['router_w'], 'L0_ffn_wg': _L0_ffn_in['wg'], 'L0_ffn_wu': _L0_ffn_in['wu'], 'L0_ffn_wd': _L0_ffn_in['wd'], 'L0_ffn_sg': _L0_ffn_in['sg'], 'L0_ffn_su': _L0_ffn_in['su'], 'L0_ffn_sd': _L0_ffn_in['sd']}
    _x0 = _d['L0_attn_x']
    _d['L0_attn_x'] = jax.random.normal(jax.random.fold_in(jax.random.key(seed), 1), (4, 1024, 512), dtype=_x0.dtype)
    del _x0
    return _d

def reference(L0_attn_x, L0_attn_qkv, L0_attn_o_proj, L0_attn_gamma, L0_attn_beta, L0_ffn_router_w, L0_ffn_wg, L0_ffn_wu, L0_ffn_wd, L0_ffn_sg, L0_ffn_su, L0_ffn_sd):

    def _L0_attn_ref(x, qkv, o_proj, gamma, beta):
        import jax, jax.numpy as jnp
        import numpy as np
        HIDDEN = 512
        KEY = 512
        EPS = 1e-05
        residual = x
        mu = jnp.mean(x, axis=-1, keepdims=True)
        var = jnp.mean((x - mu) ** 2, axis=-1, keepdims=True)
        x_norm = (x - mu) / jnp.sqrt(var + EPS) * gamma + beta
        q = x_norm @ qkv[:, :KEY]
        k = x_norm @ qkv[:, KEY:2 * KEY]
        v = x_norm @ qkv[:, 2 * KEY:]
        scale = 1.0 / jnp.sqrt(jnp.float32(KEY))
        scores = jnp.einsum('bsk,btk->bst', q, k) * scale
        S_len = x.shape[1]
        causal = jnp.tril(jnp.ones((S_len, S_len), dtype=bool))
        scores = jnp.where(causal[None], scores, -jnp.inf)
        attn = jax.nn.softmax(scores, axis=-1)
        out = attn @ v
        out = out @ o_proj
        return out + residual

    def _L0_ffn_ref(x, router_w, wg, wu, wd, sg, su, sd):
        import jax, jax.numpy as jnp
        import numpy as np
        from jax import lax
        E = 8
        K = 2
        D = 512
        H = 352
        NS = 2
        B, T = (2, 512)
        EPS = 1e-20
        HS = H * NS

        def _silu(v):
            return v * jax.nn.sigmoid(v)
        b, t, d = x.shape
        xf = x.reshape(b * t, d)
        n = xf.shape[0]
        gates = jax.nn.softmax(xf @ router_w.T, axis=-1)
        topv, topi = lax.top_k(gates, K)
        masked = jnp.zeros_like(gates).at[jnp.arange(n)[:, None], topi].set(topv)
        masked = masked / (masked.sum(axis=-1, keepdims=True) + EPS)

        def step(acc, p):
            wg_e, wu_e, wd_e, g_e = p
            y = _silu(xf @ wg_e) * (xf @ wu_e) @ wd_e
            return (acc + y * g_e[:, None], None)
        routed, _ = lax.scan(step, jnp.zeros_like(xf), (wg, wu, wd, masked.T))
        shared = _silu(xf @ sg) * (xf @ su) @ sd
        return (routed + shared).reshape(b, t, d)
    x = L0_attn_x
    xn = _layernorm(x, axis=-1)
    s = _L0_attn_ref(xn, L0_attn_qkv, L0_attn_o_proj, L0_attn_gamma, L0_attn_beta)
    g = _silu(_L0_ffn_ref(xn, L0_ffn_router_w, L0_ffn_wg, L0_ffn_wu, L0_ffn_wd, L0_ffn_sg, L0_ffn_su, L0_ffn_sd))
    x = x + s * g
    return x

_drawn_inputs = setup_inputs


def setup_inputs(seed=0):
    import zlib

    import numpy as np

    out = dict(_drawn_inputs(seed))
    spreads = {'L0_attn_gamma': (1.0, 0.6), 'L0_attn_beta': (0.0, 0.8)}
    factors = {'L0_attn_qkv': 8.0,
     'L0_attn_o_proj': 8.0,
     'L0_ffn_router_w': 4.543,
     'L0_ffn_wg': 3.986,
     'L0_ffn_wu': 3.902,
     'L0_ffn_wd': 3.905}
    for name, (base, spread) in spreads.items():
        noise = np.random.default_rng([zlib.crc32(name.encode()), seed]).standard_normal(out[name].shape)
        drawn = base * np.exp(spread * noise) if base else spread * noise
        out[name] = jnp.asarray(drawn.astype(out[name].dtype))
    for name, factor in factors.items():
        out[name] = (out[name] * factor).astype(out[name].dtype)
    return out
```

```python
from contextlib import ExitStack

import concourse.bass as bass
from concourse import mybir

F32, F16 = mybir.dt.float32, mybir.dt.float16
I32, U32 = mybir.dt.int32, mybir.dt.uint32
ALU = mybir.AluOpType
ACT = mybir.ActivationFunctionType
AX = mybir.AxisListType.X

P = 128
S_XN = 64.0
S_W = 256.0
S_H = 16.0
S_QKVO = 64.0
S_FOLD = 16.0
S_X2 = 16.0
S_Q = 4.0
LN_P = 6.931471805599453
EPS_LN = 1e-5
EPS_GATE = 1e-20


def mixture_attention_kernel(nc, x, qkv, o_proj, gamma, beta, router_w, wg, wu, wd, sg, su, sd, out):
    B, S, D = x.shape
    E, _, H = wg.shape
    N = B * S
    KC = D // P
    NT = N // P
    HC = -(-H // P)
    HP = HC * P
    HR = H - (HC - 1) * P
    NS = sg.shape[1] // H
    SLOT_TILES = 2 * NT + E
    X_FLAT = x.rearrange("b s d -> (b s) d")
    OUT_FLAT = out.rearrange("b s d -> (b s) d")

    xn_rows = nc.dram_tensor("xn_rows", [N, 2 * D], F16, kind="Internal").ap()
    shared_rows = nc.dram_tensor("shared_rows", [N, D], F32, kind="Internal").ap()
    slot_rows = nc.dram_tensor("slot_rows", [SLOT_TILES * P, D], F32, kind="Internal").ap()
    folded = nc.dram_tensor("folded", [P, 2 * KC * 2 * D], F16, kind="Internal").ap()

    with ExitStack() as ctx:
        def sb(name, shape, dt):
            return ctx.enter_context(nc.sbuf_tensor(name, shape, dt))

        def sem(name):
            return ctx.enter_context(nc.semaphore(name))

        def wait(eng, s, value):
            if not (isinstance(value, int) and value <= 0):
                eng.wait_ge(s, value)

        def wait_apart(pool, s, value, settled, settled_at):
            if not isinstance(value, int):
                value = pool.to_reg(value)
            pool.wait_ge(settled, settled_at)
            pool.wait_ge(s, value)

        wide = [ctx.enter_context(nc.psum_tensor(f"pair{i}", [P, 1024], F32)) for i in range(2)]
        banks = [wide[i // 2][:, (i % 2) * 512:(i % 2 + 1) * 512] for i in range(4)]
        banks += [ctx.enter_context(nc.psum_tensor(f"bank{i}", [P, 512], F32)) for i in range(4, 8)]

        ident = sb("ident", [P, P], F32)
        ident16 = sb("ident16", [P, P], F16)
        mean = sb("mean", [P, NT], F32)
        rstd = sb("rstd", [P, NT], F32)
        rstd_s = sb("rstd_s", [P, NT], F32)
        rstd2 = sb("rstd2", [P, NT], F32)
        logits = sb("logits", [P, NT, E], F32)
        gate = sb("gate", [P, 2, NT], F32)
        slot_of = sb("slot_of", [P, 2, NT], U32)
        token_of = sb("token_of", [P, SLOT_TILES], U32)
        expert_of = sb("expert_of", [P, SLOT_TILES], I32)
        rw_split = sb("rw_split", [P, KC, 2, E], F16)
        affine_s = sb("affine_s", [P, 2, KC], F32)
        arena = sb("arena", [P, 100 * 1024], F16)

        def carve(at, shape, dt):
            n = 1
            for s in shape:
                n *= s
            size = n * (4 if dt in (F32, I32, U32) else 2)
            v = arena[:, at // 2:(at + size) // 2]
            if dt != F16:
                v = v.bitcast(dt)
            names = "abcde"[:len(shape)]
            if len(shape) > 1:
                v = v.rearrange(f"p ({' '.join(names)}) -> p {' '.join(names)}",
                                **{c: s for c, s in zip(names, shape)})
            assert at + size <= 200 * 1024
            return v, at + size

        w_in, end = carve(0, [E, KC, 2, 2 * H], F16)
        w_down, end = carve(end, [E, HC, 2, D], F16)
        routed_end = end
        shared_in, end = carve(end, [NS, KC, 2, 2 * H], F16)
        shared_down, end = carve(end, [NS, HC, 2, D], F16)
        stage = []
        for u in range(2):
            v, end = carve(end, [2 * H], F32)
            stage.append(v)
        work_at = end

        piece_loaded = [sem("piece_loaded0"), sem("piece_loaded1")]
        piece_scaled = sem("piece_scaled")
        piece_hi = sem("piece_hi")
        piece_lo = sem("piece_lo")
        PIECES = 4 + HC
        assert KC == 4 and NS == 2 and E % 2 == 0

        def piece(g_src, u_src, d_src, to_in, to_down, e, q):
            if q < 4:
                src = (g_src, u_src)[q // 2](e)[(q % 2) * 2 * P:(q % 2 + 1) * 2 * P, :]
                src = src.rearrange("(c p) h -> p c h", p=P)
                col = (q // 2) * H

                def target(part):
                    return to_in(e)[:, (q % 2) * 2:(q % 2 + 1) * 2, part, col:col + H]
                return src, P, (2, H), target
            c = q - 4
            rows = P if c < HC - 1 else HR

            def target(part):
                return to_down(e)[0:rows, c, part, :]
            return d_src(e)[c * P:c * P + rows, :], rows, (D,), target

        def staged(u, rows, shape):
            if len(shape) == 1:
                return stage[u][0:rows, 0:shape[0]]
            return stage[u][0:rows, :].rearrange("p (c h) -> p c h", c=shape[0])

        def split_pair(pool, base, pair, e_of, srcs, targets, settled, settled_at):
            todo = [(e_of(k), q) for k in range(2) for q in range(PIECES)]

            def load(n):
                e, q = todo[n]
                src, rows, shape, _ = piece(*srcs, *targets, e, q)
                if not (isinstance(base, int) and base + n < 2):
                    wait_apart(pool, piece_lo, base + n - 1, settled, settled_at)
                pool.dma_start(staged(n % 2, rows, shape), src).then_inc(piece_loaded[n % 2], 16)

            load(0)
            load(1)
            for n, (e, q) in enumerate(todo):
                _, rows, shape, target = piece(*srcs, *targets, e, q)
                v = staged(n % 2, rows, shape)
                wait_apart(pool, piece_loaded[n % 2], (pair * PIECES + n // 2 + 1) * 16, settled, settled_at)
                pool.tensor_scalar(v, v, S_W, None, ALU.mult).then_inc(piece_scaled, 1)
                pool.wait_ge(piece_scaled, base + n + 1)
                pool.tensor_copy(target(0), v).then_inc(piece_hi, 1)
                pool.wait_ge(piece_hi, base + n + 1)
                pool.tensor_tensor(target(1), v, target(0), ALU.subtract).then_inc(piece_lo, 1)
                if n + 2 < len(todo):
                    load(n + 2)

        def stage0():
            XT = 4
            w_qkv, at = carve(0, [KC, 3 * D], F32)
            w_o, at = carve(at, [KC, D], F32)
            xs = []
            for u in range(2):
                v, at = carve(at, [XT, D], F32)
                xs.append(v)
            turned, at = carve(at, [3, KC, 2, D], F16)
            o_split, at = carve(at, [KC, 2, D], F16)
            fold, at = carve(at, [2, KC, 2, D], F16)
            st, at = carve(at, [NT, 6], F32)
            rw, at = carve(at, [D], F32)
            affine, at = carve(at, [P], F32)
            tmp, at = carve(at, [6, NT], F32)
            rtmp, at = carve(at, [2, NT], F32)
            assert at <= routed_end

            ident_zeroed = sem("ident_zeroed")
            ident_ready = sem("ident_ready")
            w_loaded = [sem("wqkv_loaded"), sem("wo_loaded"), sem("rw_loaded")]
            affine_ready = sem("affine_ready")
            x_in = [sem("stat_x_loaded0"), sem("stat_x_loaded1")]
            x_seen = sem("stat_x_seen")
            pads_zeroed = sem("pads_zeroed")
            group_done = sem("fold_group_done")
            hi_done = sem("fold_hi_done")
            lo_done = sem("fold_lo_done")
            rw_turned = sem("rw_turned")
            rw_hi = sem("rw_hi")
            rw_lo = sem("rw_lo")
            stat_step = sem("stat_step")
            var_ready = sem("var_ready")
            sqrt_done = sem("sqrt_done")
            fold_stored = sem("fold_stored")

            TURNS, SPLITS, PRODUCTS = 3 * KC, KC, 2 * KC
            GROUPS = TURNS + SPLITS + PRODUCTS

            def group_target(g):
                if g < TURNS:
                    return turned[:, g // KC, g % KC], S_QKVO
                if g < TURNS + SPLITS:
                    return o_split[:, g - TURNS], S_QKVO
                n = g - TURNS - SPLITS
                return fold[:, n // KC, n % KC], S_FOLD / (S_QKVO * S_QKVO)

            def group_source(g):
                if TURNS <= g < TURNS + SPLITS:
                    return w_o[:, g - TURNS, :]
                return banks[bank_turn(g) % 7][:, :]

            def bank_turn(g):
                return g if g < TURNS else g - SPLITS

            with nc.Block() as block:
                @block.sync
                def _(sp):
                    sp.dma_start(w_qkv, qkv.rearrange("(c p) n -> p c n", p=P)).then_inc(w_loaded[0], 16)
                    sp.dma_start(w_o, o_proj.rearrange("(c p) n -> p c n", p=P)).then_inc(w_loaded[1], 16)
                    sp.dma_start(rw[0:E, :], router_w).then_inc(w_loaded[2], 16)
                    sp.dma_start(affine[0:KC, :], gamma.rearrange("(c p) -> c p", p=P)).then_inc(w_loaded[2], 16)
                    sp.dma_start(affine[KC:2 * KC, :], beta.rearrange("(c p) -> c p", p=P)).then_inc(w_loaded[2], 16)
                    for n in range(NT // XT):
                        wait(sp, x_seen, (n - 1) * XT)
                        sp.dma_start(xs[n % 2], X_FLAT[n * XT * P:(n + 1) * XT * P, :].rearrange(
                            "(t p) d -> p t d", p=P)).then_inc(x_in[n % 2], 16)
                    sp.wait_ge(lo_done, GROUPS)
                    sp.wait_ge(hi_done, GROUPS)
                    sp.dma_start(folded, fold.rearrange("p f c s d -> p (f c s d)")).then_inc(fold_stored, 16)
                    sp.wait_ge(fold_stored, 16)

                @block.gpsimd
                def _(pool):
                    pool.memset(ident[:, :], 0.0).then_inc(ident_zeroed, 1)
                    pool.memset(ident16[:, :], 0.0).then_inc(ident_zeroed, 1)
                    pool.wait_ge(ident_zeroed, 2)
                    for m in (ident, ident16):
                        pool.affine_select(out=m[:, :], in_=m[:, :], compare_op=ALU.not_equal, fill=1.0, base=0,
                                           pattern=[[-1, P]], channel_multiplier=1).then_inc(ident_ready, 1)
                    if HR < P:
                        pool.wait_ge(ident_ready, 2)
                        pool.memset(shared_down[HR:P, :, HC - 1], 0.0).then_inc(pads_zeroed, 1)
                        pool.wait_ge(pads_zeroed, 1)
                    split_pair(pool, 0, 0, lambda k: k,
                               (lambda e: sg[:, e * H:(e + 1) * H], lambda e: su[:, e * H:(e + 1) * H],
                                lambda e: sd[e * H:(e + 1) * H, :]),
                               (lambda e: shared_in[:, e], lambda e: shared_down[:, e]), ident_ready, 2)

                @block.tensor
                def _(pe):
                    pe.wait_ge(ident_ready, 2)
                    pe.wait_ge(w_loaded[2], 48)
                    for c in range(KC):
                        last = pe.transpose(banks[7][:, c * E:(c + 1) * E], rw[0:E, c * P:(c + 1) * P],
                                            ident[0:E, 0:E])
                    last = pe.transpose(banks[7][:, KC * E:KC * E + 2 * KC], affine[0:2 * KC, :],
                                        ident[0:2 * KC, 0:2 * KC])
                    last.then_inc(rw_turned, 1)
                    pe.wait_ge(w_loaded[0], 16)
                    for g in range(GROUPS):
                        if TURNS <= g < TURNS + SPLITS:
                            continue
                        turn = bank_turn(g)
                        if turn >= 7:
                            old = turn - 7 if turn - 7 < TURNS else turn - 7 + SPLITS
                            pe.wait_ge(lo_done, old + 1)
                        b = banks[turn % 7]
                        if g < TURNS:
                            m, n = g // KC, g % KC
                            for k in range(KC):
                                last = pe.transpose(b[:, k * P:(k + 1) * P],
                                                    w_qkv[:, k, m * D + n * P:m * D + (n + 1) * P], ident[:, :])
                        else:
                            m, k = (g - TURNS - SPLITS) // KC, (g - TURNS - SPLITS) % KC
                            if k == 0:
                                pe.wait_ge(lo_done, TURNS + SPLITS)
                                pe.wait_ge(hi_done, TURNS + SPLITS)
                            left = turned[:, 0 if m == 0 else 2]
                            right = turned[:, 1] if m == 0 else o_split
                            for n in range(KC):
                                for i, (a, c) in enumerate(((0, 0), (0, 1), (1, 0))):
                                    last = pe.matmul(b[:, :], left[:, n, a, k * P:(k + 1) * P], right[:, n, c, :],
                                                     start=(n == 0 and i == 0), stop=(n == KC - 1 and i == 2))
                        last.then_inc(group_done, 1)

                @block.scalar
                def _(act):
                    act.wait_ge(rw_turned, 1)
                    nc.scalar.activation(rw_split[:, :, 0, :], banks[7][:, 0:KC * E].rearrange(
                        "p (c e) -> p c e", c=KC), ACT.Copy, scale=S_W).then_inc(rw_hi, 1)
                    nc.scalar.activation(affine_s[:, :, :], banks[7][:, KC * E:KC * E + 2 * KC].rearrange(
                        "p (a c) -> p a c", a=2), ACT.Copy, scale=S_X2).then_inc(affine_ready, 1)
                    for g in range(GROUPS):
                        if TURNS <= g < TURNS + SPLITS:
                            act.wait_ge(w_loaded[1], 16)
                        else:
                            act.wait_ge(group_done, bank_turn(g) + 1)
                        to, scale = group_target(g)
                        nc.scalar.activation(to[:, 0, :], group_source(g), ACT.Copy, scale=scale).then_inc(hi_done, 1)
                    act.wait_ge(var_ready, 1)
                    nc.scalar.activation(rtmp[:, 0, :], tmp[:, 4, :], ACT.Sqrt).then_inc(sqrt_done, 1)
                    act.wait_ge(var_ready, 2)
                    nc.scalar.activation(rtmp[:, 1, :], tmp[:, 5, :], ACT.Sqrt).then_inc(sqrt_done, 1)

                @block.vector
                def _(dve):
                    def split_lo(g):
                        dve.wait_ge(hi_done, g + 1)
                        to, scale = group_target(g)
                        nc.vector.scalar_tensor_tensor(to[:, 1, :], group_source(g), scale, to[:, 0, :],
                                                       ALU.mult, ALU.subtract).then_inc(lo_done, 1)

                    dve.wait_ge(rw_hi, 1)
                    dve.wait_ge(affine_ready, 1)
                    nc.vector.scalar_tensor_tensor(
                        rw_split[:, :, 1, :], banks[7][:, 0:KC * E].rearrange("p (c e) -> p c e", c=KC), S_W,
                        rw_split[:, :, 0, :], ALU.mult, ALU.subtract).then_inc(rw_lo, 1)
                    g = 0
                    for n in range(NT // XT):
                        dve.wait_ge(x_in[n % 2], (n // 2 + 1) * 16)
                        for t in range(XT):
                            nc.vector.bn_stats(st[:, n * XT + t, :], xs[n % 2][:, t, :]).then_inc(x_seen, 1)
                        for _ in range(3):
                            if g < GROUPS:
                                split_lo(g)
                                g += 1
                    while g < GROUPS:
                        split_lo(g)
                        g += 1

                    done = [0]

                    def link(ins):
                        done[0] += 1
                        ins.then_inc(stat_step, 1)
                        dve.wait_ge(stat_step, done[0])

                    dve.wait_ge(x_seen, NT)
                    v = nc.vector
                    link(v.tensor_tensor(tmp[:, 0, :], st[:, :, 1], st[:, :, 4], ALU.add))
                    link(v.tensor_scalar(mean[:, :], tmp[:, 0, :], 0.5, None, ALU.mult))
                    link(v.tensor_tensor(tmp[:, 1, :], st[:, :, 1], st[:, :, 4], ALU.subtract))
                    link(v.scalar_tensor_tensor(tmp[:, 2, :], tmp[:, 1, :], 0.25, tmp[:, 1, :], ALU.mult, ALU.mult))
                    link(v.tensor_tensor(tmp[:, 3, :], st[:, :, 2], st[:, :, 5], ALU.add))
                    link(v.scalar_tensor_tensor(tmp[:, 0, :], tmp[:, 3, :], 1.0 / D, tmp[:, 2, :], ALU.mult, ALU.add))

                    def rsqrt(to, value, root, one, two, k):
                        dve.wait_ge(sqrt_done, k)
                        link(v.reciprocal(one, root))
                        link(v.tensor_tensor(two, one, one, ALU.mult))
                        link(v.tensor_tensor(two, two, value, ALU.mult))
                        link(v.tensor_scalar(two, two, -0.5, 1.5, ALU.mult, ALU.add))
                        link(v.tensor_tensor(to, two, one, ALU.mult))

                    v.tensor_scalar(tmp[:, 4, :], tmp[:, 0, :], EPS_LN, None, ALU.add).then_inc(var_ready, 1)
                    dve.wait_ge(var_ready, 1)
                    rsqrt(rstd[:, :], tmp[:, 4, :], rtmp[:, 0, :], tmp[:, 1, :], tmp[:, 2, :], 1)
                    link(v.tensor_scalar(rstd_s[:, :], rstd[:, :], S_XN, None, ALU.mult))
                    link(v.tensor_tensor(tmp[:, 3, :], rstd[:, :], rstd[:, :], ALU.mult))
                    link(v.tensor_tensor(tmp[:, 3, :], tmp[:, 3, :], tmp[:, 0, :], ALU.mult))
                    v.tensor_scalar(tmp[:, 5, :], tmp[:, 3, :], EPS_LN, None, ALU.add).then_inc(var_ready, 1)
                    dve.wait_ge(var_ready, 2)
                    rsqrt(tmp[:, 3, :], tmp[:, 5, :], rtmp[:, 1, :], tmp[:, 1, :], tmp[:, 2, :], 2)
                    link(v.tensor_tensor(rstd2[:, :], tmp[:, 3, :], rstd[:, :], ALU.mult))

        PARTS = ((0, 0), (0, 1), (1, 0))

        def turn_tile(pe, rows, bank16):
            for part in range(2):
                for c in range(KC):
                    last = pe.transpose(bank16[:, part, c, :], rows[:, (part * KC + c) * P:(part * KC + c + 1) * P],
                                        ident16[:, :])
            return last

        def gate_up(pe, xt, weights, g_bank, u_bank):
            for c in range(KC):
                for i, (a, b) in enumerate(PARTS):
                    for bank, col in ((g_bank, 0), (u_bank, H)):
                        last = pe.matmul(bank[:, 0:H], xt[:, a, c, :], weights(c, b, col),
                                         start=(c == 0 and i == 0), stop=(c == KC - 1 and i == 2))
            return last

        def turn_hidden(pe, h, bank16):
            for part in range(2):
                for c in range(HC):
                    last = pe.transpose(bank16[:, part, c, :], h[:, part, c * P:(c + 1) * P], ident16[:, :])
            return last

        def down(pe, ht, weights, bank, start, stop):
            for c in range(HC):
                for i, (a, b) in enumerate(PARTS):
                    last = pe.matmul(bank[:, :], ht[:, a, c, :], weights(c, b),
                                     start=(start and c == 0 and i == 0), stop=(stop and c == HC - 1 and i == 2))
            return last

        def as16(bank, n, m):
            return bank[:, :].bitcast(F16)[:, 0:2 * n * m].rearrange("p (a b c) -> p a b c", a=2, b=n)

        UNIT_SCALE = 1.0 / (S_XN * S_W)
        H_SCALE = S_H / (S_XN * S_W)
        Y_SCALE = 1.0 / (S_H * S_W)

        def stage1():
            at = work_at
            bufs = {}
            for name, shape, dt in (("x", [D], F32), ("xn", [2 * D], F16), ("xt", [2, KC, P], F16),
                                    ("s", [H], F32), ("h", [2, HP], F16), ("ht", [2, HC, P], F16)):
                for u in range(2):
                    v, at = carve(at, shape, dt)
                    bufs[name, u] = v
            y_out, at = carve(at, [D], F32)
            g_banks, u_banks = (banks[0], banks[2]), (banks[1], banks[3])
            y_bank, logit_bank = banks[4], banks[7]
            xt_bank, ht_bank = as16(banks[5], KC, P), as16(banks[6], HC, P)

            x_loaded = [sem("x_loaded0"), sem("x_loaded1")]
            xn_ready = sem("xn_ready")
            xn_hi = sem("xn_hi")
            xn_lo = sem("xn_lo")
            xn_stored = [sem("xn_stored0"), sem("xn_stored1")]
            x_turned = sem("x_turned")
            xt_ready = sem("xt_ready")
            logits_done = sem("logits_done")
            logits_kept = sem("logits_kept")
            gu_done = sem("gu_done")
            silu_done = sem("silu_done")
            h_ready = sem("h_ready")
            h_hi = sem("h_hi")
            h_lo = sem("h_lo")
            h_turned = sem("h_turned")
            ht_ready = sem("ht_ready")
            y_done = sem("y_done")
            y_ready = sem("y_ready")
            y_stored = sem("y_stored")
            h_pads = sem("h_pads")
            routed_pads = sem("routed_pads")

            with nc.Block() as block:
                @block.sync
                def _(sp):
                    def load(t, u, k):
                        wait(sp, xn_lo, t - 1)
                        wait(sp, xn_hi, t - 1)
                        sp.dma_start(bufs["x", u], X_FLAT[bass.ds(t * P, P), :]).then_inc(x_loaded[u], 16)

                    def store_xn(t, u):
                        sp.wait_ge(xn_lo, t + 1)
                        sp.wait_ge(xn_hi, t + 1)
                        sp.dma_start(xn_rows[bass.ds(t * P, P), :], bufs["xn", u]).then_inc(xn_stored[u], 16)

                    def store_y(t):
                        sp.wait_ge(y_ready, t + 1)
                        sp.dma_start(shared_rows[bass.ds(t * P, P), :], y_out).then_inc(y_stored, 16)

                    load(0, 0, 0)
                    load(1, 1, 0)
                    store_xn(0, 0)
                    load(2, 0, 1)
                    store_xn(1, 1)
                    load(3, 1, 1)
                    with sp.Fori(0, NT // 2 - 2) as i:
                        for u in range(2):
                            store_y(2 * i + u)
                            store_xn(2 * i + u + 2, u)
                            load(2 * i + u + 4, u, i + 2)
                    for t in range(NT - 4, NT):
                        store_y(t)
                        if t + 2 < NT:
                            store_xn(t + 2, t % 2)
                    sp.wait_ge(y_stored, NT * 16)
                    for u in range(2):
                        sp.wait_ge(xn_stored[u], NT // 2 * 16)

                @block.gpsimd
                def _(pool):
                    if HR < P:
                        pool.memset(w_down[HR:P, :, HC - 1], 0.0).then_inc(routed_pads, 1)
                        pool.wait_ge(routed_pads, 1)
                    pool.memset(bufs["h", 0][:, :, H:HP], 0.0).then_inc(h_pads, 1)
                    pool.memset(bufs["h", 1][:, :, H:HP], 0.0).then_inc(h_pads, 1)
                    srcs = (lambda e: wg[bass.ds(e, 1)].rearrange("e d h -> (e d) h"),
                            lambda e: wu[bass.ds(e, 1)].rearrange("e d h -> (e d) h"),
                            lambda e: wd[bass.ds(e, 1)].rearrange("e h d -> (e h) d"))
                    targets = (lambda e: w_in[:, bass.ds(e, 1)].rearrange("p e c s h -> p (e c) s h"),
                               lambda e: w_down[:, bass.ds(e, 1)].rearrange("p e c s h -> p (e c) s h"))
                    with pool.Fori(0, E // 2) as i:
                        split_pair(pool, 2 * PIECES * (i + 1), i + 1, lambda k: 2 * i + k, srcs, targets,
                                   h_pads, 2)

                @block.tensor
                def _(pe):
                    def tile_turn(t, u):
                        pe.wait_ge(xn_lo, t + 1)
                        pe.wait_ge(xn_hi, t + 1)
                        wait(pe, xt_ready, t)
                        turn_tile(pe, bufs["xn", u], xt_bank).then_inc(x_turned, 1)

                    def router(t, u):
                        pe.wait_ge(xt_ready, t + 1)
                        wait(pe, logits_kept, t)
                        for c in range(KC):
                            for i, (a, b) in enumerate(PARTS):
                                last = pe.matmul(logit_bank[:, 0:E], bufs["xt", u][:, a, c, :], rw_split[:, c, b, :],
                                                 start=(c == 0 and i == 0), stop=(c == KC - 1 and i == 2))
                        last.then_inc(logits_done, 1)

                    def unit_in(n, u, b):
                        wait(pe, h_ready, n - 1)
                        gate_up(pe, bufs["xt", u], lambda c, s, col: shared_in[:, b, c, s, col:col + H],
                                g_banks[b], u_banks[b]).then_inc(gu_done, 1)

                    def unit_turn(n, b):
                        pe.wait_ge(h_lo, n + 1)
                        pe.wait_ge(h_hi, n + 1)
                        wait(pe, ht_ready, n)
                        turn_hidden(pe, bufs["h", b], ht_bank).then_inc(h_turned, 1)

                    def unit_down(n, t, b):
                        pe.wait_ge(ht_ready, n + 1)
                        if b == 0:
                            wait(pe, y_ready, t)
                        last = down(pe, bufs["ht", b], lambda c, s: shared_down[:, b, c, s, :], y_bank, b == 0, b == 1)
                        last.then_inc(y_done, 1)

                    def tile(t, u, first=False, last=False):
                        router(t, u)
                        for b in range(2):
                            n = 2 * t + b
                            if b == 1 and not last:
                                tile_turn(t + 1, 1 - u)
                            unit_in(n, u, b)
                            if not (first and b < 1):
                                unit_turn(n - 1, 1 - b)
                            if not first:
                                unit_down(n - 2, t - 1, b)

                    pe.wait_ge(h_pads, 2)
                    tile_turn(0, 0)
                    tile(0, 0, first=True)
                    tile(1, 1)
                    with pe.Fori(1, NT // 2 - 1) as i:
                        tile(2 * i, 0)
                        tile(2 * i + 1, 1)
                    tile(NT - 2, 0)
                    tile(NT - 1, 1, last=True)
                    unit_turn(2 * NT - 1, 1)
                    unit_down(2 * NT - 2, NT - 1, 0)
                    unit_down(2 * NT - 1, NT - 1, 1)

                @block.scalar
                def _(act):
                    def xn_high(t, u, k):
                        act.wait_ge(xn_ready, t + 1)
                        wait(act, xn_stored[u], k * 16)
                        nc.scalar.copy(bufs["xn", u][:, 0:D], bufs["x", u]).then_inc(xn_hi, 1)

                    def xt_copy(t, u):
                        act.wait_ge(x_turned, t + 1)
                        wait(act, gu_done, 2 * t - 2)
                        nc.scalar.copy(bufs["xt", u], xt_bank).then_inc(xt_ready, 1)

                    def silu(n, b):
                        act.wait_ge(gu_done, n + 1)
                        wait(act, h_lo, n - 1)
                        wait(act, h_hi, n - 1)
                        nc.scalar.activation(bufs["s", b], g_banks[b][:, 0:H], ACT.Silu,
                                             scale=UNIT_SCALE).then_inc(silu_done, 1)

                    def h_high(n, b):
                        act.wait_ge(h_ready, n + 1)
                        wait(act, h_turned, n - 1)
                        nc.scalar.copy(bufs["h", b][:, 0, 0:H], bufs["s", b]).then_inc(h_hi, 1)

                    def y_copy(t):
                        act.wait_ge(y_done, 2 * t + 2)
                        wait(act, y_stored, t * 16)
                        nc.scalar.activation(y_out, y_bank[:, :], ACT.Copy, scale=Y_SCALE).then_inc(y_ready, 1)

                    def tile(t, u, k, first=False, last=False):
                        if not last:
                            xn_high(t + 1, 1 - u, k if u == 0 else k + 1)
                        silu(2 * t, 0)
                        h_high(2 * t, 0)
                        if not last:
                            xt_copy(t + 1, 1 - u)
                        silu(2 * t + 1, 1)
                        h_high(2 * t + 1, 1)
                        if not first:
                            y_copy(t - 1)

                    xn_high(0, 0, 0)
                    xt_copy(0, 0)
                    tile(0, 0, 0, first=True)
                    tile(1, 1, 0)
                    with act.Fori(1, NT // 2 - 1) as i:
                        tile(2 * i, 0, i)
                        tile(2 * i + 1, 1, i)
                    tile(NT - 2, 0, NT // 2 - 1)
                    tile(NT - 1, 1, NT // 2 - 1, last=True)
                    y_copy(NT - 1)

                @block.vector
                def _(dve):
                    def normalise(t, u, k):
                        dve.wait_ge(x_loaded[u], (k + 1) * 16)
                        nc.vector.tensor_scalar(bufs["x", u], bufs["x", u], mean[:, bass.ds(t, 1)],
                                                rstd_s[:, bass.ds(t, 1)], ALU.subtract, ALU.mult).then_inc(xn_ready, 1)
                        dve.wait_ge(xn_hi, t + 1)
                        nc.vector.tensor_tensor(bufs["xn", u][:, D:2 * D], bufs["x", u], bufs["xn", u][:, 0:D],
                                                ALU.subtract).then_inc(xn_lo, 1)

                    def hidden(n, b):
                        dve.wait_ge(silu_done, n + 1)
                        nc.vector.scalar_tensor_tensor(bufs["s", b], u_banks[b][:, 0:H], H_SCALE, bufs["s", b],
                                                       ALU.mult, ALU.mult).then_inc(h_ready, 1)
                        dve.wait_ge(h_hi, n + 1)
                        nc.vector.tensor_tensor(bufs["h", b][:, 1, 0:H], bufs["s", b], bufs["h", b][:, 0, 0:H],
                                                ALU.subtract).then_inc(h_lo, 1)

                    def ht_copy(n, b):
                        dve.wait_ge(h_turned, n + 1)
                        wait(dve, y_done, n - 1)
                        nc.vector.tensor_copy(bufs["ht", b], ht_bank).then_inc(ht_ready, 1)

                    def tile(t, u, k, first=False, last=False):
                        if not last:
                            normalise(t + 1, 1 - u, k if u == 0 else k + 1)
                        hidden(2 * t, 0)
                        if not first:
                            ht_copy(2 * t - 1, 1)
                        dve.wait_ge(logits_done, t + 1)
                        nc.vector.tensor_copy(logits[:, bass.ds(t, 1), :].rearrange("p t e -> p (t e)"),
                                              logit_bank[:, 0:E]).then_inc(logits_kept, 1)
                        hidden(2 * t + 1, 1)
                        ht_copy(2 * t, 0)

                    normalise(0, 0, 0)
                    tile(0, 0, 0, first=True)
                    tile(1, 1, 0)
                    with dve.Fori(1, NT // 2 - 1) as i:
                        tile(2 * i, 0, i)
                        tile(2 * i + 1, 1, i)
                    tile(NT - 2, 0, NT // 2 - 1)
                    tile(NT - 1, 1, NT // 2 - 1, last=True)
                    ht_copy(2 * NT - 1, 1)

        def stage2():
            at = routed_end
            sh = {}

            def new(name, shape, dt=F32):
                nonlocal at
                sh[name], at = carve(at, shape, dt)
                return sh[name]

            W = SLOT_TILES
            eq, cand, rest, pe_x = (new(n, [NT, E]) for n in ("eq", "cand", "rest", "pe_x"))
            pick = [new(f"pick{c}", [NT, E]) for c in range(2)]
            top = [new(f"top{c}", [NT]) for c in range(2)]
            first_of, e2, z, g1, g2 = (new(n, [NT]) for n in ("first_of", "e2", "z", "g1", "g2"))
            rev = new("rev", [NT, E])
            both16 = new("both16", [NT, E], F16)
            before = new("before", [P], F16)
            ones16 = new("ones16", [P], F16)
            tile_counts, running, segment = (new(n, [E, NT]) for n in ("tile_counts", "running", "segment"))
            place = new("place", [NT, E])
            padded, tiles_f, tiles_cum, base_slot, ones_e = (
                new(n, [E]) for n in ("padded", "tiles_f", "tiles_cum", "base_slot", "ones_e"))
            tiles_i = new("tiles_i", [E], I32)
            column = new("column", [W])
            column_e = new("column_e", [W, E])
            expert_f = new("expert_f", [W])
            slot_f = new("slot_f", [2, NT])
            slot_hi_i, slot_lo_i = new("slot_hi_i", [2, NT], I32), new("slot_lo_i", [2, NT], I32)
            slot_hi, slot_lo = new("slot_hi", [2, NT]), new("slot_lo", [2, NT])
            lane = new("lane", [P])
            part_of = new("part_of", [1])
            tile_row = new("tile_row", [NT])
            token_f = new("token_f", [W])
            hot_lane = [new(f"hot_lane{u}", [P], F16) for u in range(2)]
            hot_tile = [new(f"hot_tile{u}", [2, W], F16) for u in range(2)]

            consts = sem("routing_consts")
            ones_set = sem("ones_set")
            step = sem("routing_step")
            exp_asked = sem("exp_asked")
            exp_done = sem("exp_done")
            picks_ready = sem("picks_ready")
            ranks_done = sem("ranks_done")
            hot_ready = sem("hot_ready")
            hot_used = sem("hot_used")
            tokens_done = sem("tokens_done")
            rank_bank, count_bank, token_bank = banks[0], banks[1], banks[2]

            def over_experts(v):
                return v.unsqueeze(2).to_broadcast([P, v.shape[1], E])

            with nc.Block() as block:
                @block.gpsimd
                def _(pool):
                    n = [0]

                    def put(ins):
                        n[0] += 1
                        ins.then_inc(consts, 1)
                    imprecise = dict(allow_small_or_imprecise_dtypes=True)
                    put(pool.iota(rev, [[0, NT], [-1, E]], base=E, channel_multiplier=0, **imprecise))
                    put(pool.iota(column, [[1, W]], base=0, channel_multiplier=0, **imprecise))
                    put(pool.iota(lane, [[1, P]], base=0, channel_multiplier=0, **imprecise))
                    put(pool.iota(tile_row, [[1, NT]], base=0, channel_multiplier=0, **imprecise))
                    put(pool.iota(part_of, [[1, 1]], base=0, channel_multiplier=1, **imprecise))
                    put(pool.memset(ones_e, 1.0))
                    pool.memset(ones16, 1.0).then_inc(ones_set, 1)
                    pool.wait_ge(ones_set, 1)
                    put(pool.affine_select(out=before, in_=ones16, compare_op=ALU.is_gt, fill=0.0, base=0,
                                           pattern=[[1, P]], channel_multiplier=-1))
                    put(pool.memset(segment, 1.0))
                    pool.wait_ge(consts, n[0])
                    put(pool.memset(segment[:, :, 0:1], 0.0))
                CONSTS = 9

                @block.scalar
                def _(act):
                    act.wait_ge(exp_asked, 1)
                    nc.scalar.activation(pe_x, rest, ACT.Exp, scale=UNIT_SCALE).then_inc(exp_done, 1)
                    act.wait_ge(exp_asked, 2)
                    nc.scalar.activation(e2, g2, ACT.Exp, scale=UNIT_SCALE).then_inc(exp_done, 1)

                @block.tensor
                def _(pe):
                    pe.wait_ge(picks_ready, 1)
                    pe.wait_ge(consts, CONSTS)
                    picked = both16.rearrange("p t e -> p (t e)")
                    pe.matmul(rank_bank[:, 0:NT * E], before, picked, start=True, stop=True)
                    pe.matmul(count_bank[:, 0:NT * E], ones16, picked, start=True, stop=True).then_inc(ranks_done, 1)

                    def token(n, u, start=False, stop=False):
                        pe.wait_ge(hot_ready, 3 * n + 3)
                        pe.matmul(token_bank[:, 0:2 * W], hot_lane[u], hot_tile[u].rearrange("p a w -> p (a w)"),
                                  start=start, stop=stop, skip_group_check=True).then_inc(hot_used, 1)
                    token(0, 0, start=True)
                    token(1, 1)
                    with pe.Fori(1, NT - 1) as i:
                        token(2 * i, 0)
                        token(2 * i + 1, 1)
                    token(2 * NT - 2, 0)
                    token(2 * NT - 1, 1, stop=True)

                @block.vector
                def _(dve):
                    v = nc.vector
                    done = [0]

                    def link(ins):
                        done[0] += 1
                        ins.then_inc(step, 1)
                        dve.wait_ge(step, done[0])

                    dve.wait_ge(consts, CONSTS)
                    for c in range(2):
                        src = logits[:, :, :] if c == 0 else rest
                        link(v.tensor_reduce(top[c], src, AX, ALU.max))
                        link(v.tensor_tensor(eq, src, over_experts(top[c]), ALU.is_equal))
                        link(v.tensor_tensor(cand, eq, rev, ALU.mult))
                        link(v.tensor_reduce(first_of, cand, AX, ALU.max))
                        link(v.tensor_tensor(pick[c], cand, over_experts(first_of), ALU.is_equal))
                        if c == 0:
                            link(v.scalar_tensor_tensor(rest.rearrange("p t e -> p (t e)"),
                                                        pick[0].rearrange("p t e -> p (t e)"), -3e38,
                                                        logits[:, :, :].rearrange("p t e -> p (t e)"),
                                                        ALU.mult, ALU.add))
                    v.tensor_tensor(both16, pick[0], pick[1], ALU.add).then_inc(picks_ready, 1)
                    v.tensor_tensor(rest, logits[:, :, :], over_experts(top[0]), ALU.subtract).then_inc(exp_asked, 1)
                    v.tensor_tensor(g2, top[1], top[0], ALU.subtract).then_inc(exp_asked, 1)
                    dve.wait_ge(ranks_done, 1)
                    by_expert = count_bank[:, 0:NT * E].rearrange("p (t e) -> p e t", e=E)
                    link(v.tensor_copy(tile_counts, by_expert))
                    link(v.tensor_tensor_scan(running.rearrange("p e t -> p (e t)"), segment.rearrange("p e t -> p (e t)"),
                                              tile_counts.rearrange("p e t -> p (e t)"), 0.0, ALU.mult, ALU.add))
                    link(v.tensor_scalar(tiles_i, running[:, :, NT - 1], float(P - 1), None, ALU.add))
                    link(v.tensor_scalar(tiles_i, tiles_i, P.bit_length() - 1, None, ALU.logical_shift_right))
                    link(v.tensor_copy(tiles_f, tiles_i))
                    link(v.tensor_tensor_scan(tiles_cum, ones_e, tiles_f, 0.0, ALU.mult, ALU.add))
                    link(v.tensor_tensor(base_slot, tiles_cum, tiles_f, ALU.subtract))
                    link(v.tensor_scalar(base_slot, base_slot, float(P), None, ALU.mult))
                    link(v.tensor_tensor(running, running, tile_counts, ALU.subtract))
                    link(v.tensor_tensor(running, running, base_slot.unsqueeze(2).to_broadcast([P, E, NT]), ALU.add))
                    link(v.tensor_tensor(place, rank_bank[:, 0:NT * E].rearrange("p (t e) -> p t e", e=E),
                                         running.rearrange("p e t -> p t e"), ALU.add))
                    for c in range(2):
                        link(v.tensor_tensor(cand, pick[c], place, ALU.mult))
                        link(v.tensor_reduce(slot_f[:, c, :], cand, AX, ALU.add))
                    link(v.tensor_copy(slot_of[:, :, :], slot_f))
                    link(v.tensor_copy(slot_hi_i, slot_f))
                    link(v.tensor_scalar(slot_lo_i, slot_hi_i, P - 1, None, ALU.bitwise_and))
                    link(v.tensor_scalar(slot_hi_i, slot_hi_i, P.bit_length() - 1, None, ALU.logical_shift_right))
                    link(v.tensor_copy(slot_lo, slot_lo_i))
                    link(v.tensor_copy(slot_hi, slot_hi_i))

                    def hot(n, u, c, t):
                        wait(dve, hot_used, n - 1)
                        v.tensor_scalar(hot_lane[u], lane, slot_lo[:, c, bass.ds(t, 1)], None,
                                        ALU.is_equal).then_inc(hot_ready, 1)
                        v.tensor_scalar(hot_tile[u][:, 0, :], column, slot_hi[:, c, bass.ds(t, 1)], part_of[:, 0:1],
                                        ALU.is_equal, ALU.mult).then_inc(hot_ready, 1)
                        v.tensor_scalar(hot_tile[u][:, 1, :], column, slot_hi[:, c, bass.ds(t, 1)],
                                        tile_row[:, bass.ds(t, 1)], ALU.is_equal, ALU.mult).then_inc(hot_ready, 1)
                    hot(0, 0, 0, 0)
                    hot(1, 1, 1, 0)
                    with dve.Fori(1, NT) as i:
                        hot(2 * i, 0, 0, i)
                        hot(2 * i + 1, 1, 1, i)

                    link(v.tensor_tensor(column_e, tiles_cum.unsqueeze(1).to_broadcast([P, W, E]),
                                         column.unsqueeze(2).to_broadcast([P, W, E]), ALU.is_le))
                    link(v.tensor_reduce(expert_f, column_e, AX, ALU.add))
                    link(v.tensor_scalar(expert_of[:, :], expert_f, float(E - 1), None, ALU.min))
                    dve.wait_ge(exp_done, 2)
                    link(v.tensor_reduce(z, pe_x, AX, ALU.add))
                    link(v.reciprocal(g1, z))
                    link(v.tensor_tensor(g2, g1, e2, ALU.mult))
                    link(v.scalar_tensor_tensor(z, g1, EPS_GATE, g2, ALU.add, ALU.add))
                    link(v.reciprocal(z, z))
                    link(v.tensor_tensor(gate[:, 0, :], g1, z, ALU.mult))
                    link(v.tensor_tensor(gate[:, 1, :], g2, z, ALU.mult))
                    dve.wait_ge(hot_used, 2 * NT)
                    link(v.tensor_copy(token_f, token_bank[:, 0:W]))
                    link(v.scalar_tensor_tensor(token_f, token_bank[:, W:2 * W], float(P), token_f, ALU.mult, ALU.add))
                    link(v.tensor_copy(token_of[:, :], token_f))

        def stage3():
            at = routed_end
            bufs = {}
            for name, shape, dt in (("xg", [2 * D], F16), ("xt", [2, KC, P], F16), ("s", [H], F32),
                                    ("h", [2, HP], F16), ("ht", [2, HC, P], F16), ("y", [D], F32),
                                    ("index", [1], U32)):
                for u in range(2):
                    v, at = carve(at, shape, dt)
                    bufs[name, u] = v
            g_banks, u_banks = (banks[0], banks[2]), (banks[1], banks[3])
            y_bank = banks[4], banks[7]
            xt_bank, ht_bank = as16(banks[5], KC, P), as16(banks[6], HC, P)
            T = SLOT_TILES

            index_ready = sem("index_ready")
            gathered = [sem("gathered0"), sem("gathered1")]
            x_turned = sem("slot_x_turned")
            xt_ready = sem("slot_xt_ready")
            gu_done = sem("slot_gu_done")
            silu_done = sem("slot_silu_done")
            h_ready = sem("slot_h_ready")
            h_hi = sem("slot_h_hi")
            h_lo = sem("slot_h_lo")
            h_turned = sem("slot_h_turned")
            ht_ready = sem("slot_ht_ready")
            y_done = sem("slot_y_done")
            y_ready = sem("slot_y_ready")
            y_stored = [sem("slot_y_stored0"), sem("slot_y_stored1")]
            pads = sem("slot_pads")

            with nc.Block() as block:
                @block.gpsimd
                def _(pool):
                    pool.memset(bufs["h", 0][:, :, H:HP], 0.0).then_inc(pads, 1)
                    pool.memset(bufs["h", 1][:, :, H:HP], 0.0).then_inc(pads, 1)

                    def gather(j, u, k):
                        wait(pool, x_turned, j - 1)
                        wait(pool, gathered[u], k * 16)
                        pool.tensor_copy(bufs["index", u], token_of[:, bass.ds(j, 1)]).then_inc(index_ready, 1)
                        wait_apart(pool, index_ready, j + 1, pads, 2)
                        pool.indirect_dma_start(bufs["xg", u], None, xn_rows, bass.IndirectOffsetOnAxis(
                            ap=bufs["index", u], axis=0)).then_inc(gathered[u], 16)
                    gather(0, 0, 0)
                    gather(1, 1, 0)
                    with pool.Fori(1, T // 2) as i:
                        gather(2 * i, 0, i)
                        gather(2 * i + 1, 1, i)

                @block.sync
                def _(sp):
                    with sp.Fori(0, T // 2) as i:
                        for u in range(2):
                            sp.wait_ge(y_ready, 2 * i + u + 1)
                            sp.dma_start(slot_rows[bass.ds((2 * i + u) * P, P), :], bufs["y", u]).then_inc(y_stored[u], 16)
                    for u in range(2):
                        sp.wait_ge(y_stored[u], T // 2 * 16)

                @block.tensor
                def _(pe):
                    def slot_turn(j, u, k):
                        pe.wait_ge(gathered[u], (k + 1) * 16)
                        wait(pe, xt_ready, j)
                        turn_tile(pe, bufs["xg", u], xt_bank).then_inc(x_turned, 1)

                    def weight(w, e, *at_):
                        c, s, a, b = at_
                        return w[:, bass.ds(e, 1), c, s, a:b].rearrange("p e n -> p (e n)")

                    def unit_in(j, u):
                        e = pe.value_load(expert_of[0:1, bass.ds(j, 1)], min_val=0, max_val=E - 1)
                        pe.wait_ge(xt_ready, j + 1)
                        wait(pe, h_ready, j - 1)
                        gate_up(pe, bufs["xt", u], lambda c, s, col: weight(w_in, e, c, s, col, col + H),
                                g_banks[u], u_banks[u]).then_inc(gu_done, 1)

                    def unit_turn(j, u):
                        pe.wait_ge(h_lo, j + 1)
                        pe.wait_ge(h_hi, j + 1)
                        wait(pe, ht_ready, j)
                        turn_hidden(pe, bufs["h", u], ht_bank).then_inc(h_turned, 1)

                    def unit_down(j, u):
                        e = pe.value_load(expert_of[0:1, bass.ds(j, 1)], min_val=0, max_val=E - 1)
                        pe.wait_ge(ht_ready, j + 1)
                        wait(pe, y_ready, j - 1)
                        down(pe, bufs["ht", u], lambda c, s: weight(w_down, e, c, s, 0, D),
                             y_bank[u], True, True).then_inc(y_done, 1)

                    def slot_tile(j, u, k, last=False):
                        if not last:
                            slot_turn(j + 1, 1 - u, k if u == 0 else k + 1)
                        unit_in(j, u)
                        if not (isinstance(j, int) and j < 1):
                            unit_turn(j - 1, 1 - u)
                        if not (isinstance(j, int) and j < 2):
                            unit_down(j - 2, u)

                    pe.wait_ge(pads, 2)
                    slot_turn(0, 0, 0)
                    for j in range(4):
                        slot_tile(j, j % 2, j // 2)
                    with pe.Fori(2, T // 2 - 1) as i:
                        slot_tile(2 * i, 0, i)
                        slot_tile(2 * i + 1, 1, i)
                    slot_tile(T - 2, 0, T // 2 - 1)
                    slot_tile(T - 1, 1, T // 2 - 1, last=True)
                    unit_turn(T - 1, 1)
                    unit_down(T - 2, 0)
                    unit_down(T - 1, 1)

                @block.scalar
                def _(act):
                    def xt_copy(j, u):
                        act.wait_ge(x_turned, j + 1)
                        wait(act, gu_done, j - 1)
                        nc.scalar.copy(bufs["xt", u], xt_bank).then_inc(xt_ready, 1)

                    def slot_tile(j, u, k, last=False):
                        if not last:
                            xt_copy(j + 1, 1 - u)
                        act.wait_ge(gu_done, j + 1)
                        wait(act, h_lo, j - 1)
                        wait(act, h_hi, j - 1)
                        nc.scalar.activation(bufs["s", u], g_banks[u][:, 0:H], ACT.Silu,
                                             scale=UNIT_SCALE).then_inc(silu_done, 1)
                        act.wait_ge(h_ready, j + 1)
                        wait(act, h_turned, j - 1)
                        nc.scalar.copy(bufs["h", u][:, 0, 0:H], bufs["s", u]).then_inc(h_hi, 1)
                        if not (isinstance(j, int) and j < 3):
                            y_copy(j - 3, 1 - u, k - 2 + u)

                    def y_copy(j, u, k):
                        act.wait_ge(y_done, j + 1)
                        wait(act, y_stored[u], k * 16)
                        nc.scalar.activation(bufs["y", u], y_bank[u][:, :], ACT.Copy, scale=Y_SCALE).then_inc(y_ready, 1)

                    xt_copy(0, 0)
                    for j in range(4):
                        slot_tile(j, j % 2, j // 2)
                    with act.Fori(2, T // 2 - 1) as i:
                        slot_tile(2 * i, 0, i)
                        slot_tile(2 * i + 1, 1, i)
                    slot_tile(T - 2, 0, T // 2 - 1)
                    slot_tile(T - 1, 1, T // 2 - 1, last=True)
                    for j in range(T - 3, T):
                        y_copy(j, j % 2, j // 2)

                @block.vector
                def _(dve):
                    def ht_copy(j, u):
                        dve.wait_ge(h_turned, j + 1)
                        wait(dve, y_done, j - 1)
                        nc.vector.tensor_copy(bufs["ht", u], ht_bank).then_inc(ht_ready, 1)

                    def slot_tile(j, u):
                        dve.wait_ge(silu_done, j + 1)
                        nc.vector.scalar_tensor_tensor(bufs["s", u], u_banks[u][:, 0:H], H_SCALE, bufs["s", u],
                                                       ALU.mult, ALU.mult).then_inc(h_ready, 1)
                        dve.wait_ge(h_hi, j + 1)
                        nc.vector.tensor_tensor(bufs["h", u][:, 1, 0:H], bufs["s", u], bufs["h", u][:, 0, 0:H],
                                                ALU.subtract).then_inc(h_lo, 1)
                        if not (isinstance(j, int) and j < 1):
                            ht_copy(j - 1, 1 - u)
                    slot_tile(0, 0)
                    slot_tile(1, 1)
                    with dve.Fori(1, T // 2) as i:
                        slot_tile(2 * i, 0)
                        slot_tile(2 * i + 1, 1)
                    ht_copy(T - 1, 1)

        def stage4():
            QT = S // P
            HALF = 512
            TH = HALF // P
            NH = S // HALF
            XG = NH * KC
            QG = NH * KC
            PG = QG + QT
            at = 0
            fold, at = carve(at, [2, KC, 2, D], F16)
            x2t = []
            for u in range(2):
                v_, at = carve(at, [2, KC, S], F16)
                x2t.append(v_)
            qt, at = carve(at, [2, KC, S], F16)
            vs, at = carve(at, [QT, 2, D], F16)
            x2, x2f = [], []
            for u in range(2):
                v_, at = carve(at, [TH, D], F32)
                x2.append(v_)
                v_, at = carve(at, [HALF], F32)
                x2f.append(v_)
            c = {}
            for name, shape, dt in (("p", [S], F32), ("p16", [2, S], F16), ("pt", [QT, 2, P], F16),
                                    ("x", [D], F32), ("f", [D], F32), ("y0", [D], F32), ("y1", [D], F32),
                                    ("xn", [D], F32), ("th", [D], F32), ("res", [D], F32),
                                    ("top", [1], F32), ("bias", [1], F32), ("inv", [1], F32),
                                    ("i0", [1], U32), ("i1", [1], U32)):
                for u in range(2):
                    c[name, u], at = carve(at, shape, dt)
            causal, at = carve(at, [P], F32)
            sums, at = carve(at, [4], F32)

            pv_banks = banks[4], banks[5]
            turn_banks = banks[6], banks[7]
            Q_SCALE = S_Q / (S_FOLD * S_X2)
            SOFT = 1.0 / (S_Q * S_X2 * float(D) ** 0.5)

            fold_loaded = sem("fold_loaded")
            causal_zeroed = sem("causal_zeroed")
            causal_ready = sem("causal_ready")
            x2_loaded = [sem("x2_loaded0"), sem("x2_loaded1")]
            x2_ready = sem("x2_ready")
            x2_turned = sem("x2_turned")
            x2_hi = sem("x2_hi")
            x2_full = sem("x2_full")
            x2_lo = sem("x2_lo")
            proj_done = sem("proj_done")
            proj_hi = sem("proj_hi")
            proj_lo = sem("proj_lo")
            scores_done = sem("scores_done")
            masked = sem("masked")
            top_ready = sem("top_ready")
            bias_ready = sem("bias_ready")
            exp_done = sem("probs_done")
            p_hi = sem("p_hi")
            p_lo = sem("p_lo")
            p_turned = sem("p_turned")
            pt_ready = sem("pt_ready")
            pv_done = sem("pv_done")
            x_loaded = [sem("res_x_loaded0"), sem("res_x_loaded1")]
            f_loaded = [sem("shared_loaded0"), sem("shared_loaded1")]
            y_index = sem("y_index")
            y_loaded = [[sem(f"y{n}_loaded{u}") for u in range(2)] for n in range(2)]
            xn_made = sem("xn_made")
            f_ready = sem("f_ready")
            tanh_done = sem("tanh_done")
            sum_scaled = sem("sum_scaled")
            inv_ready = sem("inv_ready")
            s_made = sem("s_made")
            g_made = sem("g_made")
            o_made = sem("o_made")
            res_ready = sem("res_ready")
            res_stored = [sem("res_stored0"), sem("res_stored1")]

            def turn_groups(t):
                b, i = t // QT, t % QT
                return b * sum(-(-(j + 1) // 4) for j in range(QT)) + sum(-(-(j + 1) // 4) for j in range(i))

            def proj_target(g, part):
                if g < QG:
                    h, ch = g // KC, g % KC
                    return qt[:, part, ch, h * HALF:(h + 1) * HALF]
                return vs[:, g - QG, part, :]

            with nc.Block() as block:
                @block.sync
                def _(sp):
                    def load_x2(b, h):
                        wait(sp, x2_turned, (b - 1) * XG + (h + 1) * KC)
                        r = b * S + h * HALF
                        sp.dma_start(x2[h], X_FLAT[r:r + HALF, :].rearrange("(t p) d -> p t d", p=P)
                                     ).then_inc(x2_loaded[h], 16)

                    def load_tile(t):
                        u = t % 2
                        wait(sp, res_ready, t - 1)
                        sp.dma_start(c["x", u], X_FLAT[t * P:(t + 1) * P, :]).then_inc(x_loaded[u], 16)
                        wait(sp, g_made, t - 1)
                        sp.dma_start(c["f", u], shared_rows[t * P:(t + 1) * P, :]).then_inc(f_loaded[u], 16)

                    def store_tile(t):
                        sp.wait_ge(res_ready, t + 1)
                        sp.dma_start(OUT_FLAT[t * P:(t + 1) * P, :], c["res", t % 2]).then_inc(res_stored[t % 2], 16)

                    load_x2(0, 0)
                    load_x2(0, 1)
                    sp.dma_start(fold.rearrange("p f c s d -> p (f c s d)"), folded).then_inc(fold_loaded, 16)
                    load_x2(1, 0)
                    load_x2(1, 1)
                    load_tile(0)
                    load_tile(1)
                    for t in range(NT):
                        b, i = t // QT, t % QT
                        store_tile(t)
                        if t + 2 < NT:
                            load_tile(t + 2)
                        if i == 0 and b + 2 < B:
                            load_x2(b + 2, 0)
                            load_x2(b + 2, 1)
                    for u in range(2):
                        sp.wait_ge(res_stored[u], NT // 2 * 16)

                @block.gpsimd
                def _(pool):
                    pool.memset(causal, 0.0).then_inc(causal_zeroed, 1)
                    pool.wait_ge(causal_zeroed, 1)
                    pool.affine_select(out=causal, in_=causal, compare_op=ALU.is_ge, fill=-3e38, base=0,
                                       pattern=[[-1, P]], channel_multiplier=1).then_inc(causal_ready, 1)

                    def gather(t):
                        u = t % 2
                        for n in range(2):
                            wait(pool, y_loaded[n][u], t // 2 * 16)
                            pool.tensor_copy(c[f"i{n}", u], slot_of[:, n, t:t + 1]).then_inc(y_index, 1)
                            pool.wait_ge(y_index, 2 * t + n + 1)
                            wait(pool, f_ready, 2 * (t - 2) + n + 1)
                            pool.indirect_dma_start(c[f"y{n}", u], None, slot_rows, bass.IndirectOffsetOnAxis(
                                ap=c[f"i{n}", u], axis=0)).then_inc(y_loaded[n][u], 16)

                    def normalised(t):
                        u = t % 2
                        pool.wait_ge(x_loaded[u], (t // 2 + 1) * 16)
                        wait(pool, res_ready, t - 1)
                        pool.tensor_scalar(c["xn", u], c["x", u], mean[:, t:t + 1], rstd[:, t:t + 1],
                                           ALU.subtract, ALU.mult).then_inc(xn_made, 1)

                    gather(0)
                    normalised(0)
                    gather(1)
                    normalised(1)
                    for t in range(NT):
                        u = t % 2
                        pool.wait_ge(o_made, t + 1)
                        wait(pool, res_stored[u], t // 2 * 16)
                        pool.tensor_tensor(c["res", u], c["xn", u], c["x", u], ALU.add).then_inc(res_ready, 1)
                        if t + 2 < NT:
                            gather(t + 2)
                            normalised(t + 2)

                @block.tensor
                def _(pe):
                    def turn_x2(b, k):
                        h, ch = k // KC, k % KC
                        pe.wait_ge(x2_ready, b * QT + (h + 1) * TH)
                        wait(pe, x2_lo, b * XG + k - 1)
                        if k < 2 and b >= 1:
                            wait(pe, pt_ready, turn_groups((b - 1) * QT))
                        for j in range(TH):
                            last = pe.transpose(turn_banks[k % 2][:, j * P:(j + 1) * P],
                                                x2[h][:, j, ch * P:(ch + 1) * P], ident[:, :])
                        last.then_inc(x2_turned, 1)

                    def project(b, g):
                        if g == 0:
                            pe.wait_ge(x2_lo, (b + 1) * XG)
                            pe.wait_ge(x2_hi, (b + 1) * XG)
                        if g < 4:
                            wait(pe, exp_done, b * QT)
                        else:
                            pe.wait_ge(proj_lo, b * PG + g - 3)
                        bank, xt = banks[g % 4], x2t[b % 2]
                        for k in range(KC):
                            for n, (a, w) in enumerate(PARTS):
                                if g < QG:
                                    h, ch = g // KC, g % KC
                                    left = fold[:, 0, k, a, ch * P:(ch + 1) * P]
                                    right = xt[:, w, k, h * HALF:(h + 1) * HALF]
                                else:
                                    left = xt[:, a, k, (g - QG) * P:(g - QG + 1) * P]
                                    right = fold[:, 1, k, w, :]
                                last = pe.matmul(bank[:, :], left, right, start=(k == 0 and n == 0),
                                                 stop=(k == KC - 1 and n == 2))
                        last.then_inc(proj_done, 1)

                    def scores(t):
                        b, i = t // QT, t % QT
                        if i < 2:
                            pe.wait_ge(proj_lo, (b + 1) * PG)
                            pe.wait_ge(proj_hi, (b + 1) * PG)
                        else:
                            pe.wait_ge(exp_done, t - 1)
                        for col in range(0, (i + 1) * P, HALF):
                            w = min(HALF, (i + 1) * P - col)
                            for k in range(KC):
                                for n, (a, r) in enumerate(PARTS):
                                    last = pe.matmul(wide[i % 2][:, col:col + w], qt[:, a, k, i * P:(i + 1) * P],
                                                     x2t[b % 2][:, r, k, col:col + w],
                                                     start=(k == 0 and n == 0), stop=(k == KC - 1 and n == 2))
                        last.then_inc(scores_done, 1)

                    def turn_probs(t):
                        i = t % QT
                        pe.wait_ge(p_lo, t + 1)
                        pe.wait_ge(p_hi, t + 1)
                        for n, first in enumerate(range(0, i + 1, 4)):
                            g = turn_groups(t) + n
                            wait(pe, pt_ready, g - 1)
                            if i == 0 or (i == 1 and n == 0):
                                pe.wait_ge(x2_lo, min(B, t // QT + 2) * XG)
                            bank = turn_banks[g % 2][:, :].bitcast(F16).rearrange("p (k s q) -> p k s q", k=4, s=2)
                            for k in range(first, min(first + 4, i + 1)):
                                for part in range(2):
                                    last = pe.transpose(bank[:, k - first, part, :],
                                                        c["p16", i % 2][:, part, k * P:(k + 1) * P], ident16[:, :])
                            last.then_inc(p_turned, 1)

                    def weigh(t):
                        i = t % QT
                        pe.wait_ge(pt_ready, turn_groups(t + 1))
                        wait(pe, s_made, t - 1)
                        for k in range(i + 1):
                            for n, (a, r) in enumerate(PARTS):
                                last = pe.matmul(pv_banks[t % 2][:, :], c["pt", i % 2][:, k, a, :], vs[:, k, r, :],
                                                 start=(k == 0 and n == 0), stop=(k == i and n == 2))
                        last.then_inc(pv_done, 1)

                    for k in range(XG):
                        turn_x2(0, k)
                    pe.wait_ge(fold_loaded, 16)
                    for b in range(B):
                        for g in range(PG):
                            project(b, g)
                            if g == 1 and b > 0:
                                weigh(b * QT - 1)
                            if g % 2 and b + 1 < B:
                                turn_x2(b + 1, g // 2)
                        scores(b * QT)
                        for i in range(QT):
                            t = b * QT + i
                            if i + 1 < QT:
                                scores(t + 1)
                            if i > 0:
                                weigh(t - 1)
                            turn_probs(t)
                    weigh(NT - 1)

                @block.scalar
                def _(act):
                    def x2_high(b, k):
                        h, ch = k // KC, k % KC
                        act.wait_ge(x2_turned, b * XG + k + 1)
                        if k == 0:
                            wait(act, scores_done, (b - 1) * QT)
                        nc.scalar.activation(x2t[b % 2][:, 0, ch, h * HALF:(h + 1) * HALF], turn_banks[k % 2][:, :],
                                             ACT.Identity, scale=affine_s[:, 0, ch:ch + 1],
                                             bias=affine_s[:, 1, ch:ch + 1]).then_inc(x2_hi, 1)

                    def proj_high(b, g):
                        act.wait_ge(proj_done, b * PG + g + 1)
                        nc.scalar.activation(proj_target(g, 0), banks[g % 4][:, :], ACT.Copy,
                                             scale=Q_SCALE).then_inc(proj_hi, 1)

                    def probs(t):
                        i, u = t % QT, t % 2
                        w = (i + 1) * P
                        act.wait_ge(bias_ready, t + 1)
                        wait(act, p_lo, t - 1)
                        wait(act, p_hi, t - 1)
                        wait(act, inv_ready, t - 3)
                        nc.scalar.activation(c["p", u][:, 0:w], wide[u][:, 0:w], ACT.Exp, bias=c["bias", u],
                                             scale=SOFT, accum_out=sums[:, t % 4:t % 4 + 1]).then_inc(exp_done, 1)
                        act.wait_ge(exp_done, t + 1)
                        wait(act, p_turned, turn_groups(t - 1))
                        nc.scalar.copy(c["p16", u][:, 0, 0:w], c["p", u][:, 0:w]).then_inc(p_hi, 1)

                    def pt_copy(t):
                        i = t % QT
                        for n, first in enumerate(range(0, i + 1, 4)):
                            g = turn_groups(t) + n
                            act.wait_ge(p_turned, g + 1)
                            wait(act, pv_done, t - 1)
                            k = min(4, i + 1 - first)
                            nc.scalar.copy(c["pt", i % 2][:, first:first + k],
                                           turn_banks[g % 2][:, :].bitcast(F16).rearrange(
                                               "p (k s q) -> p k s q", k=4, s=2)[:, 0:k]).then_inc(pt_ready, 1)

                    def tanh(t):
                        u = t % 2
                        act.wait_ge(f_ready, 2 * t + 2)
                        wait(act, o_made, t - 1)
                        nc.scalar.activation(c["th", u], c["f", u], ACT.Tanh, scale=0.5).then_inc(tanh_done, 1)

                    for k in range(XG):
                        x2_high(0, k)
                    for b in range(B):
                        if b > 0:
                            pt_copy(b * QT - 1)
                        for g in range(PG):
                            proj_high(b, g)
                            if g == 1 and b > 0:
                                tanh(b * QT - 1)
                            if g % 2 and b + 1 < B:
                                x2_high(b + 1, g // 2)
                        for i in range(QT):
                            t = b * QT + i
                            probs(t)
                            if i > 0:
                                pt_copy(t - 1)
                                tanh(t - 1)
                    pt_copy(NT - 1)
                    tanh(NT - 1)

                @block.vector
                def _(dve):
                    v = nc.vector

                    def x2_normal(b, h):
                        dve.wait_ge(x2_loaded[h], (b + 1) * 16)
                        for j in range(TH):
                            t = b * QT + h * TH + j
                            v.tensor_scalar(x2[h][:, j, :], x2[h][:, j, :], mean[:, t:t + 1], rstd2[:, t:t + 1],
                                            ALU.subtract, ALU.mult).then_inc(x2_ready, 1)

                    def x2_split(b, k):
                        h, ch = k // KC, k % KC
                        dve.wait_ge(x2_turned, b * XG + k + 1)
                        dve.wait_ge(x2_hi, b * XG + k + 1)
                        v.tensor_scalar(x2f[k % 2], turn_banks[k % 2][:, :], affine_s[:, 0, ch:ch + 1],
                                        affine_s[:, 1, ch:ch + 1], ALU.mult, ALU.add).then_inc(x2_full, 1)
                        dve.wait_ge(x2_full, b * XG + k + 1)
                        cols = slice(h * HALF, (h + 1) * HALF)
                        v.tensor_tensor(x2t[b % 2][:, 1, ch, cols], x2f[k % 2], x2t[b % 2][:, 0, ch, cols],
                                        ALU.subtract).then_inc(x2_lo, 1)

                    def proj_low(b, g):
                        dve.wait_ge(proj_hi, b * PG + g + 1)
                        v.scalar_tensor_tensor(proj_target(g, 1), banks[g % 4][:, :], Q_SCALE, proj_target(g, 0),
                                               ALU.mult, ALU.subtract).then_inc(proj_lo, 1)

                    def soften(t):
                        i, u = t % QT, t % 2
                        diagonal = wide[u][:, i * P:(i + 1) * P]
                        dve.wait_ge(scores_done, t + 1)
                        v.tensor_tensor(diagonal, diagonal, causal, ALU.add).then_inc(masked, 1)
                        dve.wait_ge(masked, t + 1)
                        v.tensor_reduce(c["top", u], wide[u][:, 0:(i + 1) * P], AX, ALU.max).then_inc(top_ready, 1)
                        dve.wait_ge(top_ready, t + 1)
                        v.tensor_scalar(c["bias", u], c["top", u], -SOFT, LN_P, ALU.mult, ALU.add).then_inc(bias_ready, 1)

                    def p_low(t):
                        w, u = (t % QT + 1) * P, t % 2
                        dve.wait_ge(p_hi, t + 1)
                        v.tensor_tensor(c["p16", u][:, 1, 0:w], c["p", u][:, 0:w], c["p16", u][:, 0, 0:w],
                                        ALU.subtract).then_inc(p_lo, 1)

                    def mix(t):
                        u = t % 2
                        dve.wait_ge(f_loaded[u], (t // 2 + 1) * 16)
                        for n in range(2):
                            dve.wait_ge(y_loaded[n][u], (t // 2 + 1) * 16)
                            wait(dve, f_ready, 2 * t + n)
                            v.scalar_tensor_tensor(c["f", u], c[f"y{n}", u], gate[:, n, t:t + 1], c["f", u],
                                                   ALU.mult, ALU.add).then_inc(f_ready, 1)

                    def combine(t):
                        u = t % 2
                        dve.wait_ge(exp_done, t + 1)
                        v.tensor_scalar(c["inv", u], sums[:, t % 4:t % 4 + 1], S_Q, None, ALU.mult).then_inc(sum_scaled, 1)
                        dve.wait_ge(sum_scaled, t + 1)
                        v.reciprocal(c["inv", u], c["inv", u]).then_inc(inv_ready, 1)
                        dve.wait_ge(inv_ready, t + 1)
                        dve.wait_ge(xn_made, t + 1)
                        dve.wait_ge(pv_done, t + 1)
                        v.scalar_tensor_tensor(c["xn", u], pv_banks[u][:, :], c["inv", u][:, 0:1], c["xn", u],
                                               ALU.mult, ALU.add).then_inc(s_made, 1)
                        dve.wait_ge(tanh_done, t + 1)
                        v.scalar_tensor_tensor(c["th", u], c["th", u], 1.0, c["f", u], ALU.add, ALU.mult
                                               ).then_inc(g_made, 1)
                        dve.wait_ge(g_made, t + 1)
                        dve.wait_ge(s_made, t + 1)
                        v.scalar_tensor_tensor(c["xn", u], c["xn", u], 0.5, c["th", u], ALU.mult, ALU.mult
                                               ).then_inc(o_made, 1)

                    x2_normal(0, 0)
                    x2_normal(0, 1)
                    for k in range(XG):
                        x2_split(0, k)
                    dve.wait_ge(causal_ready, 1)
                    for b in range(B):
                        for g in range(PG):
                            if g in (0, PG // 2 - 1) and b + 1 < B:
                                x2_normal(b + 1, min(g, 1))
                            proj_low(b, g)
                            if g == 1 and b > 0:
                                mix(b * QT - 1)
                            if g == 3 and b > 0:
                                combine(b * QT - 1)
                            if g % 2 and b + 1 < B:
                                x2_split(b + 1, g // 2)
                        for i in range(QT):
                            t = b * QT + i
                            soften(t)
                            if i > 0:
                                mix(t - 1)
                            p_low(t)
                            if i > 1:
                                combine(t - 2)
                        combine(b * QT + QT - 2)
                    mix(NT - 1)
                    combine(NT - 1)

        stage0()
        stage1()
        stage2()
        stage3()
        stage4()


_INS = ['L0_attn_x', 'L0_attn_qkv', 'L0_attn_o_proj', 'L0_attn_gamma', 'L0_attn_beta', 'L0_ffn_router_w',
        'L0_ffn_wg', 'L0_ffn_wu', 'L0_ffn_wd', 'L0_ffn_sg', 'L0_ffn_su', 'L0_ffn_sd']
_OUTS = [((4, 1024, 512), 'float32')]


def kernel(**inputs):
    import numpy as _np
    import concourse.bacc as _bacc
    from concourse import mybir as _mybir
    from concourse.bass_utils import run_bass_kernel_spmd as _run

    nc = _bacc.Bacc("TRN2", target_bir_lowering=False, num_devices=1)
    arrays, args = {}, []
    for name in _INS:
        a = _np.ascontiguousarray(inputs[name])
        arrays[f"in_{name}_dram"] = a
        args.append(nc.dram_tensor(f"in_{name}_dram", a.shape, _mybir.dt.from_np(a.dtype), kind="ExternalInput").ap())
    for i, (shape, dtype) in enumerate(_OUTS):
        dt = _mybir.dt.from_np(_np.dtype(dtype))
        args.append(nc.dram_tensor(f"out_{i}_dram", shape, dt, kind="ExternalOutput").ap())
    mixture_attention_kernel(nc, *args)
    r = _run(nc, [arrays], core_ids=[0])
    got = tuple(r.results[0][f"out_{i}_dram"] for i in range(len(_OUTS)))
    return got[0]
```

```python
from contextlib import ExitStack

import concourse.bass as bass
from concourse import mybir

F32, F16 = mybir.dt.float32, mybir.dt.float16
I32, U32 = mybir.dt.int32, mybir.dt.uint32
ALU = mybir.AluOpType
ACT = mybir.ActivationFunctionType
AX = mybir.AxisListType.X

P = 128
S_XN = 64.0
S_W = 256.0
S_H = 16.0
S_QKVO = 64.0
S_FOLD = 16.0
S_X2 = 16.0
S_Q = 4.0
LN_P = 6.931471805599453
EPS_LN = 1e-5
EPS_GATE = 1e-20


def mixture_attention_kernel(nc, x, qkv, o_proj, gamma, beta, router_w, wg, wu, wd, sg, su, sd, out):
    B, S, D = x.shape
    E, _, H = wg.shape
    N = B * S
    KC = D // P
    NT = N // P
    HC = -(-H // P)
    HP = HC * P
    HR = H - (HC - 1) * P
    NS = sg.shape[1] // H
    SLOT_TILES = 2 * NT + E - 1
    X_FLAT = x.rearrange("b s d -> (b s) d")
    OUT_FLAT = out.rearrange("b s d -> (b s) d")

    xn_rows = nc.dram_tensor("xn_rows", [N, D], F32, kind="Internal").ap()
    shared_rows = nc.dram_tensor("shared_rows", [N, D], F32, kind="Internal").ap()
    slot_rows = nc.dram_tensor("slot_rows", [SLOT_TILES * P, D], F32, kind="Internal").ap()
    folded = nc.dram_tensor("folded", [P, 2 * KC * 2 * D], F16, kind="Internal").ap()

    with ExitStack() as ctx:
        def sb(name, shape, dt):
            return ctx.enter_context(nc.sbuf_tensor(name, shape, dt))

        def sem(name):
            return ctx.enter_context(nc.semaphore(name))

        def wait(eng, s, value):
            if not (isinstance(value, int) and value <= 0):
                eng.wait_ge(s, value)

        def wait_apart(eng, s, value, settled, settled_at):
            if not isinstance(value, int):
                value = eng.to_reg(value)
            eng.wait_ge(settled, settled_at)
            eng.wait_ge(s, value)

        wide = [ctx.enter_context(nc.psum_tensor(f"pair{i}", [P, 1024], F32)) for i in range(2)]
        banks = [wide[i // 2][:, (i % 2) * 512:(i % 2 + 1) * 512] for i in range(4)]
        banks += [ctx.enter_context(nc.psum_tensor(f"bank{i}", [P, 512], F32)) for i in range(4, 8)]

        ident = sb("ident", [P, P], F32)
        mean = sb("mean", [P, NT], F32)
        rstd = sb("rstd", [P, NT], F32)
        shift = sb("shift", [P, NT], F32)
        rstd2 = sb("rstd2", [P, NT], F32)
        logits = sb("logits", [P, NT, E], F32)
        gate = sb("gate", [P, 2, NT], F32)
        slot_of = sb("slot_of", [P, 2, NT], U32)
        token_of = sb("token_of", [P, SLOT_TILES], U32)
        expert_of = sb("expert_of", [P, SLOT_TILES], I32)
        rw_split = sb("rw_split", [P, KC, 2, E], F16)
        moments = sb("moments", [P, 2, 6], F32)
        mean_var = sb("mean_var", [P, 2, 2], F32)
        var_eps = sb("var_eps", [P, 2], F32)
        root_seed = sb("root_seed", [P, 2], F32)
        root = sb("root", [P, 3], F32)
        minus_half = sb("minus_half", [P, 1], F32)
        affine_s = sb("affine_s", [P, 2, KC], F32)
        arena = sb("arena", [P, 100 * 1024], F16)

        def carve(at, shape, dt):
            n = 1
            for s in shape:
                n *= s
            size = n * (4 if dt in (F32, I32, U32) else 2)
            v = arena[:, at // 2:(at + size) // 2]
            if dt != F16:
                v = v.bitcast(dt)
            names = "abcde"[:len(shape)]
            if len(shape) > 1:
                v = v.rearrange(f"p ({' '.join(names)}) -> p {' '.join(names)}",
                                **{c: s for c, s in zip(names, shape)})
            assert at + size <= 200 * 1024
            return v, at + size

        w_in, end = carve(0, [E, KC, 2, 2 * H], F16)
        w_down, end = carve(end, [E, HC, 2, D], F16)
        routed_end = end
        shared_in, end = carve(end, [NS, KC, 2, 2 * H], F16)
        shared_down, end = carve(end, [NS, HC, 2, D], F16)
        work_at = end

        PARTS = ((0, 0), (0, 1), (1, 0))

        def stage0():
            w_qkv, at = carve(0, [KC, 3 * D], F32)
            w_o, at = carve(at, [KC, D], F32)
            turned, at = carve(at, [3, KC, 2, D], F16)
            o_split, at = carve(at, [KC, 2, D], F16)
            fold, at = carve(at, [2, KC, 2, D], F16)
            raw_gate, at = carve(at, [KC, NS * H], F32)
            raw_up, at = carve(at, [KC, NS * H], F32)
            raw_down, at = carve(at, [NS, HC, D], F32)
            rw, at = carve(at, [D], F32)
            affine, at = carve(at, [P], F32)
            assert at <= routed_end

            ident_zeroed = sem("ident_zeroed")
            ident_ready = sem("ident_ready")
            qkv_loaded = [sem(f"qkv_loaded{m}") for m in range(3)]
            o_loaded = sem("o_loaded")
            small_loaded = sem("small_loaded")
            shared_loaded = [sem(f"shared_w_loaded{m}") for m in range(3)]
            pads_zeroed = sem("pads_zeroed")
            small_turned = sem("small_turned")
            affine_ready = sem("affine_ready")
            rw_hi = sem("rw_hi")
            rw_lo = sem("rw_lo")
            group_done = sem("fold_group_done")
            hi_done = sem("fold_hi_done")
            lo_done = sem("fold_lo_done")
            shared_hi = sem("shared_w_hi")
            shared_lo = sem("shared_w_lo")
            fold_stored = sem("fold_stored")

            TURNS, SPLITS, PRODUCTS = 3 * KC, KC, 2 * KC
            GROUPS = TURNS + SPLITS + PRODUCTS

            def group_target(g):
                if g < TURNS:
                    return turned[:, g // KC, g % KC], S_QKVO
                if g < TURNS + SPLITS:
                    return o_split[:, g - TURNS], S_QKVO
                n = g - TURNS - SPLITS
                return fold[:, n // KC, n % KC], S_FOLD / (S_QKVO * S_QKVO)

            def bank_turn(g):
                return g if g < TURNS else g - SPLITS

            def group_source(g):
                if TURNS <= g < TURNS + SPLITS:
                    return w_o[:, g - TURNS, :]
                return banks[bank_turn(g) % 7][:, :]

            splits = []
            for b in range(NS):
                for m, raw in enumerate((raw_gate, raw_up)):
                    splits.append((m, raw[:, :, b * H:(b + 1) * H],
                                   lambda part, b=b, m=m: shared_in[:, b, :, part, m * H:(m + 1) * H]))
            for b in range(NS):
                splits.append((2, raw_down[:, b, 0:HC - 1, :], lambda part, b=b: shared_down[:, b, 0:HC - 1, part, :]))
                splits.append((2, raw_down[0:HR, b, HC - 1, :], lambda part, b=b: shared_down[0:HR, b, HC - 1, part, :]))
            DOWN_LOADS = 2 * NS

            def shared_wait(eng, m):
                eng.wait_ge(shared_loaded[m], 16 * (DOWN_LOADS if m == 2 else 1))

            with nc.Block() as block:
                @block.sync
                def _(sp):
                    q_rows = qkv.rearrange("(c p) n -> p c n", p=P)
                    for m in range(3):
                        cols = slice(m * D, (m + 1) * D)
                        sp.dma_start(w_qkv[:, :, cols], q_rows[:, :, cols]).then_inc(qkv_loaded[m], 16)
                    sp.dma_start(w_o, o_proj.rearrange("(c p) n -> p c n", p=P)).then_inc(o_loaded, 16)
                    sp.dma_start(raw_gate, sg.rearrange("(c p) n -> p c n", p=P)).then_inc(shared_loaded[0], 16)
                    sp.dma_start(raw_up, su.rearrange("(c p) n -> p c n", p=P)).then_inc(shared_loaded[1], 16)
                    for b in range(NS):
                        rows, whole = sd[b * H:(b + 1) * H, :], (HC - 1) * P
                        sp.dma_start(raw_down[:, b, 0:HC - 1, :], rows[0:whole, :].rearrange("(c p) n -> p c n", p=P)
                                     ).then_inc(shared_loaded[2], 16)
                        sp.dma_start(raw_down[0:HR, b, HC - 1, :], rows[whole:H, :]).then_inc(shared_loaded[2], 16)
                    sp.wait_ge(lo_done, GROUPS)
                    sp.wait_ge(hi_done, GROUPS)
                    sp.dma_start(folded, fold.rearrange("p f c s d -> p (f c s d)")).then_inc(fold_stored, 16)
                    sp.wait_ge(fold_stored, 16)

                @block.gpsimd
                def _(pool):
                    pool.memset(ident[:, :], 0.0).then_inc(ident_zeroed, 1)
                    pool.wait_ge(ident_zeroed, 1)
                    pool.affine_select(out=ident[:, :], in_=ident[:, :], compare_op=ALU.not_equal, fill=1.0, base=0,
                                       pattern=[[-1, P]], channel_multiplier=1).then_inc(ident_ready, 1)
                    if HR < P:
                        pool.wait_ge(ident_ready, 1)
                        pool.memset(shared_down[HR:P, :, HC - 1], 0.0).then_inc(pads_zeroed, 1)

                @block.tensor
                def _(pe):
                    pe.wait_ge(ident_ready, 1)
                    for g in range(GROUPS):
                        if TURNS <= g < TURNS + SPLITS:
                            continue
                        turn = bank_turn(g)
                        if turn >= 7:
                            old = turn - 7 if turn - 7 < TURNS else turn - 7 + SPLITS
                            pe.wait_ge(lo_done, old + 1)
                        b = banks[turn % 7]
                        if g < TURNS:
                            m, n = g // KC, g % KC
                            if n == 0:
                                pe.wait_ge(qkv_loaded[m], 16)
                            for k in range(KC):
                                last = pe.transpose(b[:, k * P:(k + 1) * P],
                                                    w_qkv[:, k, m * D + n * P:m * D + (n + 1) * P], ident[:, :])
                        else:
                            m, k = (g - TURNS - SPLITS) // KC, (g - TURNS - SPLITS) % KC
                            if k == 0:
                                pe.wait_ge(lo_done, TURNS + SPLITS)
                                pe.wait_ge(hi_done, TURNS + SPLITS)
                            left = turned[:, 0 if m == 0 else 2]
                            right = turned[:, 1] if m == 0 else o_split
                            for n in range(KC):
                                for i, (a, c) in enumerate(PARTS):
                                    last = pe.matmul(b[:, :], left[:, n, a, k * P:(k + 1) * P], right[:, n, c, :],
                                                     start=(n == 0 and i == 0), stop=(n == KC - 1 and i == 2))
                        last.then_inc(group_done, 1)
                    pe.wait_ge(small_loaded, 48)
                    for c in range(KC):
                        pe.transpose(banks[7][:, c * E:(c + 1) * E], rw[0:E, c * P:(c + 1) * P], ident[0:E, 0:E])
                    pe.transpose(banks[7][:, KC * E:KC * E + 2 * KC], affine[0:2 * KC, :],
                                 ident[0:2 * KC, 0:2 * KC]).then_inc(small_turned, 1)

                @block.scalar
                def _(act):
                    act.dma_start(rw[0:E, :], router_w).then_inc(small_loaded, 16)
                    act.dma_start(affine[0:KC, :], gamma.rearrange("(c p) -> c p", p=P)).then_inc(small_loaded, 16)
                    act.dma_start(affine[KC:2 * KC, :], beta.rearrange("(c p) -> c p", p=P)).then_inc(small_loaded, 16)

                    def split_hi(n):
                        m, src, target = splits[n]
                        shared_wait(act, m)
                        nc.scalar.activation(target(0), src, ACT.Copy, scale=S_W).then_inc(shared_hi, 1)

                    for g in range(GROUPS):
                        if g == TURNS:
                            act.wait_ge(o_loaded, 16)
                        if not TURNS <= g < TURNS + SPLITS:
                            act.wait_ge(group_done, bank_turn(g) + 1)
                        to, scale = group_target(g)
                        nc.scalar.activation(to[:, 0, :], group_source(g), ACT.Copy, scale=scale).then_inc(hi_done, 1)
                        if g >= TURNS + SPLITS:
                            split_hi(g - TURNS - SPLITS)
                    act.wait_ge(small_turned, 1)
                    nc.scalar.activation(rw_split[:, :, 0, :], banks[7][:, 0:KC * E].rearrange(
                        "p (c e) -> p c e", c=KC), ACT.Copy, scale=S_W).then_inc(rw_hi, 1)
                    nc.scalar.activation(affine_s[:, :, :], banks[7][:, KC * E:KC * E + 2 * KC].rearrange(
                        "p (a c) -> p a c", a=2), ACT.Copy, scale=S_X2).then_inc(affine_ready, 1)

                @block.vector
                def _(dve):
                    def split_lo(n):
                        m, src, target = splits[n]
                        shared_wait(dve, m)
                        dve.wait_ge(shared_hi, n + 1)
                        nc.vector.scalar_tensor_tensor(target(1), src, S_W, target(0), ALU.mult, ALU.subtract
                                                       ).then_inc(shared_lo, 1)

                    for g in range(GROUPS):
                        if g == TURNS:
                            dve.wait_ge(o_loaded, 16)
                        dve.wait_ge(hi_done, g + 1)
                        to, scale = group_target(g)
                        nc.vector.scalar_tensor_tensor(to[:, 1, :], group_source(g), scale, to[:, 0, :],
                                                       ALU.mult, ALU.subtract).then_inc(lo_done, 1)
                        if g >= TURNS + SPLITS:
                            split_lo(g - TURNS - SPLITS)
                    dve.wait_ge(rw_hi, 1)
                    dve.wait_ge(affine_ready, 1)
                    nc.vector.scalar_tensor_tensor(
                        rw_split[:, :, 1, :], banks[7][:, 0:KC * E].rearrange("p (c e) -> p c e", c=KC), S_W,
                        rw_split[:, :, 0, :], ALU.mult, ALU.subtract).then_inc(rw_lo, 1)

        def turn_rows(pe, rows, bank, chunks):
            for c in range(chunks):
                last = pe.transpose(bank[:, c * P:(c + 1) * P], rows[:, c * P:(c + 1) * P], ident[:, :])
            return last

        def gate_up(pe, xt, weights, g_bank, u_bank):
            for c in range(KC):
                for i, (a, b) in enumerate(PARTS):
                    for bank, col in ((g_bank, 0), (u_bank, H)):
                        last = pe.matmul(bank[:, 0:H], xt[:, a, c, :], weights(c, b, col),
                                         start=(c == 0 and i == 0), stop=(c == KC - 1 and i == 2))
            return last

        def down(pe, ht, weights, bank, start, stop):
            for c in range(HC):
                for i, (a, b) in enumerate(PARTS):
                    last = pe.matmul(bank[:, :], ht[:, a, c, :], weights(c, b),
                                     start=(start and c == 0 and i == 0), stop=(stop and c == HC - 1 and i == 2))
            return last

        def chunked(bank, chunks):
            return bank[:, 0:chunks * P].rearrange("p (c t) -> p c t", c=chunks)

        UNIT_SCALE = 1.0 / (S_XN * S_W)
        H_SCALE = S_H / (S_XN * S_W)
        Y_SCALE = 1.0 / (S_H * S_W)

        def stage1():
            assert NT == KC * E and KC == 4 and HC == 3 and NS == 2
            at = work_at
            xb, xt, sbuf, ht, in_stage, down_stage = [], [], [], [], [], []
            for keep, count, shape, dt in ((xb, 4, [D], F32), (xt, 2, [2, KC, P], F16), (sbuf, 2, [HP], F32),
                                           (ht, 2, [2, HC, P], F16), (in_stage, 2, [2 * H], F32),
                                           (down_stage, 2, [D], F32)):
                for _ in range(count):
                    v, at = carve(at, shape, dt)
                    keep.append(v)
            y_out, at = carve(at, [D], F32)
            g_banks, u_banks = (banks[0], banks[2]), (banks[1], banks[3])
            y_bank, xt_bank, ht_bank, logit_bank = banks[4], banks[5], banks[6], banks[7]

            x_loaded = [sem(f"x_loaded{r}") for r in range(4)]
            stats_step = sem("stats_step")
            var_ready = sem("var_ready")
            seed_ready = sem("seed_ready")
            root_step = sem("root_step")
            rstd_kept = sem("rstd_kept")
            xn_ready = sem("xn_ready")
            xn_stored = [sem(f"xn_stored{r}") for r in range(4)]
            x_turned = sem("x_turned")
            xt_hi = sem("xt_hi")
            xt_lo = sem("xt_lo")
            logits_done = sem("logits_done")
            logits_kept = sem("logits_kept")
            gu_done = sem("gu_done")
            silu_done = sem("silu_done")
            h_ready = sem("h_ready")
            h_turned = sem("h_turned")
            ht_hi = sem("ht_hi")
            ht_lo = sem("ht_lo")
            y_done = sem("y_done")
            y_ready = sem("y_ready")
            y_stored = sem("y_stored")
            pads = sem("stage1_pads")
            in_loaded = [sem("in_loaded0"), sem("in_loaded1")]
            in_hi = sem("in_hi")
            in_lo = sem("in_lo")
            down_loaded = [sem("down_loaded0"), sem("down_loaded1")]
            down_hi = sem("down_hi")
            down_lo = sem("down_lo")

            def over_tiles(eng, tile):
                for r in range(4):
                    tile(r, r, 0, False)
                with eng.Fori(1, E - 1) as e:
                    for r in range(4):
                        tile(4 * e + r, r, e, False)
                for r in range(4):
                    tile(NT - 4 + r, r, E - 1, r == 3)

            def ahead(t, r, e, n):
                return t + n, (r + n) % 4, e + (r + n) // 4

            def early(t, n):
                return isinstance(t, int) and t < n

            def late(t, n):
                return isinstance(t, int) and t + n >= NT

            def down_rows(r):
                return P if r < HC - 1 else HR

            def w_in_part(e, r, part):
                return w_in[:, bass.ds(e, 1), r, part, :].rearrange("p e n -> p (e n)")

            def w_down_part(e, r, part):
                return w_down[0:down_rows(r), bass.ds(e, 1), r, part, :].rearrange("p e n -> p (e n)")

            with nc.Block() as block:
                @block.sync
                def _(sp):
                    def load_x(t, r, e):
                        turned_count, stored_count = (v if isinstance(v, int) else sp.to_reg(v) for v in (t - 3, e * 16))
                        wait(sp, x_turned, turned_count)
                        wait(sp, xn_stored[r], stored_count)
                        sp.dma_start(xb[r], X_FLAT[bass.ds(t * P, P), :]).then_inc(x_loaded[r], 16)

                    def store_xn(t, r, e):
                        sp.wait_ge(xn_ready, t + 1)
                        sp.dma_start(xn_rows[bass.ds(t * P, P), :], xb[r]).then_inc(xn_stored[r], 16)

                    def load_weights(t, r, e):
                        u = r % 2
                        wait(sp, in_lo, t - 1)
                        for n, w in enumerate((wg, wu)):
                            sp.dma_start(in_stage[u][:, n * H:(n + 1) * H],
                                         w[bass.ds(e, 1), r * P:(r + 1) * P, :].rearrange("e p n -> (e p) n")
                                         ).then_inc(in_loaded[u], 16)
                        if r < HC:
                            wait(sp, down_lo, 3 * e + r - 1 if r else 3 * e)
                            rows = down_rows(r)
                            sp.dma_start(down_stage[u][0:rows, :],
                                         wd[bass.ds(e, 1), r * P:r * P + rows, :].rearrange("e p n -> (e p) n")
                                         ).then_inc(down_loaded[u], 16)

                    def store_y(t):
                        sp.wait_ge(y_ready, t + 1)
                        sp.dma_start(shared_rows[bass.ds(t * P, P), :], y_out).then_inc(y_stored, 16)

                    for n in range(3):
                        load_x(n, n, 0)
                    load_weights(0, 0, 0)
                    store_xn(0, 0, 0)

                    def tile(t, r, e, last):
                        if not late(t, 3):
                            load_x(*ahead(t, r, e, 3))
                        if not late(t, 1):
                            store_xn(*ahead(t, r, e, 1))
                            load_weights(*ahead(t, r, e, 1))
                        if not early(t, 1):
                            store_y(t - 1)

                    over_tiles(sp, tile)
                    store_y(NT - 1)
                    sp.wait_ge(y_stored, NT * 16)
                    for r in range(4):
                        sp.wait_ge(xn_stored[r], NT // 4 * 16)

                @block.gpsimd
                def _(pool):
                    if HR < P:
                        pool.memset(w_down[HR:P, :, HC - 1], 0.0).then_inc(pads, 1)
                        pool.wait_ge(pads, 1)
                    else:
                        pool.memset(minus_half[:, :], -0.5).then_inc(pads, 1)
                    pool.memset(minus_half[:, :], -0.5).then_inc(pads, 1)
                    pool.memset(sbuf[0][:, H:HP], 0.0).then_inc(pads, 1)
                    pool.memset(sbuf[1][:, H:HP], 0.0).then_inc(pads, 1)
                    pool.wait_ge(pads, 4)

                    def seed(t, u):
                        pool.wait_ge(var_ready, t + 1)
                        pool.tensor_tensor(root_seed[:, u:u + 1], var_eps[:, u:u + 1], minus_half[:, :],
                                           ALU.pow).then_inc(seed_ready, 1)
                    with pool.Fori(0, NT // 2) as i:
                        seed(2 * i, 0)
                        seed(2 * i + 1, 1)

                @block.tensor
                def _(pe):
                    def tile_turn(t, r):
                        pe.wait_ge(xn_ready, t + 1)
                        wait(pe, xt_lo, t)
                        turn_rows(pe, xb[r], xt_bank, KC).then_inc(x_turned, 1)

                    def router(t, u):
                        pe.wait_ge(xt_lo, t + 1)
                        wait(pe, logits_kept, t)
                        for c in range(KC):
                            for i, (a, b) in enumerate(PARTS):
                                last = pe.matmul(logit_bank[:, 0:E], xt[u][:, a, c, :], rw_split[:, c, b, :],
                                                 start=(c == 0 and i == 0), stop=(c == KC - 1 and i == 2))
                        last.then_inc(logits_done, 1)

                    def unit_in(n, u, b):
                        wait(pe, h_ready, n - 1)
                        gate_up(pe, xt[u], lambda c, s, col: shared_in[:, b, c, s, col:col + H],
                                g_banks[b], u_banks[b]).then_inc(gu_done, 1)

                    def unit_turn(n, b):
                        pe.wait_ge(h_ready, n + 1)
                        wait(pe, ht_lo, n)
                        turn_rows(pe, sbuf[b], ht_bank, HC).then_inc(h_turned, 1)

                    def unit_down(n, t, b):
                        pe.wait_ge(ht_lo, n + 1)
                        if b == 0:
                            wait(pe, y_ready, t)
                        down(pe, ht[b], lambda c, s: shared_down[:, b, c, s, :], y_bank,
                             b == 0, b == 1).then_inc(y_done, 1)

                    pe.wait_ge(pads, 4)
                    tile_turn(0, 0)

                    def tile(t, r, e, last):
                        router(t, r % 2)
                        for b in range(2):
                            n = 2 * t + b
                            if b == 1 and not last:
                                tile_turn(t + 1, (r + 1) % 4)
                            unit_in(n, r % 2, b)
                            if not early(n, 1):
                                unit_turn(n - 1, 1 - b)
                            if not early(n, 2):
                                unit_down(n - 2, t - 1, b)

                    over_tiles(pe, tile)
                    unit_turn(2 * NT - 1, 1)
                    unit_down(2 * NT - 2, NT - 1, 0)
                    unit_down(2 * NT - 1, NT - 1, 1)

                @block.scalar
                def _(act):
                    def x_high(t, u):
                        act.wait_ge(x_turned, t + 1)
                        wait(act, gu_done, 2 * t - 2)
                        nc.scalar.copy(xt[u][:, 0], chunked(xt_bank, KC)).then_inc(xt_hi, 1)

                    def silu(n, b):
                        act.wait_ge(gu_done, n + 1)
                        wait(act, h_turned, n - 1)
                        nc.scalar.activation(sbuf[b][:, 0:H], g_banks[b][:, 0:H], ACT.Silu,
                                             scale=UNIT_SCALE).then_inc(silu_done, 1)

                    def h_high(n, b):
                        act.wait_ge(h_turned, n + 1)
                        wait(act, y_done, n - 1)
                        nc.scalar.copy(ht[b][:, 0], chunked(ht_bank, HC)).then_inc(ht_hi, 1)

                    def in_high(t, r, e):
                        act.wait_ge(in_loaded[r % 2], (2 * e + r // 2 + 1) * 32)
                        nc.scalar.activation(w_in_part(e, r, 0), in_stage[r % 2], ACT.Copy, scale=S_W).then_inc(in_hi, 1)

                    def down_high(r, e):
                        act.wait_ge(down_loaded[r % 2], (2 * e + r // 2 + 1 if r % 2 == 0 else e + 1) * 16)
                        nc.scalar.activation(w_down_part(e, r, 0), down_stage[r % 2][0:down_rows(r), :], ACT.Copy,
                                             scale=S_W).then_inc(down_hi, 1)

                    def y_copy(t):
                        act.wait_ge(y_done, 2 * t + 2)
                        wait(act, y_stored, t * 16)
                        nc.scalar.activation(y_out, y_bank[:, :], ACT.Copy, scale=Y_SCALE).then_inc(y_ready, 1)

                    x_high(0, 0)

                    def tile(t, r, e, last):
                        silu(2 * t, 0)
                        if not early(t, 1):
                            h_high(2 * t - 1, 1)
                        in_high(t, r, e)
                        if not last:
                            x_high(t + 1, (r + 1) % 2)
                        silu(2 * t + 1, 1)
                        h_high(2 * t, 0)
                        if r < HC:
                            down_high(r, e)
                        if not early(t, 1):
                            y_copy(t - 1)

                    over_tiles(act, tile)
                    h_high(2 * NT - 1, 1)
                    y_copy(NT - 1)

                @block.vector
                def _(dve):
                    v = nc.vector

                    def stats(t, r, e):
                        u = r % 2
                        dve.wait_ge(x_loaded[r], (e + 1) * 16)
                        v.bn_stats(moments[:, u, :], xb[r]).then_inc(stats_step, 1)
                        wait_apart(dve, stats_step, 3 * t + 1, pads, 4)
                        v.bn_aggr(mean_var[:, u, :], moments[:, u, :]).then_inc(stats_step, 1)
                        dve.wait_ge(stats_step, 3 * t + 2)
                        v.tensor_scalar(var_eps[:, u:u + 1], mean_var[:, u, 1:2], EPS_LN, None, ALU.add
                                        ).then_inc(var_ready, 1)
                        v.tensor_copy(mean[:, bass.ds(t, 1)], mean_var[:, u, 0:1]).then_inc(stats_step, 1)

                    def normalise(t, r):
                        u = r % 2
                        s = root_seed[:, u:u + 1]
                        dve.wait_ge(seed_ready, t + 1)
                        v.scalar_tensor_tensor(root[:, 0:1], s, s, var_eps[:, u:u + 1], ALU.mult, ALU.mult
                                               ).then_inc(root_step, 1)
                        dve.wait_ge(root_step, 3 * t + 1)
                        v.tensor_scalar(root[:, 1:2], root[:, 0:1], -0.5, 1.5, ALU.mult, ALU.add).then_inc(root_step, 1)
                        dve.wait_ge(root_step, 3 * t + 2)
                        v.scalar_tensor_tensor(root[:, 2:3], root[:, 1:2], S_XN, s, ALU.mult, ALU.mult
                                               ).then_inc(root_step, 1)
                        v.tensor_tensor(rstd[:, bass.ds(t, 1)], root[:, 1:2], s, ALU.mult).then_inc(rstd_kept, 1)
                        dve.wait_ge(root_step, 3 * t + 3)
                        v.tensor_scalar(xb[r], xb[r], mean_var[:, u, 0:1], root[:, 2:3], ALU.subtract, ALU.mult
                                        ).then_inc(xn_ready, 1)

                    def x_low(t, u):
                        dve.wait_ge(xt_hi, t + 1)
                        v.tensor_tensor(xt[u][:, 1], chunked(xt_bank, KC), xt[u][:, 0], ALU.subtract
                                        ).then_inc(xt_lo, 1)

                    def hidden(n, b):
                        dve.wait_ge(silu_done, n + 1)
                        v.scalar_tensor_tensor(sbuf[b][:, 0:H], u_banks[b][:, 0:H], H_SCALE, sbuf[b][:, 0:H],
                                               ALU.mult, ALU.mult).then_inc(h_ready, 1)

                    def h_low(n, b):
                        dve.wait_ge(ht_hi, n + 1)
                        v.tensor_tensor(ht[b][:, 1], chunked(ht_bank, HC), ht[b][:, 0], ALU.subtract
                                        ).then_inc(ht_lo, 1)

                    def in_low(t, r, e):
                        dve.wait_ge(in_hi, t + 1)
                        v.scalar_tensor_tensor(w_in_part(e, r, 1), in_stage[r % 2], S_W, w_in_part(e, r, 0),
                                               ALU.mult, ALU.subtract).then_inc(in_lo, 1)

                    def down_low(r, e):
                        dve.wait_ge(down_hi, 3 * e + r + 1)
                        v.scalar_tensor_tensor(w_down_part(e, r, 1), down_stage[r % 2][0:down_rows(r), :], S_W,
                                               w_down_part(e, r, 0), ALU.mult, ALU.subtract).then_inc(down_lo, 1)

                    def keep_logits(t):
                        dve.wait_ge(logits_done, t + 1)
                        v.tensor_copy(logits[:, bass.ds(t, 1), :].rearrange("p t e -> p (t e)"),
                                      logit_bank[:, 0:E]).then_inc(logits_kept, 1)

                    stats(0, 0, 0)
                    stats(1, 1, 0)
                    normalise(0, 0)
                    x_low(0, 0)

                    def tile(t, r, e, last):
                        if not late(t, 1):
                            normalise(t + 1, (r + 1) % 4)
                        if not late(t, 2):
                            stats(*ahead(t, r, e, 2))
                        hidden(2 * t, 0)
                        if not early(t, 1):
                            h_low(2 * t - 1, 1)
                        keep_logits(t)
                        in_low(t, r, e)
                        if not last:
                            x_low(t + 1, (r + 1) % 2)
                        hidden(2 * t + 1, 1)
                        h_low(2 * t, 0)
                        if r < HC:
                            down_low(r, e)

                    over_tiles(dve, tile)
                    h_low(2 * NT - 1, 1)

        def stage2():
            at = routed_end
            sh = {}

            def new(name, shape, dt=F32):
                nonlocal at
                sh[name], at = carve(at, shape, dt)
                return sh[name]

            W = SLOT_TILES
            eq, cand, rest, pe_x = (new(n, [NT, E]) for n in ("eq", "cand", "rest", "pe_x"))
            pick = [new(f"pick{c}", [NT, E]) for c in range(2)]
            top = [new(f"top{c}", [NT]) for c in range(2)]
            first_of, e2, z, g1, g2 = (new(n, [NT]) for n in ("first_of", "e2", "z", "g1", "g2"))
            rev = new("rev", [NT, E])
            both16 = new("both16", [NT, E], F16)
            before = new("before", [P], F16)
            ones16 = new("ones16", [P], F16)
            tile_counts, running, segment = (new(n, [E, NT]) for n in ("tile_counts", "running", "segment"))
            place = new("place", [NT, E])
            padded, tiles_f, tiles_cum, base_slot, ones_e = (
                new(n, [E]) for n in ("padded", "tiles_f", "tiles_cum", "base_slot", "ones_e"))
            tiles_i = new("tiles_i", [E], I32)
            column = new("column", [W])
            column_e = new("column_e", [W, E])
            expert_f = new("expert_f", [W])
            slot_f = new("slot_f", [2, NT])
            slot_hi_i, slot_lo_i = new("slot_hi_i", [2, NT], I32), new("slot_lo_i", [2, NT], I32)
            slot_hi, slot_lo = new("slot_hi", [2, NT]), new("slot_lo", [2, NT])
            lane = new("lane", [P])
            token_mid = new("token_mid", [NT])
            hot_lane = [new(f"hot_lane{c}", [NT, P], F16) for c in range(2)]
            in_tile = [new(f"in_tile{c}", [NT, W], F16) for c in range(2)]
            hot_tile = [new(f"hot_tile{c}", [NT, W], F16) for c in range(2)]
            var2, seed2, root2, half2 = (new(n, [NT]) for n in ("var2", "seed2", "root2", "half2"))

            consts = sem("routing_consts")
            ones_set = sem("ones_set")
            step = sem("routing_step")
            exp_asked = sem("exp_asked")
            exp_done = sem("exp_done")
            picks_ready = sem("picks_ready")
            ranks_done = sem("ranks_done")
            lane_ready = sem("hot_lane_ready")
            in_tile_ready = sem("in_tile_ready")
            hot_ready = sem("hot_tile_ready")
            var2_ready = sem("var2_ready")
            seed2_ready = sem("seed2_ready")
            tokens_done = sem("tokens_done")
            rank_bank, count_bank, token_bank = banks[0], banks[1], banks[2]

            def over_experts(v):
                return v.unsqueeze(2).to_broadcast([P, v.shape[1], E])

            with nc.Block() as block:
                @block.gpsimd
                def _(pool):
                    n = [0]

                    def put(ins):
                        n[0] += 1
                        ins.then_inc(consts, 1)
                    imprecise = dict(allow_small_or_imprecise_dtypes=True)
                    put(pool.iota(rev, [[0, NT], [-1, E]], base=E, channel_multiplier=0, **imprecise))
                    put(pool.iota(column, [[1, W]], base=0, channel_multiplier=0, **imprecise))
                    put(pool.iota(lane, [[1, P]], base=0, channel_multiplier=0, **imprecise))
                    put(pool.iota(token_mid, [[P, NT]], base=-(N // 2), channel_multiplier=1, **imprecise))
                    put(pool.memset(half2, -0.5))
                    put(pool.memset(ones_e, 1.0))
                    pool.memset(ones16, 1.0).then_inc(ones_set, 1)
                    pool.wait_ge(ones_set, 1)
                    put(pool.affine_select(out=before, in_=ones16, compare_op=ALU.is_gt, fill=0.0, base=0,
                                           pattern=[[1, P]], channel_multiplier=-1))
                    put(pool.memset(segment, 1.0))
                    pool.wait_ge(consts, n[0])
                    put(pool.memset(segment[:, :, 0:1], 0.0))
                    pool.wait_ge(var2_ready, 1)
                    pool.tensor_tensor(seed2, var2, half2, ALU.pow).then_inc(seed2_ready, 1)
                    for c in range(2):
                        pool.wait_ge(in_tile_ready, c + 1)
                        pool.tensor_tensor(hot_tile[c], in_tile[c], token_mid.unsqueeze(2).to_broadcast([P, NT, W]),
                                           ALU.mult).then_inc(hot_ready, 1)
                CONSTS = 9

                @block.scalar
                def _(act):
                    act.wait_ge(exp_asked, 1)
                    nc.scalar.activation(pe_x, rest, ACT.Exp, scale=UNIT_SCALE).then_inc(exp_done, 1)
                    act.wait_ge(exp_asked, 2)
                    nc.scalar.activation(e2, g2, ACT.Exp, scale=UNIT_SCALE).then_inc(exp_done, 1)

                @block.tensor
                def _(pe):
                    pe.wait_ge(picks_ready, 1)
                    pe.wait_ge(consts, CONSTS)
                    picked = both16.rearrange("p t e -> p (t e)")
                    pe.matmul(rank_bank[:, 0:NT * E], before, picked, start=True, stop=True)
                    pe.matmul(count_bank[:, 0:NT * E], ones16, picked, start=True, stop=True).then_inc(ranks_done, 1)

                    def token(c, t, start, stop):
                        return pe.matmul(token_bank[:, 0:W], hot_lane[c][:, t, :], hot_tile[c][:, t, :], start=start, stop=stop, skip_group_check=True)
                    for c in range(2):
                        pe.wait_ge(lane_ready, c + 1)
                        pe.wait_ge(hot_ready, c + 1)
                        for t in range(NT):
                            last = token(c, t, start=(c == 0 and t == 0), stop=(c == 1 and t == NT - 1))
                    last.then_inc(tokens_done, 1)

                @block.vector
                def _(dve):
                    v = nc.vector
                    done = [0]

                    def link(ins):
                        done[0] += 1
                        ins.then_inc(step, 1)
                        dve.wait_ge(step, done[0])

                    link(v.tensor_tensor(var2, rstd[:, :], rstd[:, :], ALU.mult))
                    v.tensor_scalar(var2, var2, -EPS_LN, 1.0 + EPS_LN, ALU.mult, ALU.add).then_inc(var2_ready, 1)
                    link(v.scalar_tensor_tensor(shift[:, :], mean[:, :], -1.0, rstd[:, :], ALU.mult, ALU.mult))
                    dve.wait_ge(consts, CONSTS)
                    for c in range(2):
                        src = logits[:, :, :] if c == 0 else rest
                        link(v.tensor_reduce(top[c], src, AX, ALU.max))
                        link(v.tensor_tensor(eq, src, over_experts(top[c]), ALU.is_equal))
                        link(v.tensor_tensor(cand, eq, rev, ALU.mult))
                        link(v.tensor_reduce(first_of, cand, AX, ALU.max))
                        link(v.tensor_tensor(pick[c], cand, over_experts(first_of), ALU.is_equal))
                        if c == 0:
                            link(v.scalar_tensor_tensor(rest.rearrange("p t e -> p (t e)"),
                                                        pick[0].rearrange("p t e -> p (t e)"), -3e38,
                                                        logits[:, :, :].rearrange("p t e -> p (t e)"),
                                                        ALU.mult, ALU.add))
                    v.tensor_tensor(both16, pick[0], pick[1], ALU.add).then_inc(picks_ready, 1)
                    v.tensor_tensor(rest, logits[:, :, :], over_experts(top[0]), ALU.subtract).then_inc(exp_asked, 1)
                    v.tensor_tensor(g2, top[1], top[0], ALU.subtract).then_inc(exp_asked, 1)
                    dve.wait_ge(ranks_done, 1)
                    by_expert = count_bank[:, 0:NT * E].rearrange("p (t e) -> p e t", e=E)
                    link(v.tensor_copy(tile_counts, by_expert))
                    link(v.tensor_tensor_scan(running.rearrange("p e t -> p (e t)"), segment.rearrange("p e t -> p (e t)"),
                                              tile_counts.rearrange("p e t -> p (e t)"), 0.0, ALU.mult, ALU.add))
                    link(v.tensor_scalar(tiles_i, running[:, :, NT - 1], float(P - 1), None, ALU.add))
                    link(v.tensor_scalar(tiles_i, tiles_i, P.bit_length() - 1, None, ALU.logical_shift_right))
                    link(v.tensor_copy(tiles_f, tiles_i))
                    link(v.tensor_tensor_scan(tiles_cum, ones_e, tiles_f, 0.0, ALU.mult, ALU.add))
                    link(v.tensor_tensor(base_slot, tiles_cum, tiles_f, ALU.subtract))
                    link(v.tensor_scalar(base_slot, base_slot, float(P), None, ALU.mult))
                    link(v.tensor_tensor(running, running, tile_counts, ALU.subtract))
                    link(v.tensor_tensor(running, running, base_slot.unsqueeze(2).to_broadcast([P, E, NT]), ALU.add))
                    link(v.tensor_tensor(place, rank_bank[:, 0:NT * E].rearrange("p (t e) -> p t e", e=E),
                                         running.rearrange("p e t -> p t e"), ALU.add))
                    for c in range(2):
                        link(v.tensor_tensor(cand, pick[c], place, ALU.mult))
                        link(v.tensor_reduce(slot_f[:, c, :], cand, AX, ALU.add))
                    link(v.tensor_copy(slot_of[:, :, :], slot_f))
                    link(v.tensor_copy(slot_hi_i, slot_f))
                    link(v.tensor_scalar(slot_lo_i, slot_hi_i, P - 1, None, ALU.bitwise_and))
                    link(v.tensor_scalar(slot_hi_i, slot_hi_i, P.bit_length() - 1, None, ALU.logical_shift_right))
                    link(v.tensor_copy(slot_lo, slot_lo_i))
                    link(v.tensor_copy(slot_hi, slot_hi_i))

                    for c in range(2):
                        v.tensor_tensor(in_tile[c], column.unsqueeze(1).to_broadcast([P, NT, W]),
                                        slot_hi[:, c, :].unsqueeze(2).to_broadcast([P, NT, W]), ALU.is_equal
                                        ).then_inc(in_tile_ready, 1)
                        v.tensor_tensor(hot_lane[c], lane.unsqueeze(1).to_broadcast([P, NT, P]),
                                        slot_lo[:, c, :].unsqueeze(2).to_broadcast([P, NT, P]), ALU.is_equal
                                        ).then_inc(lane_ready, 1)

                    link(v.tensor_tensor(column_e, tiles_cum.unsqueeze(1).to_broadcast([P, W, E]),
                                         column.unsqueeze(2).to_broadcast([P, W, E]), ALU.is_le))
                    link(v.tensor_reduce(expert_f, column_e, AX, ALU.add))
                    link(v.tensor_scalar(expert_of[:, :], expert_f, float(E - 1), None, ALU.min))
                    dve.wait_ge(exp_done, 2)
                    link(v.tensor_reduce(z, pe_x, AX, ALU.add))
                    link(v.reciprocal(g1, z))
                    link(v.tensor_tensor(g2, g1, e2, ALU.mult))
                    link(v.scalar_tensor_tensor(z, g1, EPS_GATE, g2, ALU.add, ALU.add))
                    link(v.reciprocal(z, z))
                    link(v.tensor_tensor(gate[:, 0, :], g1, z, ALU.mult))
                    link(v.tensor_tensor(gate[:, 1, :], g2, z, ALU.mult))
                    dve.wait_ge(seed2_ready, 1)
                    link(v.tensor_tensor(root2, seed2, seed2, ALU.mult))
                    dve.wait_ge(var2_ready, 1)
                    link(v.tensor_tensor(root2, root2, var2, ALU.mult))
                    link(v.tensor_scalar(root2, root2, -0.5, 1.5, ALU.mult, ALU.add))
                    link(v.tensor_tensor(root2, root2, seed2, ALU.mult))
                    link(v.tensor_tensor(rstd2[:, :], root2, rstd[:, :], ALU.mult))
                    link(v.tensor_scalar(rstd[:, :], rstd[:, :], S_Q, None, ALU.mult))
                    link(v.tensor_scalar(shift[:, :], shift[:, :], S_Q, None, ALU.mult))
                    dve.wait_ge(tokens_done, 1)
                    link(v.tensor_scalar(token_of[:, :], token_bank[:, 0:W], float(N // 2), None, ALU.add))


        early4, end4 = {}, routed_end + 32 * 1024
        for name, shape, dt in (("x2_0", [512 // P, D], F32), ("x2_1", [512 // P, D], F32),
                                ("fold", [2, KC, 2, D], F16)):
            early4[name], end4 = carve(end4, shape, dt)
        fold_loaded = sem("fold_loaded")
        x2_loaded = [sem("x2_loaded0"), sem("x2_loaded1")]

        def stage3():
            at = routed_end
            bufs = {}
            for name, shape, dt in (("xg", [D], F32), ("xt", [2, KC, P], F16), ("s", [HP], F32),
                                    ("ht", [2, HC, P], F16), ("y", [D], F32), ("index", [1], U32)):
                for u in range(2):
                    bufs[name, u], at = carve(at, shape, dt)
            assert at <= routed_end + 32 * 1024
            g_banks, u_banks = (banks[0], banks[2]), (banks[1], banks[3])
            y_bank = banks[4], banks[7]
            xt_bank, ht_bank = banks[5], banks[6]
            T = SLOT_TILES
            assert T % 2 == 1

            index_ready = sem("index_ready")
            gathered = [sem("gathered0"), sem("gathered1")]
            x_turned = sem("slot_x_turned")
            xt_hi = sem("slot_xt_hi")
            xt_lo = sem("slot_xt_lo")
            gu_done = sem("slot_gu_done")
            silu_done = sem("slot_silu_done")
            h_ready = sem("slot_h_ready")
            h_turned = sem("slot_h_turned")
            ht_hi = sem("slot_ht_hi")
            ht_lo = sem("slot_ht_lo")
            y_done = sem("slot_y_done")
            y_ready = sem("slot_y_ready")
            y_stored = [sem("slot_y_stored0"), sem("slot_y_stored1")]
            pads = sem("slot_pads")

            def early(j, n):
                return isinstance(j, int) and j < n

            def over_slots(eng, tile, peeled):
                for j in range(peeled):
                    tile(j, j % 2, j // 2, False)
                with eng.Fori(peeled // 2, (T - 1) // 2) as i:
                    tile(2 * i, 0, i, False)
                    tile(2 * i + 1, 1, i, False)
                tile(T - 1, 0, (T - 1) // 2, True)

            with nc.Block() as block:
                @block.gpsimd
                def _(pool):
                    pool.memset(bufs["s", 0][:, H:HP], 0.0).then_inc(pads, 1)
                    pool.memset(bufs["s", 1][:, H:HP], 0.0).then_inc(pads, 1)

                    def gather(j, u, k, last):
                        wait(pool, x_turned, j - 1)
                        wait(pool, gathered[u], k * 16)
                        pool.tensor_copy(bufs["index", u], token_of[:, bass.ds(j, 1)]).then_inc(index_ready, 1)
                        wait_apart(pool, index_ready, j + 1, pads, 2)
                        pool.indirect_dma_start(bufs["xg", u], None, xn_rows, bass.IndirectOffsetOnAxis(
                            ap=bufs["index", u], axis=0)).then_inc(gathered[u], 16)
                    over_slots(pool, gather, 2)

                @block.sync
                def _(sp):
                    for h in range(2):
                        sp.dma_start(early4[f"x2_{h}"], X_FLAT[h * 512:(h + 1) * 512, :].rearrange(
                            "(t p) d -> p t d", p=P)).then_inc(x2_loaded[h], 16)
                    sp.dma_start(early4["fold"].rearrange("p f c s d -> p (f c s d)"), folded).then_inc(fold_loaded, 16)

                    def store_y(j, u, k, last):
                        sp.wait_ge(y_ready, j + 1)
                        sp.dma_start(slot_rows[bass.ds(j * P, P), :], bufs["y", u]).then_inc(y_stored[u], 16)
                    over_slots(sp, store_y, 0)
                    sp.wait_ge(y_stored[0], (T + 1) // 2 * 16)
                    sp.wait_ge(y_stored[1], T // 2 * 16)

                @block.tensor
                def _(pe):
                    def slot_turn(j, u, k):
                        pe.wait_ge(gathered[u], (k + 1) * 16)
                        wait(pe, xt_lo, j)
                        turn_rows(pe, bufs["xg", u], xt_bank, KC).then_inc(x_turned, 1)

                    def weight(w, e, c, s, a, b):
                        return w[:, bass.ds(e, 1), c, s, a:b].rearrange("p e n -> p (e n)")

                    def unit_in(j, u):
                        e = pe.value_load(expert_of[0:1, bass.ds(j, 1)], min_val=0, max_val=E - 1)
                        pe.wait_ge(xt_lo, j + 1)
                        wait(pe, h_ready, j - 1)
                        gate_up(pe, bufs["xt", u], lambda c, s, col: weight(w_in, e, c, s, col, col + H),
                                g_banks[u], u_banks[u]).then_inc(gu_done, 1)

                    def unit_turn(j, u):
                        pe.wait_ge(h_ready, j + 1)
                        wait(pe, ht_lo, j)
                        turn_rows(pe, bufs["s", u], ht_bank, HC).then_inc(h_turned, 1)

                    def unit_down(j, u):
                        e = pe.value_load(expert_of[0:1, bass.ds(j, 1)], min_val=0, max_val=E - 1)
                        pe.wait_ge(ht_lo, j + 1)
                        wait(pe, y_ready, j - 1)
                        down(pe, bufs["ht", u], lambda c, s: weight(w_down, e, c, s, 0, D),
                             y_bank[u], True, True).then_inc(y_done, 1)

                    def slot_tile(j, u, k, last):
                        if not last:
                            slot_turn(j + 1, 1 - u, k + u)
                        unit_in(j, u)
                        if not early(j, 1):
                            unit_turn(j - 1, 1 - u)
                        if not early(j, 2):
                            unit_down(j - 2, u)

                    pe.wait_ge(pads, 2)
                    slot_turn(0, 0, 0)
                    over_slots(pe, slot_tile, 4)
                    unit_turn(T - 1, 0)
                    unit_down(T - 2, 1)
                    unit_down(T - 1, 0)

                @block.scalar
                def _(act):
                    def x_high(j, u):
                        act.wait_ge(x_turned, j + 1)
                        wait(act, gu_done, j - 1)
                        nc.scalar.copy(bufs["xt", u][:, 0], chunked(xt_bank, KC)).then_inc(xt_hi, 1)

                    def h_high(j, u):
                        act.wait_ge(h_turned, j + 1)
                        wait(act, y_done, j - 1)
                        nc.scalar.copy(bufs["ht", u][:, 0], chunked(ht_bank, HC)).then_inc(ht_hi, 1)

                    def y_copy(j, u, k):
                        act.wait_ge(y_done, j + 1)
                        wait(act, y_stored[u], k * 16)
                        nc.scalar.activation(bufs["y", u], y_bank[u][:, :], ACT.Copy, scale=Y_SCALE).then_inc(y_ready, 1)

                    def slot_tile(j, u, k, last):
                        if not last:
                            x_high(j + 1, 1 - u)
                        if not early(j, 3):
                            y_copy(j - 3, 1 - u, k - 2 + u)
                        act.wait_ge(gu_done, j + 1)
                        wait(act, h_turned, j - 1)
                        nc.scalar.activation(bufs["s", u][:, 0:H], g_banks[u][:, 0:H], ACT.Silu,
                                             scale=UNIT_SCALE).then_inc(silu_done, 1)
                        if not early(j, 1):
                            h_high(j - 1, 1 - u)

                    x_high(0, 0)
                    over_slots(act, slot_tile, 4)
                    h_high(T - 1, 0)
                    for j in range(T - 3, T):
                        y_copy(j, j % 2, j // 2)

                @block.vector
                def _(dve):
                    v = nc.vector

                    def x_low(j, u):
                        dve.wait_ge(xt_hi, j + 1)
                        v.tensor_tensor(bufs["xt", u][:, 1], chunked(xt_bank, KC), bufs["xt", u][:, 0],
                                        ALU.subtract).then_inc(xt_lo, 1)

                    def h_low(j, u):
                        dve.wait_ge(ht_hi, j + 1)
                        v.tensor_tensor(bufs["ht", u][:, 1], chunked(ht_bank, HC), bufs["ht", u][:, 0],
                                        ALU.subtract).then_inc(ht_lo, 1)

                    def slot_tile(j, u, k, last):
                        if not last:
                            x_low(j + 1, 1 - u)
                        dve.wait_ge(silu_done, j + 1)
                        v.scalar_tensor_tensor(bufs["s", u][:, 0:H], u_banks[u][:, 0:H], H_SCALE, bufs["s", u][:, 0:H],
                                               ALU.mult, ALU.mult).then_inc(h_ready, 1)
                        if not early(j, 1):
                            h_low(j - 1, 1 - u)

                    x_low(0, 0)
                    over_slots(dve, slot_tile, 2)
                    h_low(T - 1, 0)

        def stage4():
            QT = S // P
            ORDER = list(range(1, QT, 2)) + list(range(QT - 2, -1, -2))
            HALF = 512
            TH = HALF // P
            NH = S // HALF
            XG = NH * KC
            QG = NH * KC
            PG = QG + QT
            BEGIN_GROUP, END_GROUP = {3: 0, 6: 1, 9: 2, 12: 3, 15: 4}, {5: 0, 8: 1, 11: 2, 14: 3}
            BEGIN_STEP, END_STEP = {2: 5, 3: 6, 4: 7}, {1: 4, 3: 5, 4: 6, 5: 7}
            assert QT == 8 and NH == 2 and KC == 4

            fold, x2 = early4["fold"], [early4["x2_0"], early4["x2_1"]]
            at = 0
            x2t = []
            for u in range(2):
                v_, at = carve(at, [2, KC, S], F16)
                x2t.append(v_)
            qt, at = carve(at, [2, KC, S], F16)
            vs, at = carve(at, [QT, 2, D], F16)
            x2f = []
            for u in range(2):
                v_, at = carve(at, [HALF], F32)
                x2f.append(v_)
            c = {}
            for name, shape, dt in (("p", [S], F32), ("pt", [2, QT, P], F16), ("x", [D], F32), ("f", [D], F32),
                                    ("y0", [D], F32), ("y1", [D], F32), ("s", [D], F32), ("th", [D], F32),
                                    ("res", [D], F32), ("top", [1], F32), ("bias", [1], F32), ("inv", [1], F32),
                                    ("i0", [1], U32), ("i1", [1], U32)):
                for u in range(2):
                    c[name, u], at = carve(at, shape, dt)
            g, at = carve(at, [QT, D], F32)
            causal, at = carve(at, [P], F32)
            sums, at = carve(at, [4], F32)
            assert at <= routed_end + 32 * 1024

            pv_banks = banks[4], banks[5]
            turn_banks = banks[6], banks[7]
            Q_SCALE = S_Q / (S_FOLD * S_X2)
            SOFT = 1.0 / (S_Q * S_X2 * float(D) ** 0.5)

            causal_zeroed = sem("causal_zeroed")
            causal_ready = sem("causal_ready")
            x2_ready = sem("x2_ready")
            x2_turned = sem("x2_turned")
            x2_hi = sem("x2_hi")
            x2_full = sem("x2_full")
            x2_lo = sem("x2_lo")
            proj_done = sem("proj_done")
            proj_hi = sem("proj_hi")
            proj_lo = sem("proj_lo")
            scores_done = sem("scores_done")
            masked = sem("masked")
            top_ready = sem("top_ready")
            bias_ready = sem("bias_ready")
            exp_done = sem("probs_done")
            p_turned = sem("p_turned")
            pt_hi = sem("pt_hi")
            pt_lo = sem("pt_lo")
            pv_done = sem("pv_done")
            x_loaded = [sem("res_x_loaded0"), sem("res_x_loaded1")]
            f_loaded = [sem("shared_loaded0"), sem("shared_loaded1")]
            y_index = sem("y_index")
            y_loaded = [[sem(f"y{n}_loaded{u}") for u in range(2)] for n in range(2)]
            y_gated = sem("y_gated")
            y_summed = sem("y_summed")
            f_ready = sem("f_ready")
            tanh_done = sem("tanh_done")
            g_made = sem("g_made")
            xn_made = sem("xn_made")
            inv_ready = sem("inv_ready")
            s_made = sem("s_made")
            o_made = sem("o_made")
            res_ready = sem("res_ready")
            res_stored = [sem("res_stored0"), sem("res_stored1")]

            def tile_of(t):
                return ORDER[t % QT]

            def place(t):
                return t // QT * QT + tile_of(t)

            def turn_groups(t):
                return sum(-(-(tile_of(s) + 1) // 4) for s in range(t))

            def proj_target(g_, part):
                if g_ < QG:
                    h, ch = g_ // KC, g_ % KC
                    return qt[:, part, ch, h * HALF:(h + 1) * HALF]
                return vs[:, g_ - QG, part, :]

            def proj_bank(g_):
                return pv_banks[g_ - (PG - 2)] if g_ >= PG - 2 else banks[g_ % 4]

            with nc.Block() as block:
                @block.sync
                def _(sp):
                    def load_x2(b, h):
                        wait(sp, x2_turned, (b - 1) * XG + (h + 1) * KC)
                        r = b * S + h * HALF
                        sp.dma_start(x2[h], X_FLAT[r:r + HALF, :].rearrange("(t p) d -> p t d", p=P)
                                     ).then_inc(x2_loaded[h], 16)

                    def load_shared(t):
                        wait(sp, g_made, t - 1)
                        r = place(t) * P
                        sp.dma_start(c["f", t % 2], shared_rows[r:r + P, :]).then_inc(f_loaded[t % 2], 16)

                    def load_x(t):
                        wait(sp, res_ready, t - 1)
                        r = place(t) * P
                        sp.dma_start(c["x", t % 2], X_FLAT[r:r + P, :]).then_inc(x_loaded[t % 2], 16)

                    def store_tile(t):
                        sp.wait_ge(res_ready, t + 1)
                        r = place(t) * P
                        sp.dma_start(OUT_FLAT[r:r + P, :], c["res", t % 2]).then_inc(res_stored[t % 2], 16)

                    for t in range(2):
                        load_shared(t)
                        load_x(t)
                    load_x2(1, 0)
                    load_x2(1, 1)
                    for t in range(2, 5):
                        load_shared(t)
                    for b in range(B):
                        for n in range(QT):
                            t = b * QT + n
                            if n < 3:
                                load_shared(t + 5)
                            if n >= QT - 2 and b + 1 < B:
                                load_shared(t + 2)
                            if n == 0 and b + 2 < B:
                                load_x2(b + 2, 0)
                                load_x2(b + 2, 1)
                            store_tile(t)
                            if t + 2 < NT:
                                load_x(t + 2)
                        if b + 1 < B:
                            for t in range((b + 1) * QT + 2, (b + 1) * QT + 5):
                                load_shared(t)
                    for u in range(2):
                        sp.wait_ge(res_stored[u], NT // 2 * 16)

                @block.gpsimd
                def _(pool):
                    pool.memset(causal, 0.0).then_inc(causal_zeroed, 1)
                    pool.wait_ge(causal_zeroed, 1)
                    pool.affine_select(out=causal, in_=causal, compare_op=ALU.is_ge, fill=-3e38, base=0,
                                       pattern=[[-1, P]], channel_multiplier=1).then_inc(causal_ready, 1)

                    def gather(t):
                        u = t % 2
                        for n in range(2):
                            wait(pool, y_loaded[n][u], t // 2 * 16)
                            pool.tensor_copy(c[f"i{n}", u], slot_of[:, n, place(t):place(t) + 1]).then_inc(y_index, 1)
                            pool.wait_ge(y_index, 2 * t + n + 1)
                            wait(pool, f_ready, t - 1)
                            pool.indirect_dma_start(c[f"y{n}", u], None, slot_rows, bass.IndirectOffsetOnAxis(
                                ap=c[f"i{n}", u], axis=0)).then_inc(y_loaded[n][u], 16)

                    def mix(t):
                        u = t % 2
                        pool.wait_ge(y_gated, 2 * t + 2)
                        pool.tensor_tensor(c["y0", u], c["y0", u], c["y1", u], ALU.add).then_inc(y_summed, 1)
                        pool.wait_ge(f_loaded[u], (t // 2 + 1) * 16)
                        pool.wait_ge(y_summed, t + 1)
                        pool.tensor_tensor(c["f", u], c["f", u], c["y0", u], ALU.add).then_inc(f_ready, 1)
                        if t + 2 < NT:
                            gather(t + 2)

                    def finish(t):
                        u = t % 2
                        pool.wait_ge(o_made, t + 1)
                        wait(pool, res_stored[u], t // 2 * 16)
                        pool.tensor_tensor(c["res", u], c["s", u], c["x", u], ALU.add).then_inc(res_ready, 1)

                    gather(0)
                    gather(1)
                    for b in range(B):
                        for g_ in range(PG):
                            if g_ in BEGIN_GROUP:
                                mix(b * QT + BEGIN_GROUP[g_])
                            if g_ == 3 and b > 0:
                                finish(b * QT - 1)
                        for n in range(QT):
                            if n in BEGIN_STEP:
                                mix(b * QT + BEGIN_STEP[n])
                            if n > 1:
                                finish(b * QT + n - 2)
                        finish(b * QT + QT - 2)
                    finish(NT - 1)

                @block.tensor
                def _(pe):
                    def turn_x2(b, k):
                        h, ch = k // KC, k % KC
                        pe.wait_ge(x2_ready, b * QT + (h + 1) * TH)
                        wait(pe, x2_lo, b * XG + k - 1)
                        if k < 2 and b >= 1:
                            wait(pe, pt_lo, turn_groups((b - 1) * QT))
                        for j in range(TH):
                            last = pe.transpose(turn_banks[k % 2][:, j * P:(j + 1) * P],
                                                x2[h][:, j, ch * P:(ch + 1) * P], ident[:, :])
                        last.then_inc(x2_turned, 1)

                    def project(b, g_):
                        if g_ == 0:
                            pe.wait_ge(x2_lo, b * XG + (KC if b == 0 else XG))
                        if g_ == KC and b == 0:
                            pe.wait_ge(x2_lo, XG)
                        if g_ < 4:
                            wait(pe, exp_done, b * QT)
                        elif g_ < PG - 2:
                            pe.wait_ge(proj_lo, b * PG + g_ - 3)
                        else:
                            wait(pe, s_made, b * QT)
                        bank, xt = proj_bank(g_), x2t[b % 2]
                        for k in range(KC):
                            for n, (a, w) in enumerate(PARTS):
                                if g_ < QG:
                                    h, ch = g_ // KC, g_ % KC
                                    left = fold[:, 0, k, a, ch * P:(ch + 1) * P]
                                    right = xt[:, w, k, h * HALF:(h + 1) * HALF]
                                else:
                                    left = xt[:, a, k, (g_ - QG) * P:(g_ - QG + 1) * P]
                                    right = fold[:, 1, k, w, :]
                                last = pe.matmul(bank[:, :], left, right, start=(k == 0 and n == 0),
                                                 stop=(k == KC - 1 and n == 2))
                        last.then_inc(proj_done, 1)

                    def scores(t):
                        b, n, i = t // QT, t % QT, tile_of(t)
                        if n < 2:
                            pe.wait_ge(proj_lo, b * PG + PG - 2)
                        else:
                            pe.wait_ge(exp_done, t - 1)
                        for col in range(0, (i + 1) * P, HALF):
                            w = min(HALF, (i + 1) * P - col)
                            for k in range(KC):
                                for m, (a, r) in enumerate(PARTS):
                                    last = pe.matmul(wide[t % 2][:, col:col + w], qt[:, a, k, i * P:(i + 1) * P],
                                                     x2t[b % 2][:, r, k, col:col + w],
                                                     start=(k == 0 and m == 0), stop=(k == KC - 1 and m == 2))
                        last.then_inc(scores_done, 1)

                    def turn_probs(t):
                        i = tile_of(t)
                        pe.wait_ge(exp_done, t + 1)
                        for n, first in enumerate(range(0, i + 1, 4)):
                            group = turn_groups(t) + n
                            wait(pe, pt_lo, group - 1)
                            if group < turn_groups(t // QT * QT) + 2:
                                pe.wait_ge(x2_lo, min(B, t // QT + 2) * XG)
                            bank = turn_banks[group % 2]
                            for k in range(first, min(first + 4, i + 1)):
                                last = pe.transpose(bank[:, (k - first) * P:(k - first + 1) * P],
                                                    c["p", t % 2][:, k * P:(k + 1) * P], ident[:, :])
                            last.then_inc(p_turned, 1)

                    def weigh(t):
                        i = tile_of(t)
                        pe.wait_ge(pt_lo, turn_groups(t + 1))
                        wait(pe, s_made, t - 1)
                        if t % QT == 0:
                            pe.wait_ge(proj_lo, (t // QT + 1) * PG)
                        for k in range(i + 1):
                            for n, (a, r) in enumerate(PARTS):
                                last = pe.matmul(pv_banks[t % 2][:, :], c["pt", t % 2][:, a, k, :], vs[:, k, r, :],
                                                 start=(k == 0 and n == 0), stop=(k == i and n == 2))
                        last.then_inc(pv_done, 1)

                    for k in range(KC):
                        turn_x2(0, k)
                    pe.wait_ge(fold_loaded, 16)
                    for b in range(B):
                        for g_ in range(PG):
                            project(b, g_)
                            if b == 0 and g_ < 2:
                                turn_x2(0, KC + 2 * g_)
                                turn_x2(0, KC + 2 * g_ + 1)
                            if g_ == 1 and b > 0:
                                weigh(b * QT - 1)
                            if g_ % 2 and b + 1 < B:
                                turn_x2(b + 1, g_ // 2)
                            if g_ == PG - 2:
                                scores(b * QT)
                        for n in range(QT):
                            t = b * QT + n
                            if n + 1 < QT:
                                scores(t + 1)
                            if n > 0:
                                weigh(t - 1)
                            turn_probs(t)
                    weigh(NT - 1)

                @block.scalar
                def _(act):
                    def x2_high(b, k):
                        h, ch = k // KC, k % KC
                        act.wait_ge(x2_turned, b * XG + k + 1)
                        if k == 0:
                            wait(act, scores_done, (b - 1) * QT)
                        nc.scalar.activation(x2t[b % 2][:, 0, ch, h * HALF:(h + 1) * HALF], turn_banks[k % 2][:, :],
                                             ACT.Identity, scale=affine_s[:, 0, ch:ch + 1],
                                             bias=affine_s[:, 1, ch:ch + 1]).then_inc(x2_hi, 1)

                    def proj_high(b, g_):
                        act.wait_ge(proj_done, b * PG + g_ + 1)
                        nc.scalar.activation(proj_target(g_, 0), proj_bank(g_)[:, :], ACT.Copy,
                                             scale=Q_SCALE).then_inc(proj_hi, 1)

                    def probs(t):
                        u = t % 2
                        w = (tile_of(t) + 1) * P
                        act.wait_ge(bias_ready, t + 1)
                        wait(act, p_turned, turn_groups(t - 1) if t > 0 else 0)
                        wait(act, inv_ready, t - 3)
                        nc.scalar.activation(c["p", u][:, 0:w], wide[u][:, 0:w], ACT.Exp, bias=c["bias", u],
                                             scale=SOFT, accum_out=sums[:, t % 4:t % 4 + 1]).then_inc(exp_done, 1)

                    def pt_high(t):
                        i = tile_of(t)
                        for n, first in enumerate(range(0, i + 1, 4)):
                            group, k = turn_groups(t) + n, min(4, i + 1 - first)
                            act.wait_ge(p_turned, group + 1)
                            wait(act, pv_done, t - 1)
                            nc.scalar.copy(c["pt", t % 2][:, 0, first:first + k],
                                           chunked(turn_banks[group % 2], k)).then_inc(pt_hi, 1)

                    def begin(t):
                        u = t % 2
                        for n in range(2):
                            act.wait_ge(y_loaded[n][u], (t // 2 + 1) * 16)
                            nc.scalar.activation(c[f"y{n}", u], c[f"y{n}", u], ACT.Copy,
                                                 scale=gate[:, n, place(t):place(t) + 1]).then_inc(y_gated, 1)

                    def end(t):
                        u = t % 2
                        act.wait_ge(f_ready, t + 1)
                        wait(act, g_made, t - 1)
                        nc.scalar.activation(c["th", u], c["f", u], ACT.Tanh, scale=0.5).then_inc(tanh_done, 1)

                    def normal(t):
                        u, p = t % 2, place(t)
                        act.wait_ge(x_loaded[u], (t // 2 + 1) * 16)
                        wait(act, res_ready, t - 1)
                        nc.scalar.activation(c["s", u], c["x", u], ACT.Identity, scale=rstd[:, p:p + 1],
                                             bias=shift[:, p:p + 1]).then_inc(xn_made, 1)

                    for k in range(KC):
                        x2_high(0, k)
                    for b in range(B):
                        if b > 0:
                            pt_high(b * QT - 1)
                        for g_ in range(PG):
                            proj_high(b, g_)
                            if b == 0 and g_ < 2:
                                x2_high(0, KC + 2 * g_)
                                x2_high(0, KC + 2 * g_ + 1)
                            if g_ % 2 and b + 1 < B:
                                x2_high(b + 1, g_ // 2)
                            if g_ in BEGIN_GROUP:
                                begin(b * QT + BEGIN_GROUP[g_])
                            if g_ in END_GROUP:
                                end(b * QT + END_GROUP[g_])
                            if g_ in (1, 5, 9):
                                t = b * QT + (g_ - 5) // 4
                                if t >= 0:
                                    normal(t)
                        for n in range(QT):
                            t = b * QT + n
                            probs(t)
                            if n > 0:
                                pt_high(t - 1)
                            if n > 2:
                                normal(t - 1)
                            if n in BEGIN_STEP:
                                begin(b * QT + BEGIN_STEP[n])
                            if n in END_STEP:
                                end(b * QT + END_STEP[n])
                    pt_high(NT - 1)
                    normal(NT - 1)

                @block.vector
                def _(dve):
                    v = nc.vector

                    def x2_normal(b, h):
                        dve.wait_ge(x2_loaded[h], (b + 1) * 16)
                        for j in range(TH):
                            t = b * QT + h * TH + j
                            v.tensor_scalar(x2[h][:, j, :], x2[h][:, j, :], mean[:, t:t + 1], rstd2[:, t:t + 1],
                                            ALU.subtract, ALU.mult).then_inc(x2_ready, 1)

                    def x2_low(b, k):
                        h, ch = k // KC, k % KC
                        dve.wait_ge(x2_hi, b * XG + k + 1)
                        v.tensor_scalar(x2f[k % 2], turn_banks[k % 2][:, :], affine_s[:, 0, ch:ch + 1],
                                        affine_s[:, 1, ch:ch + 1], ALU.mult, ALU.add).then_inc(x2_full, 1)
                        dve.wait_ge(x2_full, b * XG + k + 1)
                        cols = slice(h * HALF, (h + 1) * HALF)
                        v.tensor_tensor(x2t[b % 2][:, 1, ch, cols], x2f[k % 2], x2t[b % 2][:, 0, ch, cols],
                                        ALU.subtract).then_inc(x2_lo, 1)

                    def proj_low(b, g_):
                        dve.wait_ge(proj_hi, b * PG + g_ + 1)
                        v.scalar_tensor_tensor(proj_target(g_, 1), proj_bank(g_)[:, :], Q_SCALE, proj_target(g_, 0),
                                               ALU.mult, ALU.subtract).then_inc(proj_lo, 1)

                    def soften(t):
                        i, u = tile_of(t), t % 2
                        diagonal = wide[u][:, i * P:(i + 1) * P]
                        dve.wait_ge(scores_done, t + 1)
                        v.tensor_tensor(diagonal, diagonal, causal, ALU.add).then_inc(masked, 1)
                        dve.wait_ge(masked, t + 1)
                        v.tensor_reduce(c["top", u], wide[u][:, 0:(i + 1) * P], AX, ALU.max).then_inc(top_ready, 1)
                        dve.wait_ge(top_ready, t + 1)
                        v.tensor_scalar(c["bias", u], c["top", u], -SOFT, LN_P, ALU.mult, ALU.add).then_inc(bias_ready, 1)

                    def pt_low(t):
                        i = tile_of(t)
                        for n, first in enumerate(range(0, i + 1, 4)):
                            group, k = turn_groups(t) + n, min(4, i + 1 - first)
                            pt = c["pt", t % 2]
                            dve.wait_ge(pt_hi, group + 1)
                            v.tensor_tensor(pt[:, 1, first:first + k], chunked(turn_banks[group % 2], k),
                                            pt[:, 0, first:first + k], ALU.subtract).then_inc(pt_lo, 1)

                    def end(t):
                        dve.wait_ge(tanh_done, t + 1)
                        wait(dve, o_made, t - QT + 1)
                        v.scalar_tensor_tensor(g[:, t % QT, :], c["th", t % 2], 1.0, c["f", t % 2], ALU.add, ALU.mult
                                               ).then_inc(g_made, 1)

                    def combine(t):
                        u = t % 2
                        dve.wait_ge(exp_done, t + 1)
                        v.reciprocal(c["inv", u], sums[:, t % 4:t % 4 + 1]).then_inc(inv_ready, 1)
                        dve.wait_ge(inv_ready, t + 1)
                        dve.wait_ge(xn_made, t + 1)
                        dve.wait_ge(pv_done, t + 1)
                        v.scalar_tensor_tensor(c["s", u], pv_banks[u][:, :], c["inv", u][:, 0:1], c["s", u],
                                               ALU.mult, ALU.add).then_inc(s_made, 1)
                        dve.wait_ge(g_made, t + 1)
                        dve.wait_ge(s_made, t + 1)
                        v.scalar_tensor_tensor(c["s", u], c["s", u], 0.5 / S_Q, g[:, t % QT, :], ALU.mult, ALU.mult
                                               ).then_inc(o_made, 1)

                    x2_normal(0, 0)
                    for k in range(KC):
                        x2_low(0, k)
                        if k == 0:
                            x2_normal(0, 1)
                    for b in range(B):
                        if b > 0:
                            pt_low(b * QT - 1)
                        for g_ in range(PG):
                            proj_low(b, g_)
                            if g_ == 3 and b > 0:
                                combine(b * QT - 1)
                            if b == 0 and g_ < 2:
                                x2_low(0, KC + 2 * g_)
                                x2_low(0, KC + 2 * g_ + 1)
                            if g_ % 2 and b + 1 < B:
                                x2_low(b + 1, g_ // 2)
                            if g_ in (0, PG // 2 - 2) and b + 1 < B:
                                x2_normal(b + 1, min(g_, 1))
                            if g_ in END_GROUP:
                                end(b * QT + END_GROUP[g_])
                        if b == 0:
                            dve.wait_ge(causal_ready, 1)
                        for n in range(QT):
                            t = b * QT + n
                            soften(t)
                            if n > 0:
                                pt_low(t - 1)
                            if n > 1:
                                combine(t - 2)
                            if n in END_STEP:
                                end(b * QT + END_STEP[n])
                        combine(b * QT + QT - 2)
                    pt_low(NT - 1)
                    combine(NT - 1)

        stage0()
        stage1()
        stage2()
        stage3()
        stage4()


_INS = ['L0_attn_x', 'L0_attn_qkv', 'L0_attn_o_proj', 'L0_attn_gamma', 'L0_attn_beta', 'L0_ffn_router_w',
        'L0_ffn_wg', 'L0_ffn_wu', 'L0_ffn_wd', 'L0_ffn_sg', 'L0_ffn_su', 'L0_ffn_sd']
_OUTS = [((4, 1024, 512), 'float32')]


def kernel(**inputs):
    import numpy as _np
    import concourse.bacc as _bacc
    from concourse import mybir as _mybir
    from concourse.bass_utils import run_bass_kernel_spmd as _run

    nc = _bacc.Bacc("TRN2", target_bir_lowering=False, num_devices=1)
    arrays, args = {}, []
    for name in _INS:
        a = _np.ascontiguousarray(inputs[name])
        arrays[f"in_{name}_dram"] = a
        args.append(nc.dram_tensor(f"in_{name}_dram", a.shape, _mybir.dt.from_np(a.dtype), kind="ExternalInput").ap())
    for i, (shape, dtype) in enumerate(_OUTS):
        dt = _mybir.dt.from_np(_np.dtype(dtype))
        args.append(nc.dram_tensor(f"out_{i}_dram", shape, dt, kind="ExternalOutput").ap())
    mixture_attention_kernel(nc, *args)
    r = _run(nc, [arrays], core_ids=[0])
    got = tuple(r.results[0][f"out_{i}_dram"] for i in range(len(_OUTS)))
    return got[0]
```

```python
from contextlib import ExitStack

import concourse.bass as bass
from concourse import mybir

F32, F16 = mybir.dt.float32, mybir.dt.float16
I32, U32 = mybir.dt.int32, mybir.dt.uint32
ALU = mybir.AluOpType
ACT = mybir.ActivationFunctionType
AX = mybir.AxisListType.X

P = 128
S_XN = 64.0
S_W = 256.0
S_H = 16.0
S_QKVO = 64.0
S_FOLD = 16.0
S_X2 = 16.0
S_Q = 4.0
LN_P = 6.931471805599453
EPS_LN = 1e-5
EPS_GATE = 1e-20


def mixture_attention_kernel(nc, x, qkv, o_proj, gamma, beta, router_w, wg, wu, wd, sg, su, sd, out):
    B, S, D = x.shape
    E, _, H = wg.shape
    N = B * S
    KC = D // P
    NT = N // P
    HC = -(-H // P)
    HP = HC * P
    HR = H - (HC - 1) * P
    NS = sg.shape[1] // H
    SLOT_TILES = 2 * NT + E - 1
    X_FLAT = x.rearrange("b s d -> (b s) d")
    OUT_FLAT = out.rearrange("b s d -> (b s) d")

    xn_rows = nc.dram_tensor("xn_rows", [N, D], F32, kind="Internal").ap()
    shared_rows = nc.dram_tensor("shared_rows", [N, D], F32, kind="Internal").ap()
    slot_rows = nc.dram_tensor("slot_rows", [SLOT_TILES * P, D], F32, kind="Internal").ap()
    folded = nc.dram_tensor("folded", [P, 2 * KC * 2 * D], F16, kind="Internal").ap()

    with ExitStack() as ctx:
        def sb(name, shape, dt):
            return ctx.enter_context(nc.sbuf_tensor(name, shape, dt))

        def sem(name):
            return ctx.enter_context(nc.semaphore(name))

        def wait(eng, s, value):
            if not (isinstance(value, int) and value <= 0):
                eng.wait_ge(s, value)

        def wait_apart(eng, s, value, settled, settled_at):
            if not isinstance(value, int):
                value = eng.to_reg(value)
            eng.wait_ge(settled, settled_at)
            eng.wait_ge(s, value)

        wide = [ctx.enter_context(nc.psum_tensor(f"pair{i}", [P, 1024], F32)) for i in range(2)]
        banks = [wide[i // 2][:, (i % 2) * 512:(i % 2 + 1) * 512] for i in range(4)]
        banks += [ctx.enter_context(nc.psum_tensor(f"bank{i}", [P, 512], F32)) for i in range(4, 8)]

        ident = sb("ident", [P, P], F32)
        mean = sb("mean", [P, NT], F32)
        rstd = sb("rstd", [P, NT], F32)
        shift = sb("shift", [P, NT], F32)
        rstd2 = sb("rstd2", [P, NT], F32)
        logits = sb("logits", [P, NT, E], F32)
        gate = sb("gate", [P, 2, NT], F32)
        slot_of = sb("slot_of", [P, 2, NT], U32)
        token_of = sb("token_of", [P, SLOT_TILES], U32)
        expert_of = sb("expert_of", [P, SLOT_TILES], I32)
        rw_split = sb("rw_split", [P, KC, 2, E], F16)
        moments = sb("moments", [P, 2, 6], F32)
        mean_var = sb("mean_var", [P, 2, 2], F32)
        var_eps = sb("var_eps", [P, 2], F32)
        root_seed = sb("root_seed", [P, 2], F32)
        root = sb("root", [P, 3], F32)
        minus_half = sb("minus_half", [P, 1], F32)
        affine_s = sb("affine_s", [P, 2, KC], F32)
        rev = sb("rev", [P, NT, E], F32)
        segment = sb("segment", [P, E, NT], F32)
        column = sb("column", [P, SLOT_TILES], F32)
        lane = sb("lane", [P, P], F32)
        token_mid = sb("token_mid", [P, NT], F32)
        half2 = sb("half2", [P, NT], F32)
        ones_e = sb("ones_e", [P, E], F32)
        before = sb("before", [P, P], F16)
        ones16 = sb("ones16", [P, P], F16)
        arena = sb("arena", [P, 100 * 1024], F16)

        def carve(at, shape, dt):
            n = 1
            for s in shape:
                n *= s
            size = n * (4 if dt in (F32, I32, U32) else 2)
            v = arena[:, at // 2:(at + size) // 2]
            if dt != F16:
                v = v.bitcast(dt)
            names = "abcde"[:len(shape)]
            if len(shape) > 1:
                v = v.rearrange(f"p ({' '.join(names)}) -> p {' '.join(names)}",
                                **{c: s for c, s in zip(names, shape)})
            assert at + size <= 200 * 1024
            return v, at + size

        w_in, end = carve(0, [E, KC, 2, 2 * H], F16)
        w_down, end = carve(end, [E, HC, 2, D], F16)
        routed_end = end
        shared_in, end = carve(end, [NS, KC, 2, 2 * H], F16)
        shared_down, end = carve(end, [NS, HC, 2, D], F16)
        xb, xb_at = [], end
        for _ in range(4):
            v_, end = carve(end, [D], F32)
            xb.append(v_)
        work_at = end
        x_loaded = [sem(f"x_loaded{r}") for r in range(4)]
        fold_stored = sem("fold_stored")
        stats_step = sem("stats_step")
        var_ready = sem("var_ready")
        seed_ready = sem("seed_ready")
        root_step = sem("root_step")
        rstd_kept = sem("rstd_kept")
        xn_ready = sem("xn_ready")
        half_set = sem("half_set")

        FIRST_SPLITS = 2
        raw_at = 80 * 1024
        raw_gate, raw_end = carve(raw_at, [KC, NS * H], F32)
        raw_up, raw_end = carve(raw_end, [KC, NS * H], F32)
        raw_down, raw_end = carve(raw_end, [NS, HC, D], F32)
        shared_loaded = [sem(f"shared_w_loaded{m}") for m in range(3)]
        shared_hi = sem("shared_w_hi")
        shared_lo = sem("shared_w_lo")

        splits = []
        for b in range(NS):
            for m, raw in enumerate((raw_gate, raw_up)):
                splits.append((m, raw[:, :, b * H:(b + 1) * H],
                               lambda part, b=b, m=m: shared_in[:, b, :, part, m * H:(m + 1) * H]))
        for b in range(NS):
            splits.append((2, raw_down[:, b, 0:HC - 1, :], lambda part, b=b: shared_down[:, b, 0:HC - 1, part, :]))
            splits.append((2, raw_down[0:HR, b, HC - 1, :], lambda part, b=b: shared_down[0:HR, b, HC - 1, part, :]))
        DOWN_LOADS = 2 * NS

        def shared_wait(eng, m):
            eng.wait_ge(shared_loaded[m], 16 * (DOWN_LOADS if m == 2 else 1))

        def split_hi(act, n):
            m, src, target = splits[n]
            shared_wait(act, m)
            nc.scalar.activation(target(0), src, ACT.Copy, scale=S_W).then_inc(shared_hi, 1)

        def split_lo(dve, n):
            m, src, target = splits[n]
            dve.wait_ge(shared_hi, n + 1)
            nc.vector.scalar_tensor_tensor(target(1), src, S_W, target(0), ALU.mult, ALU.subtract
                                           ).then_inc(shared_lo, 1)

        def seed(pool, t, u):
            pool.wait_ge(var_ready, t + 1)
            pool.tensor_tensor(root_seed[:, u:u + 1], var_eps[:, u:u + 1], minus_half[:, :],
                               ALU.pow).then_inc(seed_ready, 1)
        def stats(dve, t, r, e):
            u = r % 2
            dve.wait_ge(x_loaded[r], (e + 1) * 16)
            nc.vector.bn_stats(moments[:, u, :], xb[r]).then_inc(stats_step, 1)
            wait_apart(dve, stats_step, 3 * t + 1, half_set, 1)
            nc.vector.bn_aggr(mean_var[:, u, :], moments[:, u, :]).then_inc(stats_step, 1)
            dve.wait_ge(stats_step, 3 * t + 2)
            nc.vector.tensor_scalar(var_eps[:, u:u + 1], mean_var[:, u, 1:2], EPS_LN, None, ALU.add
                            ).then_inc(var_ready, 1)
            nc.vector.tensor_copy(mean[:, bass.ds(t, 1)], mean_var[:, u, 0:1]).then_inc(stats_step, 1)

        def normalise(dve, t, r):
            u = r % 2
            s = root_seed[:, u:u + 1]
            dve.wait_ge(seed_ready, t + 1)
            nc.vector.scalar_tensor_tensor(root[:, 0:1], s, s, var_eps[:, u:u + 1], ALU.mult, ALU.mult
                                   ).then_inc(root_step, 1)
            dve.wait_ge(root_step, 3 * t + 1)
            nc.vector.tensor_scalar(root[:, 1:2], root[:, 0:1], -0.5, 1.5, ALU.mult, ALU.add).then_inc(root_step, 1)
            dve.wait_ge(root_step, 3 * t + 2)
            nc.vector.scalar_tensor_tensor(root[:, 2:3], root[:, 1:2], S_XN, s, ALU.mult, ALU.mult
                                   ).then_inc(root_step, 1)
            nc.vector.tensor_tensor(rstd[:, bass.ds(t, 1)], root[:, 1:2], s, ALU.mult).then_inc(rstd_kept, 1)
            dve.wait_ge(root_step, 3 * t + 3)
            nc.vector.tensor_scalar(xb[r], xb[r], mean_var[:, u, 0:1], root[:, 2:3], ALU.subtract, ALU.mult
                            ).then_inc(xn_ready, 1)


        PARTS = ((0, 0), (0, 1), (1, 0))

        def stage0():
            w_qkv, at = carve(0, [KC, 3 * D], F32)
            w_o, at = carve(at, [KC, D], F32)
            turned, at = carve(at, [3, KC, 2, D], F16)
            o_split, at = carve(at, [KC, 2, D], F16)
            fold, at = carve(at, [2, KC, 2, D], F16)
            assert at <= raw_at
            rw, at = carve(raw_end, [D], F32)
            affine, at = carve(at, [P], F32)
            assert at <= routed_end

            ident_zeroed = sem("ident_zeroed")
            ident_ready = sem("ident_ready")
            qkv_loaded = [sem(f"qkv_loaded{m}") for m in range(3)]
            o_loaded = sem("o_loaded")
            small_loaded = sem("small_loaded")
            pads_zeroed = sem("pads_zeroed")
            small_turned = sem("small_turned")
            affine_ready = sem("affine_ready")
            rw_hi = sem("rw_hi")
            rw_lo = sem("rw_lo")
            group_done = sem("fold_group_done")
            hi_done = sem("fold_hi_done")
            lo_done = sem("fold_lo_done")
            groups = ([("turn", m, n) for m in range(2) for n in range(KC)]
                      + [("product", 0, k) for k in range(KC // 2)] + [("turn", 2, n) for n in range(KC)]
                      + [("product", 0, k) for k in range(KC // 2, KC - 1)] + [("split", 0, n) for n in range(KC)]
                      + [("product", 0, KC - 1)] + [("product", 1, k) for k in range(KC)])
            GROUPS = len(groups)
            in_banks = [g for g in range(GROUPS) if groups[g][0] != "split"]

            def group_target(g):
                kind, m, n = groups[g]
                if kind == "turn":
                    return turned[:, m, n], S_QKVO
                if kind == "split":
                    return o_split[:, n], S_QKVO
                return fold[:, m, n], S_FOLD / (S_QKVO * S_QKVO)

            def group_source(g):
                if groups[g][0] == "split":
                    return w_o[:, groups[g][2], :]
                return banks[in_banks.index(g) % 7][:, :]

            def splits_after(g):
                n = g - (GROUPS - KC - 1)
                return (n,) if 0 <= n < FIRST_SPLITS else ()

            with nc.Block() as block:
                @block.sync
                def _(sp):
                    q_rows = qkv.rearrange("(c p) n -> p c n", p=P)
                    for m in range(3):
                        cols = slice(m * D, (m + 1) * D)
                        sp.dma_start(w_qkv[:, :, cols], q_rows[:, :, cols]).then_inc(qkv_loaded[m], 16)
                    sp.dma_start(w_o, o_proj.rearrange("(c p) n -> p c n", p=P)).then_inc(o_loaded, 16)
                    for r in range(3):
                        sp.dma_start(xb[r], X_FLAT[r * P:(r + 1) * P, :]).then_inc(x_loaded[r], 16)
                    sp.dma_start(raw_gate, sg.rearrange("(c p) n -> p c n", p=P)).then_inc(shared_loaded[0], 16)
                    sp.dma_start(raw_up, su.rearrange("(c p) n -> p c n", p=P)).then_inc(shared_loaded[1], 16)
                    for b in range(NS):
                        rows, whole = sd[b * H:(b + 1) * H, :], (HC - 1) * P
                        sp.dma_start(raw_down[:, b, 0:HC - 1, :], rows[0:whole, :].rearrange("(c p) n -> p c n", p=P)
                                     ).then_inc(shared_loaded[2], 16)
                        sp.dma_start(raw_down[0:HR, b, HC - 1, :], rows[whole:H, :]).then_inc(shared_loaded[2], 16)
                    for m in range(2):
                        sp.wait_ge(lo_done, GROUPS - (1 - m) * KC)
                        sp.dma_start(folded[:, m * KC * 2 * D:(m + 1) * KC * 2 * D],
                                     fold[:, m].rearrange("p c s d -> p (c s d)")).then_inc(fold_stored, 16)

                @block.gpsimd
                def _(pool):
                    pool.memset(ident[:, :], 0.0).then_inc(ident_zeroed, 1)
                    pool.wait_ge(ident_zeroed, 1)
                    pool.affine_select(out=ident[:, :], in_=ident[:, :], compare_op=ALU.not_equal, fill=1.0, base=0,
                                       pattern=[[-1, P]], channel_multiplier=1).then_inc(ident_ready, 1)
                    if HR < P:
                        pool.wait_ge(ident_ready, 1)
                        pool.memset(shared_down[HR:P, :, HC - 1], 0.0).then_inc(pads_zeroed, 1)
                        pool.wait_ge(pads_zeroed, 1)
                    pool.memset(minus_half[:, :], -0.5).then_inc(half_set, 1)
                    pool.wait_ge(half_set, 1)
                    seed(pool, 0, 0)
                    seed(pool, 1, 1)

                @block.tensor
                def _(pe):
                    pe.wait_ge(ident_ready, 1)
                    for turn, g in enumerate(in_banks):
                        kind, m, n = groups[g]
                        if turn >= 7:
                            pe.wait_ge(lo_done, in_banks[turn - 7] + 1)
                        bank = banks[turn % 7]
                        if kind == "turn":
                            if n == 0:
                                pe.wait_ge(qkv_loaded[m], 16)
                            for k in range(KC):
                                last = pe.transpose(bank[:, k * P:(k + 1) * P],
                                                    w_qkv[:, k, m * D + n * P:m * D + (n + 1) * P], ident[:, :])
                        else:
                            if n == 0:
                                pe.wait_ge(lo_done, g if m == 0 else g - 1)
                            left = turned[:, 0 if m == 0 else 2]
                            right = turned[:, 1] if m == 0 else o_split
                            for c in range(KC):
                                for i, (a, b) in enumerate(PARTS):
                                    last = pe.matmul(bank[:, :], left[:, c, a, n * P:(n + 1) * P], right[:, c, b, :],
                                                     start=(c == 0 and i == 0), stop=(c == KC - 1 and i == 2))
                        last.then_inc(group_done, 1)
                        if g == 2 * KC - 1:
                            pe.wait_ge(small_loaded, 48)
                            for c in range(KC):
                                pe.transpose(banks[7][:, c * E:(c + 1) * E], rw[0:E, c * P:(c + 1) * P], ident[0:E, 0:E])
                            pe.transpose(banks[7][:, KC * E:KC * E + 2 * KC], affine[0:2 * KC, :],
                                         ident[0:2 * KC, 0:2 * KC]).then_inc(small_turned, 1)

                @block.scalar
                def _(act):
                    act.dma_start(rw[0:E, :], router_w).then_inc(small_loaded, 16)
                    act.dma_start(affine[0:KC, :], gamma.rearrange("(c p) -> c p", p=P)).then_inc(small_loaded, 16)
                    act.dma_start(affine[KC:2 * KC, :], beta.rearrange("(c p) -> c p", p=P)).then_inc(small_loaded, 16)

                    for g in range(GROUPS):
                        if groups[g][0] == "split":
                            act.wait_ge(o_loaded, 16)
                        else:
                            act.wait_ge(group_done, in_banks.index(g) + 1)
                        to, scale = group_target(g)
                        nc.scalar.activation(to[:, 0, :], group_source(g), ACT.Copy, scale=scale).then_inc(hi_done, 1)
                        if g == 2 * KC - 1:
                            act.wait_ge(small_turned, 1)
                            nc.scalar.activation(rw_split[:, :, 0, :], banks[7][:, 0:KC * E].rearrange(
                                "p (c e) -> p c e", c=KC), ACT.Copy, scale=S_W).then_inc(rw_hi, 1)
                            nc.scalar.activation(affine_s[:, :, :], banks[7][:, KC * E:KC * E + 2 * KC].rearrange(
                                "p (a c) -> p a c", a=2), ACT.Copy, scale=S_X2).then_inc(affine_ready, 1)
                        for n in splits_after(g):
                            split_hi(act, n)

                @block.vector
                def _(dve):
                    for g in range(GROUPS):
                        if groups[g][0] == "split":
                            dve.wait_ge(o_loaded, 16)
                        dve.wait_ge(hi_done, g + 1)
                        to, scale = group_target(g)
                        nc.vector.scalar_tensor_tensor(to[:, 1, :], group_source(g), scale, to[:, 0, :],
                                                       ALU.mult, ALU.subtract).then_inc(lo_done, 1)
                        if g == 2 * KC - 1:
                            dve.wait_ge(rw_hi, 1)
                            dve.wait_ge(affine_ready, 1)
                            nc.vector.scalar_tensor_tensor(
                                rw_split[:, :, 1, :], banks[7][:, 0:KC * E].rearrange("p (c e) -> p c e", c=KC), S_W,
                                rw_split[:, :, 0, :], ALU.mult, ALU.subtract).then_inc(rw_lo, 1)
                        for n in splits_after(g):
                            split_lo(dve, n)
                        if g == GROUPS - KC:
                            stats(dve, 0, 0, 0)
                            stats(dve, 1, 1, 0)
                        if g >= GROUPS - 2:
                            normalise(dve, g - (GROUPS - 2), g - (GROUPS - 2))

        def turn_rows(pe, rows, bank, chunks):
            for c in range(chunks):
                last = pe.transpose(bank[:, c * P:(c + 1) * P], rows[:, c * P:(c + 1) * P], ident[:, :])
            return last

        def gate_up(pe, xt, weights, g_bank, u_bank):
            for c in range(KC):
                for i, (a, b) in enumerate(PARTS):
                    for bank, col in ((g_bank, 0), (u_bank, H)):
                        last = pe.matmul(bank[:, 0:H], xt[:, a, c, :], weights(c, b, col),
                                         start=(c == 0 and i == 0), stop=(c == KC - 1 and i == 2))
            return last

        def down(pe, ht, weights, bank, start, stop):
            for c in range(HC):
                for i, (a, b) in enumerate(PARTS):
                    last = pe.matmul(bank[:, :], ht[:, a, c, :], weights(c, b),
                                     start=(start and c == 0 and i == 0), stop=(stop and c == HC - 1 and i == 2))
            return last

        def chunked(bank, chunks):
            return bank[:, 0:chunks * P].rearrange("p (c t) -> p c t", c=chunks)

        UNIT_SCALE = 1.0 / (S_XN * S_W)
        H_SCALE = S_H / (S_XN * S_W)
        Y_SCALE = 1.0 / (S_H * S_W)

        gate_tables = []
        exp_done = sem("exp_done")
        gate_step = sem("gate_step")
        gates_made = sem("gates_made")
        xn_stored = [sem(f"xn_stored{r}") for r in range(4)]
        shared_stored = sem("shared_rows_stored")

        def stages1and2():
            assert NT == KC * E and KC == 4 and HC == 3 and NS == 2
            at = work_at
            xt, sbuf, ht, in_stage, down_stage = [], [], [], [], []
            starts = []
            for keep, count, shape, dt in ((xt, 2, [2, KC, P], F16), (sbuf, 2, [HP], F32),
                                           (ht, 2, [2, HC, P], F16), (in_stage, 2, [2 * H], F32),
                                           (down_stage, 2, [D], F32)):
                starts.append(at)
                for _ in range(count):
                    v, at = carve(at, shape, dt)
                    keep.append(v)
            in_stage_at, down_stage_at = starts[-2:]
            y_out, at = carve(at, [D], F32)
            g_banks, u_banks = (banks[0], banks[2]), (banks[1], banks[3])
            y_bank, xt_bank, ht_bank, logit_bank = banks[4], banks[5], banks[6], banks[7]

            x_turned = sem("x_turned")
            xt_hi = sem("xt_hi")
            xt_lo = sem("xt_lo")
            logits_done = sem("logits_done")
            logits_kept = sem("logits_kept")
            gu_done = sem("gu_done")
            silu_done = sem("silu_done")
            h_ready = sem("h_ready")
            h_turned = sem("h_turned")
            ht_hi = sem("ht_hi")
            ht_lo = sem("ht_lo")
            y_done = sem("y_done")
            y_ready = sem("y_ready")
            y_stored = shared_stored
            pads = sem("stage1_pads")
            down_padded = sem("down_padded")
            in_loaded = [sem("in_loaded0"), sem("in_loaded1")]
            in_hi = sem("in_hi")
            in_lo = sem("in_lo")
            down_loaded = [sem("down_loaded0"), sem("down_loaded1")]
            down_hi = sem("down_hi")
            down_lo = sem("down_lo")

            def over_tiles(eng, tile):
                for r in range(4):
                    tile(r, r, 0, False)
                with eng.Fori(1, E - 1) as e:
                    for r in range(4):
                        tile(4 * e + r, r, e, False)
                for r in range(4):
                    tile(NT - 4 + r, r, E - 1, r == 3)

            def ahead(t, r, e, n):
                return t + n, (r + n) % 4, e + (r + n) // 4

            def split_beside(t, r):
                if isinstance(t, int) and t >= NT - 4:
                    return ((0,), (1, 2), (3,), ())[r], ((0,), (1,), (2,), ())[r]
                return (r,), ((r,) if r < HC else ())

            def early(t, n):
                return isinstance(t, int) and t < n

            def late(t, n):
                return isinstance(t, int) and t + n >= NT

            def down_rows(r):
                return P if r < HC - 1 else HR

            def w_in_part(e, r, part):
                return w_in[:, bass.ds(e, 1), r, part, :].rearrange("p e n -> p (e n)")

            def w_down_part(e, r, part):
                return w_down[0:down_rows(r), bass.ds(e, 1), r, part, :].rearrange("p e n -> p (e n)")

            W = SLOT_TILES
            RING = 3
            PARTS_HOT = 4
            TG = NT // PARTS_HOT

            def tables_at(at, end, *kinds):
                made = []
                for shape, dt in kinds:
                    v, at = carve(at, shape, dt)
                    made.append(v)
                assert at <= end
                return made, at
            xb_size, in_size = D * 4, 2 * H * 4
            by_token, per_tile = ([NT, E], F32), ([NT], F32)
            (rest, cand, pick0, pick1), _ = tables_at(down_stage_at, down_stage_at + 2 * D * 4, *[by_token] * 4)
            (tile_counts, running), _ = tables_at(xb_at, xb_at + xb_size, ([E, NT], F32), ([E, NT], F32))
            (both16, place, top0, top1, first_of, e2, z, g1, g2, var2, seed2, root2), _ = tables_at(
                in_stage_at, in_stage_at + in_size, ([NT, E], F16), by_token, *[per_tile] * 10)
            (slot_f, slot_hi, slot_lo, slot_hi_i, slot_lo_i, tiles_f, tiles_cum, base_slot, tiles_i, hot_tile2
             ), _ = tables_at(in_stage_at + in_size, in_stage_at + 2 * in_size, *[([2, NT], F32)] * 3,
                              *[([2, NT], I32)] * 2, *[([E], F32)] * 3, ([E], I32), ([TG, W], F16))
            (hot_tile0, hot_tile1), _ = tables_at(down_stage_at + NT * E * 4, down_stage_at + 2 * D * 4,
                                                  *[([TG, W], F16)] * 2)
            (column_e, expert_f), _ = tables_at(xb_at, xb_at + xb_size, ([W, E], F16), ([W], F32))
            hot_tile = (hot_tile0, hot_tile1, hot_tile2)
            hot_lane = [tables_at(xb_at + (n + 1) * xb_size, xb_at + (n + 2) * xb_size, ([TG, P], F16))[0][0]
                        for n in range(RING)]
            pick, top = (pick0, pick1), (top0, top1)
            gate_tables.extend((rest, g1, g2, e2, z, root2, seed2, var2))

            consts = sem("routing_consts")
            ones_set = sem("ones_set")
            step = sem("routing_step")
            exp_asked = sem("exp_asked")
            hot_used = sem("hot_used")
            picks_ready = sem("picks_ready")
            ranks_done = sem("ranks_done")
            lane_ready = sem("hot_lane_ready")
            in_tile_ready = sem("in_tile_ready")
            hot_ready = sem("hot_tile_ready")
            var2_ready = sem("var2_ready")
            seed2_ready = sem("seed2_ready")
            rank_bank, count_bank, token_bank = banks[5], banks[7], banks[0]
            CONSTS = 9
            steps = [0]

            def link(dve, ins):
                steps[0] += 1
                ins.then_inc(step, 1)
                dve.wait_ge(step, steps[0])

            def over_experts(v):
                return v.unsqueeze(2).to_broadcast([P, v.shape[1], E])

            def pick_experts(dve):
                v = nc.vector
                dve.wait_ge(rstd_kept, NT)
                link(dve, v.tensor_tensor(var2, rstd[:, :], rstd[:, :], ALU.mult))
                v.tensor_scalar(var2, var2, -EPS_LN, 1.0 + EPS_LN, ALU.mult, ALU.add).then_inc(var2_ready, 1)
                dve.wait_ge(consts, CONSTS)
                dve.wait_ge(logits_kept, NT)
                for c in range(2):
                    src = logits[:, :, :] if c == 0 else rest
                    link(dve, v.tensor_reduce(top[c], src, AX, ALU.max))
                    link(dve, v.tensor_tensor(cand, src, over_experts(top[c]), ALU.is_equal))
                    link(dve, v.tensor_tensor(cand, cand, rev[:], ALU.mult))
                    link(dve, v.tensor_reduce(first_of, cand, AX, ALU.max))
                    link(dve, v.tensor_tensor(pick[c], cand, over_experts(first_of), ALU.is_equal))
                    if c == 0:
                        link(dve, v.scalar_tensor_tensor(rest.rearrange("p t e -> p (t e)"),
                                                    pick[0].rearrange("p t e -> p (t e)"), -3e38,
                                                    logits[:, :, :].rearrange("p t e -> p (t e)"),
                                                    ALU.mult, ALU.add))
                v.tensor_tensor(both16, pick[0], pick[1], ALU.add).then_inc(picks_ready, 1)
                v.tensor_tensor(rest, logits[:, :, :], over_experts(top[0]), ALU.subtract).then_inc(exp_asked, 1)
                v.tensor_tensor(g2, top[1], top[0], ALU.subtract).then_inc(exp_asked, 1)

            def place_slots(dve):
                v = nc.vector
                dve.wait_ge(xn_stored[0], NT // 4 * 16)
                dve.wait_ge(ranks_done, 1)
                by_expert = count_bank[:, 0:NT * E].rearrange("p (t e) -> p e t", e=E)
                link(dve, v.tensor_copy(tile_counts, by_expert))
                link(dve, v.tensor_tensor_scan(running.rearrange("p e t -> p (e t)"), segment[:].rearrange("p e t -> p (e t)"),
                                          tile_counts.rearrange("p e t -> p (e t)"), 0.0, ALU.mult, ALU.add))
                link(dve, v.tensor_scalar(tiles_i, running[:, :, NT - 1], float(P - 1), None, ALU.add))
                link(dve, v.tensor_scalar(tiles_i, tiles_i, P.bit_length() - 1, None, ALU.logical_shift_right))
                link(dve, v.tensor_copy(tiles_f, tiles_i))
                link(dve, v.tensor_tensor_scan(tiles_cum, ones_e[:], tiles_f, 0.0, ALU.mult, ALU.add))
                link(dve, v.tensor_tensor(base_slot, tiles_cum, tiles_f, ALU.subtract))
                link(dve, v.tensor_scalar(base_slot, base_slot, float(P), None, ALU.mult))
                link(dve, v.tensor_tensor(running, running, tile_counts, ALU.subtract))
                link(dve, v.tensor_tensor(running, running, base_slot.unsqueeze(2).to_broadcast([P, E, NT]), ALU.add))
                link(dve, v.tensor_tensor(place, rank_bank[:, 0:NT * E].rearrange("p (t e) -> p t e", e=E),
                                     running.rearrange("p e t -> p t e"), ALU.add))
                for c in range(2):
                    link(dve, v.tensor_tensor(cand, pick[c], place, ALU.mult))
                    link(dve, v.tensor_reduce(slot_f[:, c, :], cand, AX, ALU.add))
                link(dve, v.tensor_copy(slot_of[:, :, :], slot_f))
                link(dve, v.tensor_copy(slot_hi_i, slot_f))
                link(dve, v.tensor_scalar(slot_lo_i, slot_hi_i, P - 1, None, ALU.bitwise_and))
                link(dve, v.tensor_scalar(slot_hi_i, slot_hi_i, P.bit_length() - 1, None, ALU.logical_shift_right))
                link(dve, v.tensor_copy(slot_lo, slot_lo_i))
                link(dve, v.tensor_copy(slot_hi, slot_hi_i))

            def hot_group(n):
                return n // PARTS_HOT, slice(n % PARTS_HOT * TG, (n % PARTS_HOT + 1) * TG)

            def one_hot(dve, n):
                v = nc.vector
                c, tiles = hot_group(n)
                if n < RING:
                    dve.wait_ge(xn_stored[n + 1], NT // 4 * 16)
                else:
                    dve.wait_ge(hot_used, n - RING + 1)
                v.tensor_tensor(hot_tile[n % RING], column[:].unsqueeze(1).to_broadcast([P, TG, W]),
                                slot_hi[:, c, tiles].unsqueeze(2).to_broadcast([P, TG, W]), ALU.is_equal
                                ).then_inc(in_tile_ready, 1)
                v.tensor_tensor(hot_lane[n % RING], lane[:].unsqueeze(1).to_broadcast([P, TG, P]),
                                slot_lo[:, c, tiles].unsqueeze(2).to_broadcast([P, TG, P]), ALU.is_equal
                                ).then_inc(lane_ready, 1)

            def name_experts(dve):
                v = nc.vector
                link(dve, v.tensor_tensor(column_e, tiles_cum.unsqueeze(1).to_broadcast([P, W, E]),
                                     column[:].unsqueeze(2).to_broadcast([P, W, E]), ALU.is_le))
                link(dve, v.tensor_reduce(expert_f, column_e, AX, ALU.add))
                link(dve, v.tensor_scalar(expert_of[:, :], expert_f, float(E - 1), None, ALU.min))

            with nc.Block() as block:
                @block.sync
                def _(sp):
                    def load_x(t, r, e):
                        turned_count, stored_count = (v if isinstance(v, int) else sp.to_reg(v) for v in (t - 3, e * 16))
                        wait(sp, x_turned, turned_count)
                        wait(sp, xn_stored[r], stored_count)
                        sp.dma_start(xb[r], X_FLAT[bass.ds(t * P, P), :]).then_inc(x_loaded[r], 16)

                    def store_xn(t, r, e):
                        sp.wait_ge(xn_ready, t + 1)
                        sp.dma_start(xn_rows[bass.ds(t * P, P), :], xb[r]).then_inc(xn_stored[r], 16)

                    def load_weights(t, r, e):
                        u = r % 2
                        wait(sp, in_lo, t - 1)
                        for n, w in enumerate((wg, wu)):
                            sp.dma_start(in_stage[u][:, n * H:(n + 1) * H],
                                         w[bass.ds(e, 1), r * P:(r + 1) * P, :].rearrange("e p n -> (e p) n")
                                         ).then_inc(in_loaded[u], 16)
                        if r < HC:
                            wait(sp, down_lo, 3 * e + r - 1 if r else 3 * e)
                            rows = down_rows(r)
                            sp.dma_start(down_stage[u][0:rows, :],
                                         wd[bass.ds(e, 1), r * P:r * P + rows, :].rearrange("e p n -> (e p) n")
                                         ).then_inc(down_loaded[u], 16)

                    def store_y(t):
                        sp.wait_ge(y_ready, t + 1)
                        sp.dma_start(shared_rows[bass.ds(t * P, P), :], y_out).then_inc(y_stored, 16)

                    load_weights(0, 0, 0)
                    store_xn(0, 0, 0)

                    def tile(t, r, e, last):
                        if not late(t, 3):
                            load_x(*ahead(t, r, e, 3))
                        if not late(t, 1):
                            store_xn(*ahead(t, r, e, 1))
                            load_weights(*ahead(t, r, e, 1))
                        if not early(t, 1):
                            store_y(t - 1)

                    over_tiles(sp, tile)
                    store_y(NT - 1)

                @block.gpsimd
                def _(pool):
                    pool.memset(sbuf[0][:, H:HP], 0.0).then_inc(pads, 1)
                    pool.memset(sbuf[1][:, H:HP], 0.0).then_inc(pads, 1)
                    pool.wait_ge(pads, 2)
                    seed(pool, 2, 0)
                    if HR < P:
                        pool.wait_ge(seed_ready, 3)
                        pool.wait_ge(shared_lo, len(splits))
                        pool.memset(w_down[HR:P, :, HC - 1], 0.0).then_inc(down_padded, 1)
                        pool.wait_ge(down_padded, 1)
                    seed(pool, 3, 1)
                    n = [0]

                    def put(ins):
                        n[0] += 1
                        ins.then_inc(consts, 1)
                    imprecise = dict(allow_small_or_imprecise_dtypes=True)
                    put(pool.iota(rev[:], [[0, NT], [-1, E]], base=E, channel_multiplier=0, **imprecise))
                    put(pool.iota(column[:], [[1, W]], base=0, channel_multiplier=0, **imprecise))
                    put(pool.iota(lane[:], [[1, P]], base=0, channel_multiplier=0, **imprecise))
                    put(pool.iota(token_mid[:], [[P, NT]], base=-(N // 2), channel_multiplier=1, **imprecise))
                    put(pool.memset(half2[:], -0.5))
                    put(pool.memset(ones_e[:], 1.0))
                    pool.memset(ones16[:], 1.0).then_inc(ones_set, 1)
                    pool.wait_ge(ones_set, 1)
                    put(pool.affine_select(out=before[:], in_=ones16[:], compare_op=ALU.is_gt, fill=0.0, base=0,
                                           pattern=[[1, P]], channel_multiplier=-1))
                    put(pool.memset(segment[:], 1.0))
                    pool.wait_ge(consts, n[0])
                    put(pool.memset(segment[:, :, 0:1], 0.0))
                    with pool.Fori(2, NT // 2) as i:
                        seed(pool, 2 * i, 0)
                        seed(pool, 2 * i + 1, 1)
                    pool.wait_ge(var2_ready, 1)
                    pool.tensor_tensor(seed2, var2, half2[:], ALU.pow).then_inc(seed2_ready, 1)
                    for n in range(2 * PARTS_HOT):
                        hot = hot_tile[n % RING]
                        pool.wait_ge(in_tile_ready, n + 1)
                        pool.tensor_tensor(hot, hot, token_mid[:, hot_group(n)[1]].unsqueeze(2).to_broadcast([P, TG, W]),
                                           ALU.mult).then_inc(hot_ready, 1)

                @block.tensor
                def _(pe):
                    def tile_turn(t, r):
                        pe.wait_ge(xn_ready, t + 1)
                        wait(pe, xt_lo, t)
                        turn_rows(pe, xb[r], xt_bank, KC).then_inc(x_turned, 1)

                    def router(t, u):
                        pe.wait_ge(xt_lo, t + 1)
                        wait(pe, logits_kept, t)
                        for c in range(KC):
                            for i, (a, b) in enumerate(PARTS):
                                last = pe.matmul(logit_bank[:, 0:E], xt[u][:, a, c, :], rw_split[:, c, b, :],
                                                 start=(c == 0 and i == 0), stop=(c == KC - 1 and i == 2))
                        last.then_inc(logits_done, 1)

                    def unit_in(n, u, b):
                        wait(pe, h_ready, n - 1)
                        gate_up(pe, xt[u], lambda c, s, col: shared_in[:, b, c, s, col:col + H],
                                g_banks[b], u_banks[b]).then_inc(gu_done, 1)

                    def unit_turn(n, b):
                        pe.wait_ge(h_ready, n + 1)
                        wait(pe, ht_lo, n)
                        turn_rows(pe, sbuf[b], ht_bank, HC).then_inc(h_turned, 1)

                    def unit_down(n, t, b):
                        pe.wait_ge(ht_lo, n + 1)
                        if b == 0:
                            wait(pe, y_ready, t)
                        down(pe, ht[b], lambda c, s: shared_down[:, b, c, s, :], y_bank,
                             b == 0, b == 1).then_inc(y_done, 1)

                    pe.wait_ge(pads, 2)
                    tile_turn(0, 0)
                    router(0, 0)

                    def tile(t, r, e, last):
                        if not last:
                            tile_turn(t + 1, (r + 1) % 4)
                        for b in range(2):
                            n = 2 * t + b
                            if early(n, 2):
                                pe.wait_ge(shared_lo, FIRST_SPLITS if b == 0 else 2 * NS)
                            unit_in(n, r % 2, b)
                            if not early(n, 1):
                                unit_turn(n - 1, 1 - b)
                            if b == 0 and not last:
                                router(t + 1, (r + 1) % 2)
                            if b == 0 and last:
                                pe.wait_ge(picks_ready, 1)
                                picked = both16.rearrange("p t e -> p (t e)")
                                pe.matmul(rank_bank[:, 0:NT * E], before[:, :], picked, start=True, stop=True)
                                pe.matmul(count_bank[:, 0:NT * E], ones16[:, :], picked, start=True, stop=True
                                          ).then_inc(ranks_done, 1)
                            if not early(n, 2):
                                if isinstance(n, int) and n == 2:
                                    pe.wait_ge(shared_lo, len(splits))
                                unit_down(n - 2, t - 1, b)

                    over_tiles(pe, tile)
                    unit_turn(2 * NT - 1, 1)
                    unit_down(2 * NT - 2, NT - 1, 0)
                    unit_down(2 * NT - 1, NT - 1, 1)
                    for n in range(2 * PARTS_HOT):
                        pe.wait_ge(lane_ready, n + 1)
                        pe.wait_ge(hot_ready, n + 1)
                        for t in range(TG):
                            last = pe.matmul(token_bank[:, 0:W], hot_lane[n % RING][:, t, :], hot_tile[n % RING][:, t, :],
                                             start=(n == 0 and t == 0), stop=(n == 2 * PARTS_HOT - 1 and t == TG - 1),
                                             skip_group_check=True)
                        last.then_inc(hot_used, 1)

                @block.scalar
                def _(act):
                    def x_high(t, u):
                        act.wait_ge(x_turned, t + 1)
                        wait(act, gu_done, 2 * t - 2)
                        nc.scalar.copy(xt[u][:, 0], chunked(xt_bank, KC)).then_inc(xt_hi, 1)

                    def silu(n, b):
                        act.wait_ge(gu_done, n + 1)
                        wait(act, h_turned, n - 1)
                        nc.scalar.activation(sbuf[b][:, 0:H], g_banks[b][:, 0:H], ACT.Silu,
                                             scale=UNIT_SCALE).then_inc(silu_done, 1)

                    def h_high(n, b):
                        act.wait_ge(h_turned, n + 1)
                        wait(act, y_done, n - 1)
                        nc.scalar.copy(ht[b][:, 0], chunked(ht_bank, HC)).then_inc(ht_hi, 1)

                    def in_high(t, r, e):
                        act.wait_ge(in_loaded[r % 2], (2 * e + r // 2 + 1) * 32)
                        nc.scalar.activation(w_in_part(e, r, 0), in_stage[r % 2], ACT.Copy, scale=S_W).then_inc(in_hi, 1)

                    def down_high(r, e):
                        act.wait_ge(down_loaded[r % 2], (2 * e + r // 2 + 1 if r % 2 == 0 else e + 1) * 16)
                        nc.scalar.activation(w_down_part(e, r, 0), down_stage[r % 2][0:down_rows(r), :], ACT.Copy,
                                             scale=S_W).then_inc(down_hi, 1)

                    def y_copy(t):
                        act.wait_ge(y_done, 2 * t + 2)
                        wait(act, y_stored, t * 16)
                        nc.scalar.activation(y_out, y_bank[:, :], ACT.Copy, scale=Y_SCALE).then_inc(y_ready, 1)

                    x_high(0, 0)
                    for n in range(FIRST_SPLITS, 2 * NS):
                        split_hi(act, n)

                    def tile(t, r, e, last):
                        if not last:
                            x_high(t + 1, (r + 1) % 2)
                        silu(2 * t, 0)
                        if not early(t, 1):
                            h_high(2 * t - 1, 1)
                        ins, downs = split_beside(t, r)
                        for n in ins[:1]:
                            in_high(t - r + n, n, e)
                        if late(t, 2):
                            for n in downs:
                                down_high(n, e)
                        silu(2 * t + 1, 1)
                        h_high(2 * t, 0)
                        if early(t, 1):
                            for n in range(2 * NS, len(splits)):
                                split_hi(act, n)
                        for n in ins[1:]:
                            in_high(t - r + n, n, e)
                        if not late(t, 2):
                            for n in downs:
                                down_high(n, e)
                        if not early(t, 1):
                            y_copy(t - 1)

                    act.wait_ge(fold_stored, 32)
                    over_tiles(act, tile)
                    h_high(2 * NT - 1, 1)
                    y_copy(NT - 1)
                    act.wait_ge(exp_asked, 2)
                    nc.scalar.activation(rest, rest, ACT.Exp, scale=UNIT_SCALE).then_inc(exp_done, 1)
                    nc.scalar.activation(e2, g2, ACT.Exp, scale=UNIT_SCALE).then_inc(exp_done, 1)

                @block.vector
                def _(dve):
                    v = nc.vector

                    def x_low(t, u):
                        dve.wait_ge(xt_hi, t + 1)
                        v.tensor_tensor(xt[u][:, 1], chunked(xt_bank, KC), xt[u][:, 0], ALU.subtract
                                        ).then_inc(xt_lo, 1)

                    def hidden(n, b):
                        dve.wait_ge(silu_done, n + 1)
                        v.scalar_tensor_tensor(sbuf[b][:, 0:H], u_banks[b][:, 0:H], H_SCALE, sbuf[b][:, 0:H],
                                               ALU.mult, ALU.mult).then_inc(h_ready, 1)

                    def h_low(n, b):
                        dve.wait_ge(ht_hi, n + 1)
                        v.tensor_tensor(ht[b][:, 1], chunked(ht_bank, HC), ht[b][:, 0], ALU.subtract
                                        ).then_inc(ht_lo, 1)

                    def in_low(t, r, e):
                        dve.wait_ge(in_hi, t + 1)
                        v.scalar_tensor_tensor(w_in_part(e, r, 1), in_stage[r % 2], S_W, w_in_part(e, r, 0),
                                               ALU.mult, ALU.subtract).then_inc(in_lo, 1)

                    def down_low(r, e):
                        dve.wait_ge(down_hi, 3 * e + r + 1)
                        v.scalar_tensor_tensor(w_down_part(e, r, 1), down_stage[r % 2][0:down_rows(r), :], S_W,
                                               w_down_part(e, r, 0), ALU.mult, ALU.subtract).then_inc(down_lo, 1)

                    def keep_logits(t):
                        dve.wait_ge(logits_done, t + 1)
                        v.tensor_copy(logits[:, bass.ds(t, 1), :].rearrange("p t e -> p (t e)"),
                                      logit_bank[:, 0:E]).then_inc(logits_kept, 1)

                    x_low(0, 0)
                    for n in range(FIRST_SPLITS, 2 * NS):
                        split_lo(dve, n)

                    keep_logits(0)

                    def tile(t, r, e, last):
                        if not last:
                            x_low(t + 1, (r + 1) % 2)
                        if not late(t, 2):
                            stats(dve, *ahead(t, r, e, 2))
                        hidden(2 * t, 0)
                        if not early(t, 1):
                            h_low(2 * t - 1, 1)
                        if not last:
                            keep_logits(t + 1)
                        ins, downs = split_beside(t, r)
                        for n in ins[:1]:
                            in_low(t - r + n, n, e)
                        if not late(t, 2):
                            normalise(dve, t + 2, (r + 2) % 4)
                        elif not last:
                            for n in downs:
                                down_low(n, e)
                            pick_experts(dve)
                        if last:
                            place_slots(dve)
                        hidden(2 * t + 1, 1)
                        h_low(2 * t, 0)
                        if early(t, 1):
                            for n in range(2 * NS, len(splits)):
                                split_lo(dve, n)
                        for n in ins[1:]:
                            in_low(t - r + n, n, e)
                        if not late(t, 2):
                            for n in downs:
                                down_low(n, e)

                    over_tiles(dve, tile)
                    one_hot(dve, 0)
                    h_low(2 * NT - 1, 1)
                    for n in range(1, 2 * PARTS_HOT):
                        one_hot(dve, n)
                    name_experts(dve)
                    dve.wait_ge(hot_used, 2 * PARTS_HOT)
                    nc.vector.tensor_scalar(token_of[:, :], token_bank[:, 0:W], float(N // 2), None, ALU.add
                                            ).then_inc(step, 1)

        HALF = 512
        TH, NH = HALF // P, S // HALF
        XG = NH * KC
        QT = S // P
        early_at = routed_end + 20 * 1024
        x2, x2f = [], []
        x2t00, end4 = carve(early_at, [2, KC, HALF], F16)
        for _ in range(NH):
            v_, end4 = carve(end4, [TH, D], F32)
            x2.append(v_)
        for _ in range(2):
            v_, end4 = carve(end4, [HALF], F32)
            x2f.append(v_)
        attn_fold, end4 = carve(end4, [2, KC, 2, D], F16)
        x2t_first, at4 = carve(0, [2 * NH - 1, 2, KC, HALF], F16)
        x2t = [[x2t00, x2t_first[:, 0]], [x2t_first[:, 1], x2t_first[:, 2]]]
        assert NH == 2
        fold_loaded = sem("fold_loaded")
        x2_loaded = [sem("x2_loaded0"), sem("x2_loaded1")]
        slot_rows_stored = [sem("slot_y_stored0"), sem("slot_y_stored1")]
        x2_ready = sem("x2_ready")
        x2_turned = sem("x2_turned")
        x2_hi = sem("x2_hi")
        x2_full = sem("x2_full")
        x2_lo = sem("x2_lo")

        def normalise_x2(dve, b, h):
            dve.wait_ge(x2_loaded[h], (b + 1) * 16)
            for j in range(TH):
                t = b * QT + h * TH + j
                nc.vector.tensor_scalar(x2[h][:, j, :], x2[h][:, j, :], mean[:, t:t + 1], rstd2[:, t:t + 1],
                                        ALU.subtract, ALU.mult).then_inc(x2_ready, 1)

        def turn_x2_into(pe, b, k, bank):
            h, ch = k // KC, k % KC
            pe.wait_ge(x2_ready, b * QT + (h + 1) * TH)
            for j in range(TH):
                last = pe.transpose(bank[:, j * P:(j + 1) * P], x2[h][:, j, ch * P:(ch + 1) * P], ident[:, :])
            last.then_inc(x2_turned, 1)

        def x2_high_from(act, b, k, bank):
            h, ch = k // KC, k % KC
            act.wait_ge(x2_turned, b * XG + k + 1)
            nc.scalar.activation(x2t[b % 2][h][:, 0, ch, :], bank[:, :], ACT.Identity, scale=affine_s[:, 0, ch:ch + 1],
                                 bias=affine_s[:, 1, ch:ch + 1]).then_inc(x2_hi, 1)

        def x2_low_from(dve, b, k, bank):
            h, ch = k // KC, k % KC
            dve.wait_ge(x2_hi, b * XG + k + 1)
            nc.vector.tensor_scalar(x2f[k % 2], bank[:, :], affine_s[:, 0, ch:ch + 1], affine_s[:, 1, ch:ch + 1],
                                    ALU.mult, ALU.add).then_inc(x2_full, 1)
            dve.wait_ge(x2_full, b * XG + k + 1)
            nc.vector.tensor_tensor(x2t[b % 2][h][:, 1, ch, :], x2f[k % 2], x2t[b % 2][h][:, 0, ch, :],
                                    ALU.subtract).then_inc(x2_lo, 1)

        gate_steps = [0]

        def gate_link(dve, ins):
            gate_steps[0] += 1
            ins.then_inc(gate_step, 1)
            dve.wait_ge(gate_step, gate_steps[0])

        def make_gates(dve):
            v = nc.vector
            rest, g1, g2, e2, z, root2, seed2, var2 = gate_tables
            dve.wait_ge(exp_done, 2)
            gate_link(dve, v.tensor_reduce(z, rest, AX, ALU.add))
            gate_link(dve, v.reciprocal(g1, z))
            gate_link(dve, v.tensor_tensor(g2, g1, e2, ALU.mult))
            gate_link(dve, v.scalar_tensor_tensor(z, g1, EPS_GATE, g2, ALU.add, ALU.add))
            gate_link(dve, v.reciprocal(z, z))
            gate_link(dve, v.tensor_tensor(gate[:, 0, :], g1, z, ALU.mult))
            gate_link(dve, v.tensor_tensor(gate[:, 1, :], g2, z, ALU.mult))
            gate_link(dve, v.tensor_tensor(root2, seed2, seed2, ALU.mult))
            gate_link(dve, v.tensor_tensor(root2, root2, var2, ALU.mult))
            gate_link(dve, v.tensor_scalar(root2, root2, -0.5, 1.5, ALU.mult, ALU.add))
            gate_link(dve, v.tensor_tensor(root2, root2, seed2, ALU.mult))
            gate_link(dve, v.tensor_tensor(rstd2[:, :], root2, rstd[:, :], ALU.mult))
            gate_link(dve, v.tensor_scalar(rstd[:, :], rstd[:, :], S_Q, None, ALU.mult))
            v.scalar_tensor_tensor(shift[:, :], mean[:, :], -1.0, rstd[:, :], ALU.mult, ALU.mult).then_inc(gates_made, 1)

        def stage3():
            at = routed_end
            bufs = {}
            for name, shape, dt in (("xg", [D], F32), ("xt", [2, KC, P], F16), ("s", [HP], F32),
                                    ("ht", [2, HC, P], F16), ("y", [D], F32), ("index", [1], U32)):
                for u in range(2):
                    bufs[name, u], at = carve(at, shape, dt)
            assert at <= early_at
            g_banks, u_banks = (banks[0], banks[2]), (banks[1], banks[3])
            y_bank = banks[4], banks[7]
            xt_bank, ht_bank = banks[5], banks[6]
            T = SLOT_TILES
            assert T % 2 == 1

            index_ready = sem("index_ready")
            gathered = [sem("gathered0"), sem("gathered1")]
            x_turned = sem("slot_x_turned")
            xt_hi = sem("slot_xt_hi")
            xt_lo = sem("slot_xt_lo")
            gu_done = sem("slot_gu_done")
            silu_done = sem("slot_silu_done")
            h_ready = sem("slot_h_ready")
            h_turned = sem("slot_h_turned")
            ht_hi = sem("slot_ht_hi")
            ht_lo = sem("slot_ht_lo")
            y_done = sem("slot_y_done")
            y_ready = sem("slot_y_ready")
            y_stored = slot_rows_stored
            pads = sem("slot_pads")

            def early(j, n):
                return isinstance(j, int) and j < n

            def over_slots(eng, tile, peeled, done=0):
                for j in range(done, peeled):
                    tile(j, j % 2, j // 2, False)
                with eng.Fori(peeled // 2, (T - 1) // 2) as i:
                    tile(2 * i, 0, i, False)
                    tile(2 * i + 1, 1, i, False)
                tile(T - 1, 0, (T - 1) // 2, True)

            with nc.Block() as block:
                @block.gpsimd
                def _(pool):
                    pool.memset(bufs["s", 0][:, H:HP], 0.0).then_inc(pads, 1)
                    pool.memset(bufs["s", 1][:, H:HP], 0.0).then_inc(pads, 1)

                    def gather(j, u, k, last):
                        wait(pool, x_turned, j - 1)
                        wait(pool, gathered[u], k * 16)
                        pool.tensor_copy(bufs["index", u], token_of[:, bass.ds(j, 1)]).then_inc(index_ready, 1)
                        if isinstance(j, int) and j == 0:
                            for r in range(4):
                                pool.wait_ge(xn_stored[r], NT // 4 * 16)
                        wait_apart(pool, index_ready, j + 1, pads, 2)
                        pool.indirect_dma_start(bufs["xg", u], None, xn_rows, bass.IndirectOffsetOnAxis(
                            ap=bufs["index", u], axis=0)).then_inc(gathered[u], 16)
                    over_slots(pool, gather, 2)

                @block.sync
                def _(sp):
                    def store_y(j, u, k, last):
                        sp.wait_ge(y_ready, j + 1)
                        sp.dma_start(slot_rows[bass.ds(j * P, P), :], bufs["y", u]).then_inc(y_stored[u], 16)
                    for j in range(4):
                        store_y(j, j % 2, j // 2, False)
                    sp.wait_ge(shared_stored, NT * 16)
                    sp.wait_ge(gates_made, 1)
                    for h in range(2):
                        sp.dma_start(x2[h], X_FLAT[h * 512:(h + 1) * 512, :].rearrange(
                            "(t p) d -> p t d", p=P)).then_inc(x2_loaded[h], 16)
                    sp.dma_start(attn_fold.rearrange("p f c s d -> p (f c s d)"), folded).then_inc(fold_loaded, 16)
                    over_slots(sp, store_y, 4, done=4)

                @block.tensor
                def _(pe):
                    def slot_turn(j, u, k):
                        pe.wait_ge(gathered[u], (k + 1) * 16)
                        wait(pe, xt_lo, j)
                        turn_rows(pe, bufs["xg", u], xt_bank, KC).then_inc(x_turned, 1)

                    def weight(w, e, c, s, a, b):
                        return w[:, bass.ds(e, 1), c, s, a:b].rearrange("p e n -> p (e n)")

                    def unit_in(j, u):
                        e = pe.value_load(expert_of[0:1, bass.ds(j, 1)], min_val=0, max_val=E - 1)
                        pe.wait_ge(xt_lo, j + 1)
                        wait(pe, h_ready, j - 1)
                        gate_up(pe, bufs["xt", u], lambda c, s, col: weight(w_in, e, c, s, col, col + H),
                                g_banks[u], u_banks[u]).then_inc(gu_done, 1)

                    def unit_turn(j, u):
                        pe.wait_ge(h_ready, j + 1)
                        wait(pe, ht_lo, j)
                        turn_rows(pe, bufs["s", u], ht_bank, HC).then_inc(h_turned, 1)

                    def unit_down(j, u):
                        e = pe.value_load(expert_of[0:1, bass.ds(j, 1)], min_val=0, max_val=E - 1)
                        pe.wait_ge(ht_lo, j + 1)
                        wait(pe, y_ready, j - 1)
                        down(pe, bufs["ht", u], lambda c, s: weight(w_down, e, c, s, 0, D),
                             y_bank[u], True, True).then_inc(y_done, 1)

                    def early_x2(k):
                        wait(pe, x2_lo, k)
                        if k == 0:
                            pe.wait_ge(xt_lo, T)
                        turn_x2_into(pe, 0, k, xt_bank)

                    def slot_tile(j, u, k, last):
                        if not last:
                            slot_turn(j + 1, 1 - u, k + u)
                        unit_in(j, u)
                        if last:
                            early_x2(0)
                        if not early(j, 1):
                            unit_turn(j - 1, 1 - u)
                        if not early(j, 2):
                            unit_down(j - 2, u)

                    pe.wait_ge(pads, 2)
                    slot_turn(0, 0, 0)
                    over_slots(pe, slot_tile, 4)
                    early_x2(1)
                    unit_turn(T - 1, 0)
                    unit_down(T - 2, 1)
                    early_x2(2)
                    unit_down(T - 1, 0)
                    early_x2(3)

                @block.scalar
                def _(act):
                    def x_high(j, u):
                        act.wait_ge(x_turned, j + 1)
                        wait(act, gu_done, j - 1)
                        nc.scalar.copy(bufs["xt", u][:, 0], chunked(xt_bank, KC)).then_inc(xt_hi, 1)

                    def h_high(j, u):
                        act.wait_ge(h_turned, j + 1)
                        wait(act, y_done, j - 1)
                        nc.scalar.copy(bufs["ht", u][:, 0], chunked(ht_bank, HC)).then_inc(ht_hi, 1)

                    def y_copy(j, u, k):
                        act.wait_ge(y_done, j + 1)
                        wait(act, y_stored[u], k * 16)
                        nc.scalar.activation(bufs["y", u], y_bank[u][:, :], ACT.Copy, scale=Y_SCALE).then_inc(y_ready, 1)

                    def slot_tile(j, u, k, last):
                        if not last:
                            x_high(j + 1, 1 - u)
                        if not early(j, 3):
                            y_copy(j - 3, 1 - u, k - 2 + u)
                        act.wait_ge(gu_done, j + 1)
                        wait(act, h_turned, j - 1)
                        nc.scalar.activation(bufs["s", u][:, 0:H], g_banks[u][:, 0:H], ACT.Silu,
                                             scale=UNIT_SCALE).then_inc(silu_done, 1)
                        if last:
                            x2_high_from(act, 0, 0, xt_bank)
                        if not early(j, 1):
                            h_high(j - 1, 1 - u)

                    x_high(0, 0)
                    over_slots(act, slot_tile, 4)
                    x2_high_from(act, 0, 1, xt_bank)
                    h_high(T - 1, 0)
                    y_copy(T - 3, (T - 3) % 2, (T - 3) // 2)
                    x2_high_from(act, 0, 2, xt_bank)
                    y_copy(T - 2, (T - 2) % 2, (T - 2) // 2)
                    x2_high_from(act, 0, 3, xt_bank)
                    y_copy(T - 1, (T - 1) % 2, (T - 1) // 2)

                @block.vector
                def _(dve):
                    v = nc.vector

                    def x_low(j, u):
                        dve.wait_ge(xt_hi, j + 1)
                        v.tensor_tensor(bufs["xt", u][:, 1], chunked(xt_bank, KC), bufs["xt", u][:, 0],
                                        ALU.subtract).then_inc(xt_lo, 1)

                    def h_low(j, u):
                        dve.wait_ge(ht_hi, j + 1)
                        v.tensor_tensor(bufs["ht", u][:, 1], chunked(ht_bank, HC), bufs["ht", u][:, 0],
                                        ALU.subtract).then_inc(ht_lo, 1)

                    def slot_tile(j, u, k, last):
                        if last:
                            for h in range(NH):
                                normalise_x2(dve, 0, h)
                        else:
                            x_low(j + 1, 1 - u)
                        dve.wait_ge(silu_done, j + 1)
                        v.scalar_tensor_tensor(bufs["s", u][:, 0:H], u_banks[u][:, 0:H], H_SCALE, bufs["s", u][:, 0:H],
                                               ALU.mult, ALU.mult).then_inc(h_ready, 1)
                        if last:
                            x2_low_from(dve, 0, 0, xt_bank)
                        if not early(j, 1):
                            h_low(j - 1, 1 - u)

                    x_low(0, 0)
                    for j in range(2):
                        slot_tile(j, j % 2, j // 2, False)
                    make_gates(dve)
                    over_slots(dve, slot_tile, 2, done=2)
                    x2_low_from(dve, 0, 1, xt_bank)
                    h_low(T - 1, 0)
                    for k in (2, 3):
                        x2_low_from(dve, 0, k, xt_bank)

        def stage4():
            ORDER = list(range(1, QT, 2)) + list(range(QT - 2, -1, -2))
            QG = NH * KC
            PG = QG + QT
            BEGIN_GROUP, END_GROUP = {3: 0, 6: 1, 9: 2, 11: 3, 13: 4}, {5: 0, 8: 1, 11: 2, 13: 3}
            BEGIN_STEP, END_STEP = {1: 5, 3: 6, 5: 7}, {0: 4, 3: 5, 5: 6, 7: 7}
            assert QT == 8 and NH == 2 and KC == 4 and TH == KC

            x2_turns = [dict(zip([1, 3, 5, 7, 9, 10, 12, 14], [(b + 1, k) for k in range(XG)])) for b in range(B - 1)]
            x2_turns[0] = dict(zip([0, 1, 2, 3, 4, 5, 6, 7, 9, 10, 12, 14],
                                   [(0, k) for k in range(KC, XG)] + [(1, k) for k in range(XG)]))
            x2_turns.append({})
            fold = attn_fold
            qt, at = carve(at4, [2, KC, S], F16)
            vs, at = carve(at, [QT, 2, D], F16)
            X_AHEAD = 4
            c = {}
            for name, shape, dt in (("p", [S], F32), ("pt", [2, QT, P], F16), ("f", [D], F32),
                                    ("y0", [D], F32), ("y1", [D], F32), ("s", [D], F32), ("th", [D], F32),
                                    ("res", [D], F32), ("top", [1], F32), ("bias", [1], F32), ("inv", [1], F32),
                                    ("i0", [1], U32), ("i1", [1], U32)):
                for u in range(2):
                    c[name, u], at = carve(at, shape, dt)
            for u in range(X_AHEAD):
                c["x", u], at = carve(at, [D], F32)
            g, at = carve(at, [QT, D], F32)
            causal, at = carve(at, [P], F32)
            sums, at = carve(at, [4], F32)
            assert at <= early_at

            pv_banks = banks[4], banks[5]
            turn_banks = banks[6], banks[7]
            Q_SCALE = S_Q / (S_FOLD * S_X2)
            SOFT = 1.0 / (S_Q * S_X2 * float(D) ** 0.5)

            causal_zeroed = sem("causal_zeroed")
            causal_ready = sem("causal_ready")
            proj_done = sem("proj_done")
            proj_hi = sem("proj_hi")
            proj_lo = sem("proj_lo")
            scores_done = sem("scores_done")
            masked = sem("masked")
            top_ready = sem("top_ready")
            bias_ready = sem("bias_ready")
            exp_done = sem("probs_done")
            p_turned = sem("p_turned")
            pt_hi = sem("pt_hi")
            pt_lo = sem("pt_lo")
            pv_done = sem("pv_done")
            x_loaded = [sem(f"res_x_loaded{u}") for u in range(X_AHEAD)]
            f_loaded = [sem("shared_loaded0"), sem("shared_loaded1")]
            y_index = sem("y_index")
            y_loaded = [[sem(f"y{n}_loaded{u}") for u in range(2)] for n in range(2)]
            y_gated = sem("y_gated")
            y_summed = sem("y_summed")
            f_ready = sem("f_ready")
            tanh_done = sem("tanh_done")
            g_made = sem("g_made")
            xn_made = sem("xn_made")
            inv_ready = sem("inv_ready")
            s_made = sem("s_made")
            o_made = sem("o_made")
            res_ready = sem("res_ready")
            res_stored = [sem("res_stored0"), sem("res_stored1")]

            def tile_of(t):
                return ORDER[t % QT]

            def place(t):
                return t // QT * QT + tile_of(t)

            def turn_groups(t):
                return sum(-(-(tile_of(s) + 1) // 4) for s in range(t))

            def proj_group(g_):
                return g_ % (KC + TH) // KC, g_ // (KC + TH), g_ % KC

            def proj_target(g_, part):
                is_v, h, n = proj_group(g_)
                return vs[:, h * TH + n, part, :] if is_v else qt[:, part, n, h * HALF:(h + 1) * HALF]

            def proj_bank(g_):
                return pv_banks[g_ - (PG - 2)] if g_ >= PG - 2 else banks[g_ % 4]

            with nc.Block() as block:
                @block.sync
                def _(sp):
                    def load_x2(b, h):
                        wait(sp, x2_turned, (b - 1) * XG + (h + 1) * KC)
                        r = b * S + h * HALF
                        sp.dma_start(x2[h], X_FLAT[r:r + HALF, :].rearrange("(t p) d -> p t d", p=P)
                                     ).then_inc(x2_loaded[h], 16)

                    def load_shared(t):
                        wait(sp, g_made, t - 1)
                        r = place(t) * P
                        sp.dma_start(c["f", t % 2], shared_rows[r:r + P, :]).then_inc(f_loaded[t % 2], 16)

                    def load_x(t):
                        wait(sp, res_ready, t - X_AHEAD + 1)
                        r, u = place(t) * P, t % X_AHEAD
                        sp.dma_start(c["x", u], X_FLAT[r:r + P, :]).then_inc(x_loaded[u], 16)

                    def store_tile(t):
                        sp.wait_ge(res_ready, t + 1)
                        r = place(t) * P
                        sp.dma_start(OUT_FLAT[r:r + P, :], c["res", t % 2]).then_inc(res_stored[t % 2], 16)

                    for t in range(2):
                        load_shared(t)
                        load_x(t)
                        load_x(t + 2)
                    load_x2(1, 0)
                    load_x2(1, 1)
                    for t in range(2, 5):
                        load_shared(t)
                    for b in range(B):
                        for n in range(QT):
                            t = b * QT + n
                            if n < 3:
                                load_shared(t + 5)
                            if n >= QT - 2 and b + 1 < B:
                                load_shared(t + 2)
                            if n == 0 and b + 2 < B:
                                load_x2(b + 2, 0)
                                load_x2(b + 2, 1)
                            store_tile(t)
                            if t + X_AHEAD < NT:
                                load_x(t + X_AHEAD)
                        if b + 1 < B:
                            for t in range((b + 1) * QT + 2, (b + 1) * QT + 5):
                                load_shared(t)
                    for u in range(2):
                        sp.wait_ge(res_stored[u], NT // 2 * 16)

                @block.gpsimd
                def _(pool):
                    pool.memset(causal, 0.0).then_inc(causal_zeroed, 1)
                    pool.wait_ge(causal_zeroed, 1)
                    pool.affine_select(out=causal, in_=causal, compare_op=ALU.is_ge, fill=-3e38, base=0,
                                       pattern=[[-1, P]], channel_multiplier=1).then_inc(causal_ready, 1)

                    def gather(t):
                        u = t % 2
                        for n in range(2):
                            wait(pool, y_loaded[n][u], t // 2 * 16)
                            pool.tensor_copy(c[f"i{n}", u], slot_of[:, n, place(t):place(t) + 1]).then_inc(y_index, 1)
                            pool.wait_ge(y_index, 2 * t + n + 1)
                            wait(pool, f_ready, t - 1)
                            pool.indirect_dma_start(c[f"y{n}", u], None, slot_rows, bass.IndirectOffsetOnAxis(
                                ap=c[f"i{n}", u], axis=0)).then_inc(y_loaded[n][u], 16)

                    def mix(t):
                        u = t % 2
                        pool.wait_ge(y_gated, 2 * t + 2)
                        pool.tensor_tensor(c["y0", u], c["y0", u], c["y1", u], ALU.add).then_inc(y_summed, 1)
                        pool.wait_ge(f_loaded[u], (t // 2 + 1) * 16)
                        pool.wait_ge(y_summed, t + 1)
                        pool.tensor_tensor(c["f", u], c["f", u], c["y0", u], ALU.add).then_inc(f_ready, 1)
                        if t + 2 < NT:
                            gather(t + 2)

                    def finish(t):
                        u = t % 2
                        pool.wait_ge(o_made, t + 1)
                        wait(pool, res_stored[u], t // 2 * 16)
                        pool.tensor_tensor(c["res", u], c["s", u], c["x", t % X_AHEAD], ALU.add).then_inc(res_ready, 1)

                    pool.wait_ge(slot_rows_stored[0], (SLOT_TILES + 1) // 2 * 16)
                    pool.wait_ge(slot_rows_stored[1], SLOT_TILES // 2 * 16)
                    gather(0)
                    gather(1)
                    for b in range(B):
                        for g_ in range(PG):
                            if g_ in BEGIN_GROUP:
                                mix(b * QT + BEGIN_GROUP[g_])
                            if g_ == 3 and b > 0:
                                finish(b * QT - 1)
                        for n in range(QT):
                            if n in BEGIN_STEP:
                                mix(b * QT + BEGIN_STEP[n])
                            if n > 1:
                                finish(b * QT + n - 2)
                        finish(b * QT + QT - 2)
                    finish(NT - 1)

                @block.tensor
                def _(pe):
                    def turn_x2(b, k):
                        wait(pe, x2_lo, b * XG + k - 1)
                        if k < 2 and b >= 1:
                            wait(pe, pt_lo, turn_groups((b - 1) * QT))
                        turn_x2_into(pe, b, k, turn_banks[k % 2])

                    def project(b, g_):
                        if g_ == 0:
                            pe.wait_ge(x2_lo, b * XG + (KC if b == 0 else XG))
                        if g_ == KC + TH and b == 0:
                            pe.wait_ge(x2_lo, XG)
                        if g_ < 4:
                            wait(pe, exp_done, b * QT - 1 + g_ // 2)
                        elif g_ < PG - 2:
                            pe.wait_ge(proj_lo, b * PG + g_ - 3)
                        else:
                            wait(pe, s_made, b * QT)
                        bank, xt = proj_bank(g_), x2t[b % 2]
                        is_v, h, m = proj_group(g_)
                        for k in range(KC):
                            for n, (a, w) in enumerate(PARTS):
                                cols = slice(m * P, (m + 1) * P)
                                if is_v:
                                    left, right = xt[h][:, a, k, cols], fold[:, 1, k, w, :]
                                else:
                                    left, right = fold[:, 0, k, a, cols], xt[h][:, w, k, :]
                                last = pe.matmul(bank[:, :], left, right, start=(k == 0 and n == 0),
                                                 stop=(k == KC - 1 and n == 2))
                        last.then_inc(proj_done, 1)

                    def scores(t):
                        b, n, i = t // QT, t % QT, tile_of(t)
                        if n < 2:
                            pe.wait_ge(proj_lo, b * PG + PG - 2)
                        else:
                            pe.wait_ge(exp_done, t - 1)
                        for col in range(0, (i + 1) * P, HALF):
                            w = min(HALF, (i + 1) * P - col)
                            for k in range(KC):
                                for m, (a, r) in enumerate(PARTS):
                                    last = pe.matmul(wide[t % 2][:, col:col + w], qt[:, a, k, i * P:(i + 1) * P],
                                                     x2t[b % 2][col // HALF][:, r, k, 0:w],
                                                     start=(k == 0 and m == 0), stop=(k == KC - 1 and m == 2))
                        last.then_inc(scores_done, 1)

                    def turn_probs(t):
                        i = tile_of(t)
                        pe.wait_ge(exp_done, t + 1)
                        for n, first in enumerate(range(0, i + 1, 4)):
                            group = turn_groups(t) + n
                            wait(pe, pt_lo, group - 1)
                            if group < turn_groups(t // QT * QT) + 2:
                                pe.wait_ge(x2_lo, min(B, t // QT + 2) * XG)
                            bank = turn_banks[group % 2]
                            for k in range(first, min(first + 4, i + 1)):
                                last = pe.transpose(bank[:, (k - first) * P:(k - first + 1) * P],
                                                    c["p", t % 2][:, k * P:(k + 1) * P], ident[:, :])
                            last.then_inc(p_turned, 1)

                    def weigh(t):
                        i = tile_of(t)
                        pe.wait_ge(pt_lo, turn_groups(t + 1))
                        wait(pe, s_made, t - 1)
                        if t % QT == 0:
                            pe.wait_ge(proj_lo, (t // QT + 1) * PG)
                        for k in range(i + 1):
                            for n, (a, r) in enumerate(PARTS):
                                last = pe.matmul(pv_banks[t % 2][:, :], c["pt", t % 2][:, a, k, :], vs[:, k, r, :],
                                                 start=(k == 0 and n == 0), stop=(k == i and n == 2))
                        last.then_inc(pv_done, 1)

                    pe.wait_ge(fold_loaded, 16)
                    for b in range(B):
                        for g_ in range(PG):
                            project(b, g_)
                            if g_ == 0 and b > 0:
                                weigh(b * QT - 2)
                                turn_probs(b * QT - 1)
                            if g_ == 2 and b > 0:
                                weigh(b * QT - 1)
                            if g_ in x2_turns[b]:
                                turn_x2(*x2_turns[b][g_])
                            if g_ == PG - 2:
                                scores(b * QT)
                        for n in range(QT):
                            t = b * QT + n
                            if n + 1 < QT:
                                scores(t + 1)
                            if n + 1 == QT and b + 1 < B:
                                continue
                            if n > 0:
                                weigh(t - 1)
                            turn_probs(t)
                    weigh(NT - 1)

                @block.scalar
                def _(act):
                    def x2_high(b, k):
                        if k == 0:
                            wait(act, scores_done, (b - 1) * QT)
                        x2_high_from(act, b, k, turn_banks[k % 2])

                    def proj_high(b, g_):
                        act.wait_ge(proj_done, b * PG + g_ + 1)
                        nc.scalar.activation(proj_target(g_, 0), proj_bank(g_)[:, :], ACT.Copy,
                                             scale=Q_SCALE).then_inc(proj_hi, 1)

                    def probs(t):
                        u = t % 2
                        w = (tile_of(t) + 1) * P
                        act.wait_ge(bias_ready, t + 1)
                        wait(act, p_turned, turn_groups(t - 1) if t > 0 else 0)
                        wait(act, inv_ready, t - 3)
                        nc.scalar.activation(c["p", u][:, 0:w], wide[u][:, 0:w], ACT.Exp, bias=c["bias", u],
                                             scale=SOFT, accum_out=sums[:, t % 4:t % 4 + 1]).then_inc(exp_done, 1)

                    def pt_high(t):
                        i = tile_of(t)
                        for n, first in enumerate(range(0, i + 1, 4)):
                            group, k = turn_groups(t) + n, min(4, i + 1 - first)
                            act.wait_ge(p_turned, group + 1)
                            wait(act, pv_done, t - 1)
                            nc.scalar.copy(c["pt", t % 2][:, 0, first:first + k],
                                           chunked(turn_banks[group % 2], k)).then_inc(pt_hi, 1)

                    def begin(t):
                        u = t % 2
                        for n in range(2):
                            act.wait_ge(y_loaded[n][u], (t // 2 + 1) * 16)
                            nc.scalar.activation(c[f"y{n}", u], c[f"y{n}", u], ACT.Copy,
                                                 scale=gate[:, n, place(t):place(t) + 1]).then_inc(y_gated, 1)

                    def end(t):
                        u = t % 2
                        act.wait_ge(f_ready, t + 1)
                        wait(act, g_made, t - 1)
                        nc.scalar.activation(c["th", u], c["f", u], ACT.Tanh, scale=0.5).then_inc(tanh_done, 1)

                    def normal(t):
                        u, p = t % 2, place(t)
                        act.wait_ge(x_loaded[t % X_AHEAD], (t // X_AHEAD + 1) * 16)
                        wait(act, res_ready, t - 1)
                        nc.scalar.activation(c["s", u], c["x", t % X_AHEAD], ACT.Identity, scale=rstd[:, p:p + 1],
                                             bias=shift[:, p:p + 1]).then_inc(xn_made, 1)

                    for b in range(B):
                        for g_ in range(PG):
                            proj_high(b, g_)
                            if g_ == 0 and b > 0:
                                pt_high(b * QT - 1)
                            if g_ in x2_turns[b]:
                                x2_high(*x2_turns[b][g_])
                            if g_ in BEGIN_GROUP:
                                begin(b * QT + BEGIN_GROUP[g_])
                            if g_ in END_GROUP:
                                end(b * QT + END_GROUP[g_])
                            if g_ in (1, 5, 9):
                                t = b * QT + (g_ - 5) // 4
                                if t >= 0:
                                    normal(t)
                        for n in range(QT):
                            t = b * QT + n
                            probs(t)
                            if n > 0:
                                pt_high(t - 1)
                            if n > 2:
                                normal(t - 1)
                            if n in BEGIN_STEP:
                                begin(b * QT + BEGIN_STEP[n])
                            if n in END_STEP:
                                end(b * QT + END_STEP[n])
                    pt_high(NT - 1)
                    normal(NT - 1)

                @block.vector
                def _(dve):
                    v = nc.vector

                    def proj_low(b, g_):
                        dve.wait_ge(proj_hi, b * PG + g_ + 1)
                        v.scalar_tensor_tensor(proj_target(g_, 1), proj_bank(g_)[:, :], Q_SCALE, proj_target(g_, 0),
                                               ALU.mult, ALU.subtract).then_inc(proj_lo, 1)

                    def soften(t):
                        i, u = tile_of(t), t % 2
                        diagonal = wide[u][:, i * P:(i + 1) * P]
                        dve.wait_ge(scores_done, t + 1)
                        v.tensor_tensor(diagonal, diagonal, causal, ALU.add).then_inc(masked, 1)
                        dve.wait_ge(masked, t + 1)
                        v.tensor_reduce(c["top", u], wide[u][:, 0:(i + 1) * P], AX, ALU.max).then_inc(top_ready, 1)
                        dve.wait_ge(top_ready, t + 1)
                        v.tensor_scalar(c["bias", u], c["top", u], -SOFT, LN_P, ALU.mult, ALU.add).then_inc(bias_ready, 1)

                    def pt_low(t):
                        i = tile_of(t)
                        for n, first in enumerate(range(0, i + 1, 4)):
                            group, k = turn_groups(t) + n, min(4, i + 1 - first)
                            pt = c["pt", t % 2]
                            dve.wait_ge(pt_hi, group + 1)
                            v.tensor_tensor(pt[:, 1, first:first + k], chunked(turn_banks[group % 2], k),
                                            pt[:, 0, first:first + k], ALU.subtract).then_inc(pt_lo, 1)

                    def end(t):
                        dve.wait_ge(tanh_done, t + 1)
                        wait(dve, o_made, t - QT + 1)
                        v.scalar_tensor_tensor(g[:, t % QT, :], c["th", t % 2], 1.0, c["f", t % 2], ALU.add, ALU.mult
                                               ).then_inc(g_made, 1)

                    def combine(t):
                        u = t % 2
                        dve.wait_ge(exp_done, t + 1)
                        v.reciprocal(c["inv", u], sums[:, t % 4:t % 4 + 1]).then_inc(inv_ready, 1)
                        dve.wait_ge(inv_ready, t + 1)
                        dve.wait_ge(xn_made, t + 1)
                        dve.wait_ge(pv_done, t + 1)
                        v.scalar_tensor_tensor(c["s", u], pv_banks[u][:, :], c["inv", u][:, 0:1], c["s", u],
                                               ALU.mult, ALU.add).then_inc(s_made, 1)
                        dve.wait_ge(g_made, t + 1)
                        dve.wait_ge(s_made, t + 1)
                        v.scalar_tensor_tensor(c["s", u], c["s", u], 0.5 / S_Q, g[:, t % QT, :], ALU.mult, ALU.mult
                                               ).then_inc(o_made, 1)

                    for b in range(B):
                        for g_ in range(PG):
                            proj_low(b, g_)
                            if g_ == 3 and b > 0:
                                combine(b * QT - 1)
                            if g_ == 0 and b > 0:
                                pt_low(b * QT - 1)
                            if g_ in x2_turns[b]:
                                seq, k = x2_turns[b][g_]
                                x2_low_from(dve, seq, k, turn_banks[k % 2])
                            seq, k = x2_turns[b].get(g_ + 1, (0, 1))
                            if seq == b + 1 and k % KC == 0:
                                normalise_x2(dve, seq, k // KC)
                            if g_ == 1 and b > 0:
                                combine(b * QT - 2)
                            if g_ in END_GROUP:
                                end(b * QT + END_GROUP[g_])
                        if b == 0:
                            dve.wait_ge(causal_ready, 1)
                        for n in range(QT):
                            t = b * QT + n
                            soften(t)
                            if n > 0:
                                pt_low(t - 1)
                            if n > 1:
                                combine(t - 2)
                            if n in END_STEP:
                                end(b * QT + END_STEP[n])
                    pt_low(NT - 1)
                    combine(NT - 2)
                    combine(NT - 1)

        stage0()
        stages1and2()
        stage3()
        stage4()


_INS = ['L0_attn_x', 'L0_attn_qkv', 'L0_attn_o_proj', 'L0_attn_gamma', 'L0_attn_beta', 'L0_ffn_router_w',
        'L0_ffn_wg', 'L0_ffn_wu', 'L0_ffn_wd', 'L0_ffn_sg', 'L0_ffn_su', 'L0_ffn_sd']
_OUTS = [((4, 1024, 512), 'float32')]


def kernel(**inputs):
    import numpy as _np
    import concourse.bacc as _bacc
    from concourse import mybir as _mybir
    from concourse.bass_utils import run_bass_kernel_spmd as _run

    nc = _bacc.Bacc("TRN2", target_bir_lowering=False, num_devices=1)
    arrays, args = {}, []
    for name in _INS:
        a = _np.ascontiguousarray(inputs[name])
        arrays[f"in_{name}_dram"] = a
        args.append(nc.dram_tensor(f"in_{name}_dram", a.shape, _mybir.dt.from_np(a.dtype), kind="ExternalInput").ap())
    for i, (shape, dtype) in enumerate(_OUTS):
        dt = _mybir.dt.from_np(_np.dtype(dtype))
        args.append(nc.dram_tensor(f"out_{i}_dram", shape, dt, kind="ExternalOutput").ap())
    mixture_attention_kernel(nc, *args)
    r = _run(nc, [arrays], core_ids=[0])
    got = tuple(r.results[0][f"out_{i}_dram"] for i in range(len(_OUTS)))
    return got[0]
```
